# Optimizing a Trainium2 kernel written in Bass

```python
import numpy as np
import jax
import jax.numpy as jnp

def _softmax(x, axis=-1):
    return jax.nn.softmax(x, axis=axis)

def _gelu(x):
    return jax.nn.gelu(x, approximate=True)

def _silu(x):
    return jax.nn.silu(x)

def _sigmoid(x):
    return jax.nn.sigmoid(x)

def _layernorm(x, axis=-1, eps=1e-05):
    m = jnp.mean(x, axis=axis, keepdims=True)
    v = jnp.var(x, axis=axis, keepdims=True)
    return (x - m) / jnp.sqrt(v + eps)

def _scatter_add(tgt, idx, src, axis=0):
    return tgt.at[idx].add(src)

def _segment_sum(src, seg, n):
    return jax.ops.segment_sum(src, seg, n)
kernel_name = 'mk_early_fusion_d1_tok_img512_r4_35d35e'

def setup_inputs(seed: int=0):
    np.random.seed(seed)
    _w = jnp.asarray

    def _rec_inputs():
        import jax
        import jax.numpy as jnp
        _rk = jax.random.key(seed)
        x = -0.000356955 + 1 * jax.random.normal(jax.random.fold_in(_rk, 1), (16, 3, 96, 96), jnp.float32)
        txt = -3.85354e-11 + 0.999983 * jax.random.normal(jax.random.fold_in(_rk, 2), (16, 128, 128), jnp.float32)
        return (x, txt)
    x, txt = _rec_inputs()

    def _L0_tok_setup():
        import jax, jax.numpy as jnp
        import numpy as np
        P = 16
        SHIFT = P // 2
        EPS = 1e-05

        def _shift2d(img, dy, dx):
            H, W = (img.shape[2], img.shape[3])
            pad = ((0, 0), (0, 0), (max(dy, 0), max(-dy, 0)), (max(dx, 0), max(-dx, 0)))
            z = jnp.pad(img, pad)
            return z[:, :, max(-dy, 0):max(-dy, 0) + H, max(-dx, 0):max(-dx, 0) + W]

        def _patchify(img):
            B, C, H, W = img.shape
            nH, nW = (H // P, W // P)
            t = img.reshape(B, C, nH, P, nW, P).transpose(0, 2, 4, 1, 3, 5)
            return t.reshape(B, nH * nW, C * P * P)
        key = jax.random.key(seed)
        ks = jax.random.split(key, 8)
        B, C, H, Wd = (128, 3, 224, 224)
        embed_dim = 128
        d_main = embed_dim // 2
        d_shift = embed_dim // 8
        fan_in = C * P * P
        std = 0.02
        x = jax.random.normal(ks[0], (B, C, H, Wd), dtype=jnp.float32)
        W_main = jax.random.normal(ks[1], (d_main, fan_in), dtype=jnp.float32) * std
        b_main = jnp.zeros((d_main,), dtype=jnp.float32)
        W_sx = jax.random.normal(ks[2], (d_shift, fan_in), dtype=jnp.float32) * std
        b_sx = jnp.zeros((d_shift,), dtype=jnp.float32)
        W_sy = jax.random.normal(ks[3], (d_shift, fan_in), dtype=jnp.float32) * std
        b_sy = jnp.zeros((d_shift,), dtype=jnp.float32)
        ln_g = jnp.ones((embed_dim,), dtype=jnp.float32)
        ln_b = jnp.zeros((embed_dim,), dtype=jnp.float32)
        return {'x': x, 'W_main': W_main, 'b_main': b_main, 'W_sx': W_sx, 'b_sx': b_sx, 'W_sy': W_sy, 'b_sy': b_sy, 'ln_g': ln_g, 'ln_b': ln_b}
    _L0_tok_all = _L0_tok_setup()
    _L0_tok_in = {k: v for k, v in _L0_tok_all.items() if k in ('W_main', 'b_main', 'W_sx', 'b_sx', 'W_sy', 'b_sy', 'ln_g', 'ln_b')}
    del _L0_tok_all

    def _L0_attn_setup():
        import math
        import jax, jax.numpy as jnp
        import numpy as np
        D_MODEL = 128
        N_HEADS = 8
        FACTOR = 5
        key = jax.random.key(seed)
        ks = jax.random.split(key, 9)
        B, L, d = (2, 512, D_MODEL)
        s = 0.02
        inp = {'x': jax.random.normal(ks[0], (B, L, d), dtype=jnp.float32)}
        inp['Wq'] = jax.random.normal(ks[1], (d, d), dtype=jnp.float32) * s
        inp['bq'] = jnp.zeros((d,), dtype=jnp.float32)
        inp['Wk'] = jax.random.normal(ks[2], (d, d), dtype=jnp.float32) * s
        inp['bk'] = jnp.zeros((d,), dtype=jnp.float32)
        inp['Wv'] = jax.random.normal(ks[3], (d, d), dtype=jnp.float32) * s
        inp['bv'] = jnp.zeros((d,), dtype=jnp.float32)
        inp['Wo'] = jax.random.normal(ks[4], (d, d), dtype=jnp.float32) * s
        inp['bo'] = jnp.zeros((d,), dtype=jnp.float32)
        return inp
    _L0_attn_all = _L0_attn_setup()
    _L0_attn_in = {k: v for k, v in _L0_attn_all.items() if k in ('Wq', 'bq', 'Wk', 'bk', 'Wv', 'bv', 'Wo', 'bo')}
    del _L0_attn_all

    def _L0_ffn_setup():
        import jax, jax.numpy as jnp
        import numpy as np
        E = 64
        K = 6
        NS = 2
        D = 128
        F = 128

        def _swiglu_ffn(x, wg, wu, wd):
            return jax.nn.silu(x @ wg) * (x @ wu) @ wd
        key = jax.random.key(seed)
        ks = jax.random.split(key, 8)
        s = 0.02
        return {'hidden_states': jax.random.normal(ks[0], (2, 256, D), dtype=jnp.float32), 'Wr': jax.random.normal(ks[1], (D, E), dtype=jnp.float32) * s, 'sWg': jax.random.normal(ks[2], (NS, D, F), dtype=jnp.float32) * s, 'sWu': jax.random.normal(ks[3], (NS, D, F), dtype=jnp.float32) * s, 'sWd': jax.random.normal(ks[4], (NS, F, D), dtype=jnp.float32) * s, 'Wg': jax.random.normal(ks[5], (E, D, F), dtype=jnp.float32) * s, 'Wu': jax.random.normal(ks[6], (E, D, F), dtype=jnp.float32) * s, 'Wd': jax.random.normal(ks[7], (E, F, D), dtype=jnp.float32) * s}
    _L0_ffn_all = _L0_ffn_setup()
    _L0_ffn_in = {k: v for k, v in _L0_ffn_all.items() if k in ('Wr', 'sWg', 'sWu', 'sWd', 'Wg', 'Wu', 'Wd')}
    del _L0_ffn_all
    return {'x': x, 'txt': txt, 'L0_tok_W_main': _L0_tok_in['W_main'], 'L0_tok_b_main': _L0_tok_in['b_main'], 'L0_tok_W_sx': _L0_tok_in['W_sx'], 'L0_tok_b_sx': _L0_tok_in['b_sx'], 'L0_tok_W_sy': _L0_tok_in['W_sy'], 'L0_tok_b_sy': _L0_tok_in['b_sy'], 'L0_tok_ln_g': _L0_tok_in['ln_g'], 'L0_tok_ln_b': _L0_tok_in['ln_b'], 'L0_attn_Wq': _L0_attn_in['Wq'], 'L0_attn_bq': _L0_attn_in['bq'], 'L0_attn_Wk': _L0_attn_in['Wk'], 'L0_attn_bk': _L0_attn_in['bk'], 'L0_attn_Wv': _L0_attn_in['Wv'], 'L0_attn_bv': _L0_attn_in['bv'], 'L0_attn_Wo': _L0_attn_in['Wo'], 'L0_attn_bo': _L0_attn_in['bo'], 'L0_ffn_Wr': _L0_ffn_in['Wr'], 'L0_ffn_sWg': _L0_ffn_in['sWg'], 'L0_ffn_sWu': _L0_ffn_in['sWu'], 'L0_ffn_sWd': _L0_ffn_in['sWd'], 'L0_ffn_Wg': _L0_ffn_in['Wg'], 'L0_ffn_Wu': _L0_ffn_in['Wu'], 'L0_ffn_Wd': _L0_ffn_in['Wd']}

def reference(x, txt, L0_tok_W_main, L0_tok_b_main, L0_tok_W_sx, L0_tok_b_sx, L0_tok_W_sy, L0_tok_b_sy, L0_tok_ln_g, L0_tok_ln_b, L0_attn_Wq, L0_attn_bq, L0_attn_Wk, L0_attn_bk, L0_attn_Wv, L0_attn_bv, L0_attn_Wo, L0_attn_bo, L0_ffn_Wr, L0_ffn_sWg, L0_ffn_sWu, L0_ffn_sWd, L0_ffn_Wg, L0_ffn_Wu, L0_ffn_Wd):
    import jax
    import jax.numpy as jnp

    def _L0_tok_ref(x, W_main, b_main, W_sx, b_sx, W_sy, b_sy, ln_g, ln_b):
        import jax, jax.numpy as jnp
        import numpy as np
        P = 16
        SHIFT = P // 2
        EPS = 1e-05

        def _shift2d(img, dy, dx):
            H, W = (img.shape[2], img.shape[3])
            pad = ((0, 0), (0, 0), (max(dy, 0), max(-dy, 0)), (max(dx, 0), max(-dx, 0)))
            z = jnp.pad(img, pad)
            return z[:, :, max(-dy, 0):max(-dy, 0) + H, max(-dx, 0):max(-dx, 0) + W]

        def _patchify(img):
            B, C, H, W = img.shape
            nH, nW = (H // P, W // P)
            t = img.reshape(B, C, nH, P, nW, P).transpose(0, 2, 4, 1, 3, 5)
            return t.reshape(B, nH * nW, C * P * P)

        def proj(img, W, b):
            return jnp.einsum('bnf,of->bno', _patchify(img), W) + b
        main = proj(x, W_main, b_main)
        xl = proj(_shift2d(x, 0, -SHIFT), W_sx, b_sx)
        xr = proj(_shift2d(x, 0, SHIFT), W_sx, b_sx)
        yu = proj(_shift2d(x, -SHIFT, 0), W_sy, b_sy)
        yd = proj(_shift2d(x, SHIFT, 0), W_sy, b_sy)
        tok = jnp.concatenate([main, xl, xr, yu, yd], axis=-1)
        mu = jnp.mean(tok, axis=-1, keepdims=True)
        var = jnp.mean(jnp.square(tok - mu), axis=-1, keepdims=True)
        return (tok - mu) * jax.lax.rsqrt(var + EPS) * ln_g + ln_b

    def _L0_attn_ref(x, Wq, bq, Wk, bk, Wv, bv, Wo, bo):
        import math
        import jax, jax.numpy as jnp
        import numpy as np
        D_MODEL = 128
        N_HEADS = 8
        FACTOR = 5
        B, L, d = x.shape
        H = N_HEADS
        E = d // H
        Q = (x @ Wq.T + bq).reshape(B, L, H, E).transpose(0, 2, 1, 3)
        K = (x @ Wk.T + bk).reshape(B, L, H, E).transpose(0, 2, 1, 3)
        V = (x @ Wv.T + bv).reshape(B, L, H, E).transpose(0, 2, 1, 3)
        scale = E ** 0.5
        attn = jnp.einsum('bhle,bhse->bhls', Q, K) / scale
        k = min(int(FACTOR * math.log(L)), L)
        topv, top_idx = jax.lax.top_k(attn, k)
        sm = jax.nn.softmax(topv, axis=-1)
        bi = jnp.arange(B)[:, None, None, None]
        hi = jnp.arange(H)[None, :, None, None]
        li = jnp.arange(L)[None, None, :, None]
        attn_w = jnp.zeros_like(attn).at[bi, hi, li, top_idx].set(sm)
        out = jnp.einsum('bhls,bhse->bhle', attn_w, V)
        out = out.transpose(0, 2, 1, 3).reshape(B, L, d)
        return out @ Wo.T + bo

    def _L0_ffn_ref(hidden_states, Wr, sWg, sWu, sWd, Wg, Wu, Wd):
        import jax, jax.numpy as jnp
        import numpy as np
        E = 64
        K = 6
        NS = 2
        D = 128
        F = 128

        def _swiglu_ffn(x, wg, wu, wd):
            return jax.nn.silu(x @ wg) * (x @ wu) @ wd
        B, S, d = hidden_states.shape
        x = hidden_states.reshape(-1, d)
        N = x.shape[0]
        shared = jnp.zeros_like(x)
        for e in range(NS):
            shared = shared + _swiglu_ffn(x, sWg[e], sWu[e], sWd[e])
        logits = x @ Wr
        probs = jax.nn.softmax(logits, axis=-1)
        top_w, top_i = jax.lax.top_k(probs, K)
        top_w = top_w / jnp.sum(top_w, axis=-1, keepdims=True)
        gate = jnp.zeros((N, E), dtype=x.dtype).at[jnp.arange(N)[:, None], top_i].set(top_w)
        routed = jnp.zeros_like(x)
        for e in range(E):
            routed = routed + _swiglu_ffn(x, Wg[e], Wu[e], Wd[e]) * gate[:, e:e + 1]
        out = (shared + routed + x).reshape(B, S, d)
        return out
    h = _L0_tok_ref(x, L0_tok_W_main, L0_tok_b_main, L0_tok_W_sx, L0_tok_b_sx, L0_tok_W_sy, L0_tok_b_sy, L0_tok_ln_g, L0_tok_ln_b)
    h = jnp.concatenate([h, txt], axis=1)
    h = h + _L0_attn_ref(_layernorm(h, axis=-1), L0_attn_Wq, L0_attn_bq, L0_attn_Wk, L0_attn_bk, L0_attn_Wv, L0_attn_bv, L0_attn_Wo, L0_attn_bo)
    h = h + _L0_ffn_ref(_layernorm(h, axis=-1), L0_ffn_Wr, L0_ffn_sWg, L0_ffn_sWu, L0_ffn_sWd, L0_ffn_Wg, L0_ffn_Wu, L0_ffn_Wd)
    return h

_drawn_inputs = setup_inputs


def setup_inputs(seed=0):
    import zlib

    import numpy as np

    out = dict(_drawn_inputs(seed))
    spreads = {'L0_tok_b_main': (0.0, 0.1),
     'L0_tok_b_sx': (0.0, 0.1),
     'L0_tok_b_sy': (0.0, 0.1),
     'L0_tok_ln_g': (1.0, 0.2),
     'L0_tok_ln_b': (0.0, 0.1),
     'L0_attn_bq': (0.0, 0.8),
     'L0_attn_bk': (0.0, 0.8),
     'L0_attn_bv': (0.0, 0.388),
     'L0_attn_bo': (0.0, 0.1)}
    factors = {'L0_attn_Wq': 5.104,
     'L0_attn_Wk': 4.857,
     'L0_attn_Wv': 4.509,
     'L0_ffn_Wr': 8.0,
     'L0_ffn_sWg': 8.0,
     'L0_ffn_sWu': 8.0,
     'L0_ffn_sWd': 8.0,
     'L0_ffn_Wg': 8.0,
     'L0_ffn_Wu': 8.0,
     'L0_ffn_Wd': 8.0}
    for name, (base, spread) in spreads.items():
        noise = np.random.default_rng([zlib.crc32(name.encode()), seed]).standard_normal(out[name].shape)
        drawn = base * np.exp(spread * noise) if base else spread * noise
        out[name] = jnp.asarray(drawn.astype(out[name].dtype))
    for name, factor in factors.items():
        out[name] = (out[name] * factor).astype(out[name].dtype)
    return out
```

```python
from contextlib import ExitStack

import concourse.bass as bass
import numpy as np
from concourse import mybir

F32 = mybir.dt.float32
I32 = mybir.dt.int32
ALU = mybir.AluOpType
ACT = mybir.ActivationFunctionType
AX = mybir.AxisListType

P = 128
B = 16
D = 128
NP_ = 36
NT = 128
L = NP_ + NT
H = 8
E = D // H
ROWS = H * L
PAIRS = B // 2
TILES = 2 * ROWS // P + 1
GT = 3
GROUPS = TILES // GT
MID = ROWS // P
TAIL = ROWS - MID * P
TOPK = 25
EPS = 1e-5
MARK = -3.0e38
CHUNKS = 6


NE = 64
NS = 2
KE = 6
T2 = 2 * NP_
PT = 2 * L
TOKENS = B * L
CAP = TOKENS + P
REC = D + NE
ETILES = (TOKENS * KE + NE * (P - 1)) // P
SENT = -2.9e38


def slot(g):
    return g % 3 if g < GROUPS - 1 else 3


def s_bank(g):
    return g % 2 if g < GROUPS - 1 else 2


def build(nc, a, out):
    es = ExitStack()
    with es:
        def sb(name, shape, dt=F32, where=es):
            return where.enter_context(nc.sbuf_tensor(name, shape, dt))

        def bank(name, shape, where):
            return where.enter_context(nc.psum_tensor(name, shape, F32))

        ident = sb("ident", [P, P])
        h_text = sb("h_text", [P, B, D])
        h_patch = sb("h_patch", [NP_, B, D])
        h2_patch = sb("h2_patch", [2 * NP_, PAIRS, D])
        shift36 = sb("shift36", [NP_, 2 * NP_])
        rows = sb("rows", [1, 2 * D])
        ones = sb("ones", [1, P])
        rstd_t = sb("rstd_t", [P, B])
        nbias_t = sb("nbias_t", [P, B])
        rstd_p = sb("rstd_p", [NP_, B])
        nbias_p = sb("nbias_p", [NP_, B])
        wq = sb("wq", [P, D])
        wk = sb("wk", [P, D])
        wv = sb("wv", [P, D])
        wo = sb("wo", [P, D])
        bq = sb("bq", [P, 1])
        bk = sb("bk", [P, 1])
        head_mask = sb("head_mask", [P, H])
        w_gu = sb("w_gu", [P, NE + NS, 2 * D])
        w_d = sb("w_d", [P, NE + NS, D])
        weights_in = es.enter_context(nc.semaphore("weights_in"))
        dispatch = nc.dram_tensor("dispatch", (NE * CAP + P, REC), F32).ap()
        results = nc.dram_tensor("results", (ETILES * P, D), F32).ap()
        prologue(nc, es, sb, bank, a, dict(locals()))
        attention(nc, es, sb, bank, a, dict(locals()))
        base = sb("base", [P, 3 * PAIRS, D])
        xT_all = sb("xT_all", [P, PAIRS * PT])
        places = sb("places", [P, 3 * PAIRS, NE])
        carry = sb("carry", [P, NE])
        route(nc, es, sb, bank, a, dict(locals()))
        where = sb("where", [P, 3 * PAIRS, 8], I32)
        table = sb("table", [1, 3, 2 * P], I32)
        plan(nc, es, sb, bank, a, dict(locals()))
        experts(nc, es, sb, bank, a, dict(locals()))
        combine(nc, es, sb, bank, a, out, dict(locals()))


def prologue(nc, es, sb, bank, a, v):
    ident, h_text, h_patch, rows, ones = v["ident"], v["h_text"], v["h_patch"], v["rows"], v["ones"]
    with ExitStack() as local:
        def lsb(name, shape, dt=F32):
            return sb(name, shape, dt, local)

        def sem(name):
            return local.enter_context(nc.semaphore(name))

        patches = lsb("patches", [P, CHUNKS, B * NP_])
        w_all = lsb("w_all", [P, CHUNKS, D])
        perm = lsb("perm", [P, 5, D])
        grid = lsb("grid", [P, B, 8, 8])
        tok_T = lsb("tok_T", [P, B * NP_])
        b_tok = lsb("b_tok", [P, 1])
        gain = lsb("gain", [NP_, D])
        shiftb = lsb("shiftb", [NP_, D])
        stats_p = lsb("stats_p", [NP_, B, 6])
        stats_t = lsb("stats_t", [P, B, 6])
        mv_p = lsb("mv_p", [NP_, B, 2])
        mv_t = lsb("mv_t", [P, B, 2])
        sd_p = lsb("sd_p", [NP_, B])
        sd_t = lsb("sd_t", [P, B])
        ps_u = [bank(f"ps_u{i}", [P, 512], local) for i in range(2)]
        ps_tok = [bank(f"ps_tok{i}", [P, 4, D], local) for i in range(4)]
        w_in, c_in, t_in = sem("w_in"), sem("c_in"), sem("t_in")
        p_in = [sem(f"p_in{c}") for c in range(CHUNKS)]
        b_in = sem("b_in")
        proj_done, grid_zero, grid_ready, tok_ready = sem("proj_done"), sem("grid_zero"), sem("grid_ready"), sem("tok_ready")
        sum_ready, tokT_ready = sem("sum_ready"), sem("tokT_ready")
        dve, sd_ready, var_ready = sem("dve"), sem("sd_ready"), sem("var_ready")
        SPLIT = 14
        with nc.Block() as block:
            @block.sync
            def _(sp):
                sp.dma_start(w_all[:, :, :], a["w_all"]).then_inc(w_in, 16)
                for c in range(CHUNKS):
                    sp.dma_start(patches[:, c, :], a["patches"][:, c, :]).then_inc(p_in[c], 16)
                sp.dma_start(h_text[:, :, :], a["txt"]).then_inc(t_in, 16)
                for lo in range(0, NE + NS, 11):
                    sp.dma_start(v["w_gu"][:, lo:lo + 11, :], a["w_gu"][:, lo:lo + 11, :]).then_inc(v["weights_in"], 16)
                    sp.dma_start(v["w_d"][:, lo:lo + 11, :], a["w_d"][:, lo:lo + 11, :]).then_inc(v["weights_in"], 16)

            @block.scalar
            def _(act):
                for t, n in ((ident, "ident"), (perm, "perm"), (v["shift36"], "shift36"), (rows, "rows"),
                             (v["wq"], "wq"), (v["wk"], "wk"), (v["wv"], "wv"), (v["wo"], "wo"),
                             (v["bq"], "bq"), (b_tok, "b_tok"), (v["bk"], "bk"), (v["head_mask"], "head_mask")):
                    act.dma_start(t.ap() if hasattr(t, "ap") else t[:], a[n]).then_inc(c_in, 16)
                act.dma_start(gain[:, :], a["ln_g"].partition_broadcast(NP_)).then_inc(b_in, 16)
                act.dma_start(shiftb[:, :], a["ln_b"].partition_broadcast(NP_)).then_inc(b_in, 16)
                act.wait_ge(grid_zero, 1)
                act.wait_ge(proj_done, 1)
                act.activation(grid[:, 0:SPLIT, 1:7, 1:7],
                               ps_u[0][:, 0:SPLIT * NP_].rearrange("p (b i j) -> p b i j", b=SPLIT, i=6),
                               ACT.Copy).then_inc(grid_ready, 1)
                act.wait_ge(proj_done, 2)
                act.activation(grid[:, SPLIT:B, 1:7, 1:7],
                               ps_u[1][:, 0:(B - SPLIT) * NP_].rearrange("p (b i j) -> p b i j", b=B - SPLIT, i=6),
                               ACT.Copy).then_inc(grid_ready, 1)
                for half, (lo, hi) in enumerate(((0, SPLIT), (SPLIT, B))):
                    act.wait_ge(c_in, 16 * 12)
                    act.wait_ge(sum_ready, half + 1)
                    act.activation(tok_T[:, lo * NP_:hi * NP_], ps_u[half][:, 0:(hi - lo) * NP_], ACT.Identity,
                                   bias=b_tok[:, 0:1]).then_inc(tokT_ready, 1)
                act.wait_ge(var_ready, 1)
                act.activation(sd_t[:, :], mv_t[:, :, 1], ACT.Sqrt).then_inc(sd_ready, 1)
                act.wait_ge(var_ready, 2)
                act.activation(sd_p[:, :], mv_p[:, :, 1], ACT.Sqrt).then_inc(sd_ready, 1)
                act.wait_ge(var_ready, 3)
                act.activation(sd_p[:, :], mv_p[:, :, 1], ACT.Sqrt).then_inc(sd_ready, 1)

            @block.tensor
            def _(pe):
                pe.wait_ge(w_in, 16)
                for half, (lo, hi) in enumerate(((0, SPLIT), (SPLIT, B))):
                    for c in range(CHUNKS):
                        if half == 0:
                            pe.wait_ge(p_in[c], 16)
                        last = pe.matmul(ps_u[half][:, 0:(hi - lo) * NP_], w_all[:, c, :],
                                         patches[:, c, lo * NP_:hi * NP_], start=(c == 0), stop=(c == CHUNKS - 1))
                    last.then_inc(proj_done, 1)
                pe.wait_ge(c_in, 16 * 12)
                for half, (lo, hi) in enumerate(((0, SPLIT), (SPLIT, B))):
                    pe.wait_ge(grid_ready, half + 1)
                    for s, (di, dj) in enumerate(((0, 0), (0, 1), (0, -1), (1, 0), (-1, 0))):
                        last = pe.matmul(ps_u[half][:, 0:(hi - lo) * NP_].rearrange("p (b i j) -> p b i j", i=6, j=6),
                                         perm[:, s, :], grid[:, lo:hi, 1 + di:7 + di, 1 + dj:7 + dj],
                                         start=(s == 0), stop=(s == 4))
                    last.then_inc(sum_ready, 1)
                for b in range(B):
                    pe.wait_ge(tokT_ready, 1 if b < SPLIT else 2)
                    pe.transpose(ps_tok[b // 4][0:NP_, b % 4, :], tok_T[:, b * NP_:(b + 1) * NP_],
                                 ident[:, :]).then_inc(tok_ready, 1)

            @block.vector
            def _(ve):
                n = [0]

                def then(ins):
                    ins.then_inc(dve, 1)
                    n[0] += 1

                def settle():
                    ve.wait_ge(dve, n[0])

                ve.memset(grid[:, :, :, :], 0.0).then_inc(grid_zero, 1)
                then(ve.memset(ones[:, :], 1.0))
                ve.wait_ge(t_in, 16)
                for b in range(B):
                    then(ve.bn_stats(stats_t[:, b, :], h_text[:, b, :]))
                settle()
                for b in range(B):
                    then(ve.bn_aggr(mv_t[:, b, :], stats_t[:, b, :]))
                settle()
                ve.tensor_scalar(mv_t[:, :, 1], mv_t[:, :, 1], EPS, None, ALU.add).then_inc(var_ready, 1)
                for b in range(B):
                    ve.wait_ge(tok_ready, b // 4 * 4 + 4)
                    then(ve.bn_stats(stats_p[:, b, :], ps_tok[b // 4][0:NP_, b % 4, :]))
                settle()
                for b in range(B):
                    then(ve.bn_aggr(mv_p[:, b, :], stats_p[:, b, :]))
                settle()
                ve.tensor_scalar(mv_p[:, :, 1], mv_p[:, :, 1], EPS, None, ALU.add).then_inc(var_ready, 1)
                ve.wait_ge(sd_ready, 2)
                then(ve.reciprocal(sd_p[:, :], sd_p[:, :]))
                settle()
                for b in range(B):
                    then(ve.tensor_scalar(h_patch[:, b, :], ps_tok[b // 4][0:NP_, b % 4, :], mv_p[:, b, 0:1],
                                          sd_p[:, b:b + 1], ALU.subtract, ALU.mult))
                ve.wait_ge(b_in, 32)
                settle()
                then(ve.tensor_tensor(h_patch[:, :, :], h_patch[:, :, :],
                                      gain[:, :].rearrange("p (a d) -> p a d", a=1).broadcast_to([NP_, B, D]), ALU.mult))
                settle()
                then(ve.tensor_tensor(h_patch[:, :, :], h_patch[:, :, :],
                                      shiftb[:, :].rearrange("p (a d) -> p a d", a=1).broadcast_to([NP_, B, D]), ALU.add))
                settle()
                for b in range(B):
                    then(ve.bn_stats(stats_p[:, b, :], h_patch[:, b, :]))
                settle()
                for b in range(B):
                    then(ve.bn_aggr(mv_p[:, b, :], stats_p[:, b, :]))
                settle()
                ve.tensor_scalar(mv_p[:, :, 1], mv_p[:, :, 1], EPS, None, ALU.add).then_inc(var_ready, 1)
                then(ve.reciprocal(v["rstd_t"][:, :], sd_t[:, :]))
                ve.wait_ge(sd_ready, 3)
                then(ve.reciprocal(v["rstd_p"][:, :], sd_p[:, :]))
                settle()
                for mv, rstd, nb in ((mv_t, "rstd_t", "nbias_t"), (mv_p, "rstd_p", "nbias_p")):
                    then(ve.scalar_tensor_tensor(out=v[nb][:, :], in0=mv[:, :, 0], scalar=-1.0, in1=v[rstd][:, :],
                                                 op0=ALU.mult, op1=ALU.mult))
                settle()


def attention(nc, es, sb, bank, a, v):
    ident, h_text, h_patch, rows, ones = v["ident"], v["h_text"], v["h_patch"], v["rows"], v["ones"]
    h2_patch, shift36, head_mask = v["h2_patch"], v["shift36"], v["head_mask"]
    wq, wk, wv, wo, bq, bk = (v[n] for n in ("wq", "wk", "wv", "wo", "bq", "bk"))
    rstd_t, nbias_t, rstd_p, nbias_p = (v[n] for n in ("rstd_t", "nbias_t", "rstd_p", "nbias_p"))
    with ExitStack() as local:
        def lsb(name, shape, dt=F32):
            return sb(name, shape, dt, local)

        def sem(name):
            return local.enter_context(nc.semaphore(name))

        xh_t = lsb("xh_t", [P, 2, D])
        xh_p = lsb("xh_p", [NP_, 2, D])
        x_T = lsb("x_T", [P, 2, L])
        q_T = lsb("q_T", [P, 2, L])
        k_T = lsb("k_T", [P, 2, L])
        q_exp = lsb("q_exp", [P, 2, H, L])
        q_flat = q_exp[:, :, :, :].rearrange("p u h l -> p (u h l)")
        v_t = lsb("v_t", [P, 2, H, D])
        v_p = lsb("v_p", [NP_, 2, H, D])
        scores = lsb("scores", [P, 4, GT, L])
        work = lsb("work", [P, 4, GT, L])
        e_all = lsb("e_all", [P, 4, GT, L])
        sum_all = lsb("sum_all", [P, 4, GT])
        sum_rest = lsb("sum_rest", [P, 4, GT])
        inv = lsb("inv", [P, 4, GT])
        top = lsb("top", [P, 4, GT, 8])
        topw = lsb("topw", [P, GT, 8])
        neg_max = lsb("neg_max", [P, 4, GT])
        pT_t = lsb("pT_t", [P, TILES * P])
        pT_p = lsb("pT_p", [NP_, TILES * P])
        oT_t = lsb("oT_t", [P, 2, NT])
        oT_p = lsb("oT_p", [P, 2 * NP_])
        b_scores = [bank(f"b_scores{i}", [P, 512], local) for i in range(3)]
        b_ptt = bank("b_ptt", [P, GT, P], local)
        b_ptp = bank("b_ptp", [P, GT, P], local)
        b_x = bank("b_x", [P, 512], local)
        b_q = bank("b_q", [P, 512], local)
        b_v = bank("b_v", [P, 4, D], local)

        zeroed = sem("zeroed")
        marker = sem("marker")
        xh_ready = sem("xh_ready")
        xT_done = sem("xT_done")
        xT_ready = sem("xT_ready")
        qkv_done = sem("qkv_done")
        q_ready = sem("q_ready")
        k_ready = sem("k_ready")
        v_ready = sem("v_ready")
        qe_ready = sem("qe_ready")
        s_done = sem("s_done")
        s_ready = sem("s_ready")
        m_ready = sem("m_ready")
        nm_ready = sem("nm_ready")
        w_ready = sem("w_ready")
        ea_ready = sem("ea_ready")
        er_ready = sem("er_ready")
        inv_ready = sem("inv_ready")
        diff_ready = sem("diff_ready")
        p_ready = sem("p_ready")
        pt_done = sem("pt_done")
        pt_ready = sem("pt_ready")
        o_done = sem("o_done")
        o_ready = sem("o_ready")
        y_done = sem("y_done")
        y_ready = sem("y_ready")
        chain = sem("chain")


        def loop(eng, body):
            body(0, True, False)
            with eng.Fori(1, PAIRS - 1) as i:
                body(i, False, False)
            body(PAIRS - 1, False, True)

        with nc.Block() as block:
            @block.tensor
            def _(pe):
                def transposes(n):
                    pe.wait_ge(xh_ready, 4 * (n + 1))
                    pe.sem_inc(marker, 1)
                    for u in range(2):
                        pe.transpose(b_x[:, u * L:u * L + NP_], xh_p[:, u, :], ident[0:NP_, 0:NP_])
                        last = pe.transpose(b_x[:, u * L + NP_:u * L + L], xh_t[:, u, :], ident[:, :])
                    last.then_inc(xT_done, 1)

                def projections(n):
                    pe.wait_ge(xT_ready, n + 1)
                    pe.matmul(b_q[:, 0:2 * L], wq[:, :], x_T[:, :, :].rearrange("p u l -> p (u l)"), start=True, stop=True)
                    pe.matmul(b_x[:, 0:2 * L], wk[:, :], x_T[:, :, :].rearrange("p u l -> p (u l)"), start=True, stop=True)
                    for u in range(2):
                        for t, (lo, n_) in enumerate(((NP_, NT), (0, NP_))):
                            o = b_v[0:n_, 2 * t + u, :]
                            pe.matmul(o, x_T[:, u, lo:lo + n_], wv[:, :], start=True, stop=False)
                            last = pe.matmul(o, ones[0:1, 0:n_], rows[0:1, 0:D], start=False, stop=True)
                    last.then_inc(qkv_done, 1)

                def score_group(i, g, G):
                    if g == 0:
                        pe.wait_ge(k_ready, 2 * i + 1)
                        pe.sem_inc(marker, 1)
                        pe.wait_ge(qe_ready, 2 * i + 1)
                        pe.sem_inc(marker, 1)
                    if g == 3:
                        pe.wait_ge(k_ready, 2 * i + 2)
                        pe.sem_inc(marker, 1)
                        pe.wait_ge(qe_ready, 2 * i + 2)
                        pe.sem_inc(marker, 1)
                    back = {0: 3, 1: 3, GROUPS - 1: GROUPS}.get(g, 2)
                    if not (isinstance(G, int) and (G < 2 or G == GROUPS - 1)):
                        pe.wait_ge(ea_ready, 3 * (G - back + 1))
                        pe.sem_inc(marker, 1)
                        pe.wait_ge(s_ready, G - back + 1)
                        pe.sem_inc(marker, 1)
                    bk_ = b_scores[s_bank(g)]
                    for t in range(GT):
                        k = GT * g + t
                        o = bk_[:, t * L:(t + 1) * L]
                        if k < MID:
                            last = pe.matmul(o, q_flat[:, k * P:(k + 1) * P], k_T[:, 0, :], start=True, stop=True)
                        elif k == MID:
                            pe.matmul(o, q_flat[:, ROWS - (P - TAIL):ROWS + TAIL], k_T[:, 1, :], start=True, stop=True)
                            last = pe.matmul(bk_[0:TAIL, t * L:(t + 1) * L], q_flat[:, ROWS - TAIL:ROWS], k_T[:, 0, :],
                                             start=True, stop=True)
                        else:
                            r = ROWS + TAIL + (k - MID - 1) * P
                            last = pe.matmul(o, q_flat[:, r:r + P], k_T[:, 1, :], start=True, stop=True)
                    last.then_inc(s_done, 1)

                def prob_transposes(g, G):
                    pe.wait_ge(p_ready, G + 1)
                    if not isinstance(G, int) or G >= 1:
                        pe.sem_inc(marker, 1)
                        pe.wait_ge(pt_ready, 2 * G)
                    for t in range(GT):
                        pr = e_all[:, slot(g), t, :]
                        pe.transpose(b_ptt[:, t, :], pr[:, NP_:L], ident[:, :])
                        last = pe.transpose(b_ptp[0:NP_, t, :], pr[:, 0:NP_], ident[:, :])
                    last.then_inc(pt_done, 1)

                def attend(i, u, dst):
                    pe.wait_ge(pt_ready, 2 * (GROUPS * i + (4 if u == 0 else 7)))
                    pe.sem_inc(marker, 1)
                    if u == 0:
                        pe.wait_ge(v_ready, 2 * (i + 1))
                        pe.sem_inc(marker, 1)
                    base = 0 if u == 0 else TILES * P - ROWS
                    for h in range(H):
                        c = base + h * L
                        pe.matmul(dst, v_t[:, u, h, :], pT_t[:, c:c + L], start=(h == 0), stop=False)
                        last = pe.matmul(dst, v_p[:, u, h, :], pT_p[:, c:c + L], start=False, stop=(h == H - 1))
                    last.then_inc(o_done, 1)

                def out_projection(i):
                    pe.wait_ge(o_ready, 4 * (i + 1))
                    pe.sem_inc(marker, 1)
                    for u in range(2):
                        o = b_x[:, u * D:(u + 1) * D]
                        pe.matmul(o, oT_t[:, u, :], wo[:, :], start=True, stop=False)
                        pe.matmul(o, ident[:, :], h_text[:, 2 * i + u, :], start=False, stop=False)
                        pe.matmul(o, ones[0:1, :], rows[0:1, D:2 * D], start=False, stop=True)
                    o = b_x[0:2 * NP_, 2 * D:3 * D]
                    pe.matmul(o, oT_p[:, :], wo[:, :], start=True, stop=False)
                    for u in range(2):
                        sel = ident[0:NP_, 0:2 * NP_] if u == 0 else shift36[:, :]
                        pe.matmul(o, sel, h_patch[:, 2 * i + u, :], start=False, stop=False)
                    pe.matmul(o, ones[0:1, 0:2 * NP_], rows[0:1, D:2 * D], start=False, stop=True).then_inc(y_done, 1)

                def body(i, first, last):
                    for g in range(GROUPS):
                        G = GROUPS * i + g
                        if g + 2 < GROUPS:
                            score_group(i, g + 2, G + 2)
                        elif not last:
                            score_group(i + 1, g + 2 - GROUPS, G + 2)
                        if not (first and g < 2):
                            prob_transposes((g - 2) % GROUPS, G - 2)
                        if g == 1 and not last:
                            if not first:
                                pe.wait_ge(o_ready, 4 * i - 2)
                                pe.sem_inc(marker, 1)
                            transposes(i + 1)
                        if g == 2 and not first:
                            attend(i - 1, 1, b_q[:, 0:L])
                            out_projection(i - 1)
                        if g == 3 and not last:
                            if not first:
                                pe.wait_ge(o_ready, 4 * i)
                                pe.sem_inc(marker, 1)
                            pe.wait_ge(v_ready, 2 * (i + 1))
                            pe.sem_inc(marker, 1)
                            if not first:
                                pe.wait_ge(y_ready, 3 * i)
                                pe.sem_inc(marker, 1)
                            projections(i + 1)
                        if g == 6:
                            if not last:
                                pe.wait_ge(k_ready, 2 * (i + 2))
                                pe.sem_inc(marker, 1)
                            attend(i, 0, b_x[:, 0:L])

                pe.wait_ge(zeroed, 2)
                transposes(0)
                projections(0)
                for g in range(2):
                    score_group(0, g, g)
                loop(pe, body)
                for g in range(2):
                    prob_transposes(GROUPS - 2 + g, GROUPS * PAIRS - 2 + g)
                attend(PAIRS - 1, 1, b_q[:, 0:L])
                out_projection(PAIRS - 1)

            @block.scalar
            def _(act):
                def normalize(n, first):
                    if not first:
                        act.wait_ge(xT_done, n)
                    for u in range(2):
                        b = 2 * n + u
                        act.activation(xh_t[:, u, :], h_text[:, b, :], ACT.Identity, bias=nbias_t[:, b:b + 1] if isinstance(b, int) else nbias_t[:, bass.ds(b, 1)],
                                       scale=rstd_t[:, b:b + 1] if isinstance(b, int) else rstd_t[:, bass.ds(b, 1)]).then_inc(xh_ready, 1)
                        act.activation(xh_p[:, u, :], h_patch[:, b, :], ACT.Identity, bias=nbias_p[:, b:b + 1] if isinstance(b, int) else nbias_p[:, bass.ds(b, 1)],
                                       scale=rstd_p[:, b:b + 1] if isinstance(b, int) else rstd_p[:, bass.ds(b, 1)]).then_inc(xh_ready, 1)

                def take_xT(n):
                    act.wait_ge(xT_done, n + 1)
                    if not isinstance(n, int) or n > 0:
                        act.wait_ge(qkv_done, n)
                    act.activation(x_T[:, :, :], b_x[:, 0:2 * L].rearrange("p (u l) -> p u l", u=2), ACT.Copy).then_inc(xT_ready, 1)

                def take_q(n):
                    act.wait_ge(qkv_done, n + 1)
                    if not isinstance(n, int) or n > 0:
                        act.wait_ge(qe_ready, 2 * n)
                    act.activation(q_T[:, :, :], b_q[:, 0:2 * L].rearrange("p (u l) -> p u l", u=2), ACT.Identity,
                                   bias=bq[:, 0:1]).then_inc(q_ready, 1)

                def take_k(n, u, G):
                    act.wait_ge(s_done, G)
                    act.activation(k_T[:, u, :], b_x[:, u * L:(u + 1) * L], ACT.Identity, bias=bk[:, 0:1]).then_inc(k_ready, 1)

                def take_v(n):
                    act.wait_ge(qkv_done, n + 1)
                    if not isinstance(n, int) or n > 0:
                        act.wait_ge(o_done, 2 * n)
                    for t, (dst, rows_) in enumerate(((v_t, P), (v_p, NP_))):
                        flat = dst[:, :, :, :].rearrange("p u h d -> p u (h d)")
                        for u in range(2):
                            diag = bass.AP(tensor=flat.tensor, offset=flat[:, u, :].offset,
                                           ap=[flat.ap[0], [D + E, H], [1, E]])
                            ins = act.activation(diag, b_v[0:rows_, 2 * t + u, :].rearrange("p (h e) -> p h e", h=H), ACT.Copy)
                        ins.then_inc(v_ready, 1)

                def take_o(i, u, src):
                    act.wait_ge(o_done, 2 * i + u + 1)
                    if u == 0 and not (isinstance(i, int) and i == 0):
                        act.wait_ge(y_done, i)
                    act.activation(oT_t[:, u, :], src[:, NP_:L], ACT.Copy).then_inc(o_ready, 1)
                    act.activation(oT_p[:, u * NP_:(u + 1) * NP_], src[:, 0:NP_], ACT.Copy).then_inc(o_ready, 1)

                def take_y(i):
                    act.wait_ge(y_done, i + 1)
                    for u in range(2):
                        act.activation(h_text[:, 2 * i + u, :], b_x[:, u * D:(u + 1) * D], ACT.Copy).then_inc(y_ready, 1)
                    act.activation(h2_patch[:, i, :], b_x[0:2 * NP_, 2 * D:3 * D], ACT.Copy).then_inc(y_ready, 1)

                def copy_scores(i, g, G):
                    act.wait_ge(s_done, G + 1)
                    if not (isinstance(G, int) and G < 4):
                        act.wait_ge(w_ready, 3 * (G - 2))
                    act.activation(scores[:, slot(g), :, :], b_scores[s_bank(g)][:, 0:GT * L].rearrange("p (t l) -> p t l", t=GT),
                                   ACT.Copy).then_inc(s_ready, 1)

                def exp_all(g, G):
                    act.wait_ge(nm_ready, G + 1)
                    if not (isinstance(G, int) and G < 4):
                        act.wait_ge(pt_done, G - 2)
                    for t in range(GT):
                        act.activation(e_all[:, slot(g), t, :], b_scores[s_bank(g)][:, t * L:(t + 1) * L], ACT.Exp,
                                       bias=neg_max[:, slot(g), t:t + 1],
                                       accum_out=sum_all[:, slot(g), t:t + 1]).then_inc(ea_ready, 1)

                def exp_rest(g, G):
                    for t in range(GT):
                        act.wait_ge(w_ready, 3 * G + t + 1)
                        act.activation(work[:, slot(g), t, :], work[:, slot(g), t, :], ACT.Exp,
                                       bias=neg_max[:, slot(g), t:t + 1],
                                       accum_out=sum_rest[:, slot(g), t:t + 1]).then_inc(er_ready, 1)

                def take_pt(g, G):
                    act.wait_ge(pt_done, G + 1)
                    if g == 0 and not (isinstance(G, int) and G == 0):
                        act.wait_ge(o_done, 2 * (G // GROUPS) if isinstance(G, int) else 2 * G_pair[0])
                    lo = GT * g * P
                    act.activation(pT_t[:, lo:lo + GT * P], b_ptt[:, :, :].rearrange("p t r -> p (t r)"), ACT.Copy).then_inc(pt_ready, 1)
                    act.activation(pT_p[:, lo:lo + GT * P], b_ptp[0:NP_, :, :].rearrange("p t r -> p (t r)"), ACT.Copy).then_inc(pt_ready, 1)

                G_pair = [0]

                def body(i, first, last):
                    G_pair[0] = i
                    for g in range(GROUPS):
                        G = GROUPS * i + g
                        exp_all(g, G)
                        if not (first and g == 0):
                            exp_rest((g - 1) % GROUPS, G - 1)
                        if not (first and g < 2):
                            take_pt((g - 2) % GROUPS, G - 2)
                        if g + 2 < GROUPS:
                            copy_scores(i, g + 2, G + 2)
                        elif not last:
                            copy_scores(i + 1, g + 2 - GROUPS, G + 2)
                        if g == 0:
                            if not first:
                                take_o(i - 1, 0, b_x[:, 0:L])
                            if not last:
                                normalize(i + 1, False)
                        if g == 1 and not last:
                            take_xT(i + 1)
                        if g == 2 and not first:
                            take_o(i - 1, 1, b_q[:, 0:L])
                        if g == 3:
                            if not first:
                                take_v(i)
                                take_y(i - 1)
                        if g == 4 and not last:
                            take_q(i + 1)
                            take_k(i + 1, 0, GROUPS * i + 4)
                        if g == 5 and not last:
                            take_k(i + 1, 1, GROUPS * i + 7)

                normalize(0, True)
                take_xT(0)
                take_q(0)
                for u in range(2):
                    act.activation(k_T[:, u, :], b_x[:, u * L:(u + 1) * L], ACT.Identity, bias=bk[:, 0:1]).then_inc(k_ready, 1)
                take_v(0)
                for g in range(2):
                    copy_scores(0, g, g)
                loop(act, body)
                exp_rest(GROUPS - 1, GROUPS * PAIRS - 1)
                take_pt(GROUPS - 2, GROUPS * PAIRS - 2)
                take_pt(GROUPS - 1, GROUPS * PAIRS - 1)
                take_o(PAIRS - 1, 0, b_x[:, 0:L])
                take_o(PAIRS - 1, 1, b_q[:, 0:L])
                take_y(PAIRS - 1)

            @block.gpsimd
            def _(po):
                po.memset(v_t[:, :, :, :], 0.0).then_inc(zeroed, 1)
                po.memset(v_p[:, :, :, :], 0.0).then_inc(zeroed, 1)

                def spread(n, u):
                    if u == 0:
                        po.wait_ge(q_ready, n + 1)
                        if not isinstance(n, int) or n > 0:
                            po.sem_inc(marker, 1)
                    if not isinstance(n, int) or n > 0:
                        po.wait_ge(s_done, GROUPS * n - (3 if u == 0 else 0))
                    po.tensor_tensor(q_exp[:, u, :, :],
                                     q_T[:, u, :].rearrange("p (a l) -> p a l", a=1).broadcast_to([P, H, L]),
                                     head_mask[:, :].rearrange("p (h a) -> p h a", a=1).broadcast_to([P, H, L]),
                                     ALU.mult).then_inc(qe_ready, 1)

                def negate(g, G):
                    po.wait_ge(m_ready, G + 1)
                    po.sem_inc(marker, 1)
                    if not (isinstance(G, int) and G < 4):
                        po.wait_ge(er_ready, 3 * (G - 2))
                        po.sem_inc(marker, 1)
                    po.tensor_scalar(neg_max[:, slot(g), :], top[:, slot(g), :, 0], -1.0, None, ALU.mult).then_inc(nm_ready, 1)

                def probabilities(g, G):
                    po.wait_ge(er_ready, 3 * (G + 1))
                    po.tensor_tensor(e_all[:, slot(g), :, :], e_all[:, slot(g), :, :], work[:, slot(g), :, :],
                                     ALU.subtract).then_inc(diff_ready, 1)
                    po.wait_ge(inv_ready, G + 1)
                    po.sem_inc(marker, 1)
                    po.wait_ge(diff_ready, G + 1)
                    po.tensor_tensor(e_all[:, slot(g), :, :], e_all[:, slot(g), :, :],
                                     inv[:, slot(g), :].rearrange("p (t a) -> p t a", a=1).broadcast_to([P, GT, L]),
                                     ALU.mult).then_inc(p_ready, 1)

                def body(i, first, last):
                    for g in range(GROUPS):
                        G = GROUPS * i + g
                        negate(g, G)
                        if not (first and g == 0):
                            probabilities((g - 1) % GROUPS, G - 1)
                        if g == 4 and not last:
                            spread(i + 1, 0)
                        if g == 6 and not last:
                            spread(i + 1, 1)

                spread(0, 0)
                spread(0, 1)
                loop(po, body)
                probabilities(GROUPS - 1, GROUPS * PAIRS - 1)

            @block.vector
            def _(ve):
                def invert(g, G, link):
                    ve.wait_ge(er_ready, 3 * (G + 1))
                    link(ve.tensor_tensor(inv[:, slot(g), :], sum_all[:, slot(g), :], sum_rest[:, slot(g), :], ALU.subtract))
                    link.settle()
                    ve.reciprocal(inv[:, slot(g), :], inv[:, slot(g), :]).then_inc(inv_ready, 1)

                class Link:
                    def __init__(self):
                        self.n = 0

                    def __call__(self, ins):
                        self.n += 1
                        ins.then_inc(chain, 1)
                        return self.n

                    def settle(self):
                        ve.wait_ge(chain, self.n)

                def body(i, first, last):
                    link = Link()
                    ve.sem_clear(chain)
                    for g in range(GROUPS):
                        G = GROUPS * i + g
                        s = slot(g)
                        ve.wait_ge(s_ready, G + 1)
                        ve.sem_inc(marker, 1)
                        if not (isinstance(G, int) and G < 4):
                            ve.wait_ge(nm_ready, G - 2)
                            ve.sem_inc(marker, 1)
                            ve.wait_ge(diff_ready, G - 2)
                            ve.sem_inc(marker, 1)
                        seen = [link(ve.max(top[:, s, t, :], scores[:, s, t, :])) for t in range(GT)]
                        for t in range(GT):
                            ve.wait_ge(chain, seen[t])
                            if t == GT - 1:
                                ve.sem_inc(m_ready, 1)
                            seen[t] = link(ve.match_replace(work[:, s, t, :], top[:, s, t, :], scores[:, s, t, :], MARK))
                        for rnd in range(2):
                            for t in range(GT):
                                ve.wait_ge(chain, seen[t])
                                seen[t] = link(ve.max(topw[:, t, :], work[:, s, t, :]))
                            for t in range(GT):
                                ve.wait_ge(chain, seen[t])
                                seen[t] = link(ve.match_replace(work[:, s, t, :], topw[:, t, :], work[:, s, t, :], MARK))
                        for t in range(GT):
                            ve.wait_ge(chain, seen[t])
                            seen[t] = link(ve.max(topw[:, t, :], work[:, s, t, :]))
                        if not (first and g == 0):
                            invert((g - 1) % GROUPS, G - 1, link)
                        ve.wait_ge(chain, seen[GT - 1])
                        n = link(ve.memset(topw[:, :, 1:8], MARK))
                        for t in range(GT):
                            ve.wait_ge(chain, n)
                            ve.match_replace(work[:, s, t, :], topw[:, t, :], work[:, s, t, :], MARK).then_inc(w_ready, 1)
                    link.settle()
                    ve.wait_ge(w_ready, 3 * (GROUPS * (i + 1)))
                    ve.sem_inc(marker, 1)

                loop(ve, body)
                link = Link()
                ve.sem_clear(chain)
                invert(GROUPS - 1, GROUPS * PAIRS - 1, link)


def route(nc, es, sb, bank, a, v):
    ident, h_text, h2_patch, ones = v["ident"], v["h_text"], v["h2_patch"], v["ones"]
    base, xT_all, places, carry, dispatch = v["base"], v["xT_all"], v["places"], v["carry"], v["dispatch"]
    with ExitStack() as local:
        def lsb(name, shape, dt=F32):
            return sb(name, shape, dt, local)

        def sem(name):
            return local.enter_context(nc.semaphore(name))

        wr = lsb("wr", [P, NE])
        tri = lsb("tri", [P, P])
        ones_sq = lsb("ones_sq", [P, P])
        region = lsb("region", [1, NE])
        minus_half = lsb("minus_half", [P, 3])
        zeros = lsb("zeros", [P, REC])
        stats = lsb("stats", [P, 3, 6])
        mv = lsb("mv", [P, 3, 2])
        rstd = lsb("rstd", [P, 3])
        nbias = lsb("nbias", [P, 3])
        rec = lsb("rec", [P, 3, REC])
        xT = lsb("xT", [P, PT])
        logits = lsb("logits", [P, 3, NE + 2])
        taken = lsb("taken", [P, 3, NE + 2])
        mask = lsb("mask", [P, 3, NE])
        chosen = lsb("chosen", [P, NE])
        best = lsb("best", [P, 3, 8])
        neg_max = lsb("neg_max2", [P, 3])
        ex = lsb("ex", [P, 3, NE])
        inv = lsb("inv2", [P, 3])
        rows_f = lsb("rows_f", [P, 3, 8])
        rows_i = lsb("rows_i", [P, 3, 8], I32)
        b_xT = bank("b_xT", [P, 512], local)
        b_lg = bank("b_lg", [P, 3, NE], local)
        b_rank = bank("b_rank", [P, 3, NE], local)
        c_in, ready0 = sem("c_in2"), sem("ready0")
        marker = sem("marker2")
        dve = sem("dve2")
        mv_ready = sem("mv_ready")
        rstd_ready = sem("rstd_ready")
        nb_ready = sem("nb_ready")
        xn_ready = sem("xn_ready")
        base_ready = sem("base_ready")
        xT_done = sem("xT_done2")
        xT_ready = sem("xT_ready2")
        lg_done = sem("lg_done")
        lg_ready = sem("lg_ready")
        nm_ready = sem("nm_ready2")
        ex_ready = sem("ex_ready")
        mask_ready = sem("mask_ready")
        rank_done = sem("rank_done")
        gate_ready = sem("gate_ready")
        idx_ready = sem("idx_ready")
        carried = sem("carried")
        sent = sem("sent")
        zero_out = sem("zero_out")
        PARTS = ((0, P), (1, P), (2, T2))

        def source(i, t):
            return h_text[:, 2 * i + t, :] if t < 2 else h2_patch[:, i, :]

        with nc.Block() as block:
            @block.sync
            def _(sp):
                for t, n in ((wr, "wr"), (tri, "tri"), (region, "region")):
                    sp.dma_start(t[:, :], a[n]).then_inc(c_in, 16)
                sp.wait_ge(ready0, 10)
                sp.dma_start(dispatch[NE * CAP:NE * CAP + P, :], zeros[:, :]).then_inc(zero_out, 16)
                sp.wait_ge(zero_out, 16)

            @block.gpsimd
            def _(po):
                po.memset(zeros[:, :], 0.0).then_inc(ready0, 1)
                po.memset(minus_half[:, :], -0.5).then_inc(ready0, 1)
                po.memset(ones_sq[:, :], 1.0).then_inc(ready0, 1)
                po.memset(rec[:, :, :], 0.0).then_inc(ready0, 1)
                po.memset(mask[:, :, :], 0.0).then_inc(ready0, 1)
                po.memset(logits[:, :, :], SENT).then_inc(ready0, 1)
                po.memset(mv[:, :, :], 1.0).then_inc(ready0, 1)
                po.memset(carry[:, :], 0.0).then_inc(ready0, 1)
                po.memset(ex[:, :, :], 1.0).then_inc(ready0, 1)
                po.wait_ge(ready0, 10)

                def body(i):
                    po.wait_ge(mv_ready, i + 1)
                    po.sem_inc(marker, 1)
                    po.tensor_scalar(rstd[:, :], mv[:, :, 1], EPS, None, ALU.add).then_inc(rstd_ready, 1)
                    po.wait_ge(rstd_ready, 2 * i + 1)
                    po.tensor_tensor(rstd[:, :], rstd[:, :], minus_half[:, :], ALU.pow).then_inc(rstd_ready, 1)
                    po.wait_ge(xn_ready, 3 * (i + 1))
                    po.sem_inc(marker, 1)
                    for t, n in PARTS:
                        po.tensor_tensor(base[0:n, 3 * i + t, :], source(i, t), rec[0:n, t, 0:D], ALU.add).then_inc(base_ready, 1)
                    po.wait_ge(gate_ready, i + 1)
                    po.sem_inc(marker, 1)
                    po.wait_ge(idx_ready, i + 1)
                    po.sem_inc(marker, 1)
                    for t, n in PARTS:
                        for k in range(KE):
                            po.indirect_dma_start(dispatch, bass.IndirectOffsetOnAxis(rows_i[0:n, t, k:k + 1], 0),
                                                  rec[0:n, t, :], None).then_inc(sent, 16)

                with po.Fori(0, PAIRS) as i:
                    body(i)
                po.wait_ge(sent, 16 * 3 * KE * PAIRS)

            @block.scalar
            def _(act):
                act.wait_ge(ready0, 10)

                def body(i):
                    act.wait_ge(nb_ready, i + 1)
                    act.sem_inc(marker, 1)
                    act.wait_ge(sent, i * (16 * 3 * KE)) if not isinstance(i, int) else None
                    act.sem_inc(marker, 1)
                    for t, n in PARTS:
                        act.activation(rec[0:n, t, 0:D], source(i, t), ACT.Identity, bias=nbias[0:n, t:t + 1],
                                       scale=rstd[0:n, t:t + 1]).then_inc(xn_ready, 1)
                    act.wait_ge(xT_done, i + 1)
                    act.activation(xT[:, :], b_xT[:, 0:PT], ACT.Copy).then_inc(xT_ready, 1)
                    act.activation(xT_all[:, bass.ds(i * PT, PT)], b_xT[:, 0:PT], ACT.Copy).then_inc(xT_ready, 1)
                    act.wait_ge(lg_done, i + 1)
                    act.activation(logits[:, 0:2, 0:NE], b_lg[:, 0:2, :], ACT.Copy).then_inc(lg_ready, 1)
                    act.activation(logits[0:T2, 2, 0:NE], b_lg[0:T2, 2, :], ACT.Copy).then_inc(lg_ready, 1)
                    act.wait_ge(nm_ready, i + 1)
                    for t, n in PARTS:
                        act.activation(ex[0:n, t, :], b_lg[0:n, t, :], ACT.Exp, bias=neg_max[0:n, t:t + 1]).then_inc(ex_ready, 1)

                body(0)
                with act.Fori(1, PAIRS) as i:
                    body(i)

            @block.tensor
            def _(pe):
                pe.wait_ge(c_in, 48)
                pe.wait_ge(ready0, 10)

                def body(i):
                    pe.wait_ge(xn_ready, 3 * (i + 1))
                    pe.sem_inc(marker, 1)
                    at = 0
                    for t, n in PARTS:
                        last = pe.transpose(b_xT[:, at:at + n], rec[0:n, t, 0:D], ident[0:n, 0:n])
                        at += n
                    last.then_inc(xT_done, 1)
                    pe.wait_ge(xT_ready, 2 * (i + 1))
                    pe.sem_inc(marker, 1)
                    at = 0
                    for t, n in PARTS:
                        last = pe.matmul(b_lg[0:n, t, :], xT[:, at:at + n], wr[:, :], start=True, stop=True)
                        at += n
                    last.then_inc(lg_done, 1)
                    pe.wait_ge(mask_ready, 2 * (i + 1))
                    pe.sem_inc(marker, 1)
                    for t, n in PARTS:
                        o = b_rank[:, t, :]
                        pe.matmul(o, ones[0:1, :], region[:, :], start=True, stop=False)
                        pe.matmul(o, ones_sq[:, :], carry[:, :], start=False, stop=False)
                        for before in range(t):
                            pe.matmul(o, ones_sq[:, :], mask[:, before, :], start=False, stop=False)
                        last = pe.matmul(o, tri[:, :], mask[:, t, :], start=False, stop=True)
                    last.then_inc(rank_done, 1)

                with pe.Fori(0, PAIRS) as i:
                    body(i)

            @block.vector
            def _(ve):
                ve.memset(base[64:P, :, :].rearrange("p (i t) d -> p i t d", t=3)[:, :, 2, :], 0.0).then_inc(ready0, 1)
                ve.wait_ge(ready0, 10)

                def body(i):
                    ve.sem_clear(dve)
                    n_ = [0]

                    def then(ins):
                        ins.then_inc(dve, 1)
                        n_[0] += 1

                    def settle():
                        ve.wait_ge(dve, n_[0])

                    for t, n in PARTS:
                        then(ve.bn_stats(stats[0:n, t, :], source(i, t)))
                    settle()
                    for t, n in PARTS:
                        then(ve.bn_aggr(mv[0:n, t, :], stats[0:n, t, :]))
                    settle()
                    ve.sem_inc(mv_ready, 1)
                    ve.wait_ge(rstd_ready, 2 * (i + 1))
                    ve.scalar_tensor_tensor(out=nbias[:, :], in0=mv[:, :, 0], scalar=-1.0, in1=rstd[:, :],
                                            op0=ALU.mult, op1=ALU.mult).then_inc(nb_ready, 1)
                    ve.wait_ge(lg_ready, 2 * (i + 1))
                    ve.sem_inc(marker, 1)
                    for t, n in PARTS:
                        then(ve.max(best[0:n, t, :], logits[0:n, t, 0:NE]))
                    settle()
                    for t, n in PARTS:
                        then(ve.tensor_scalar(neg_max[0:n, t:t + 1], best[0:n, t, 0:1], -1.0, None, ALU.mult))
                    settle()
                    ve.sem_inc(nm_ready, 1)
                    then(ve.memset(best[:, :, KE:8], SENT))
                    settle()
                    for t, n in PARTS:
                        then(ve.match_replace(taken[0:n, t, :], best[0:n, t, :], logits[0:n, t, :], MARK))
                    settle()
                    for lo, hi, n in ((0, 2, P), (2, 3, T2)):
                        then(ve.tensor_scalar(mask[0:n, lo:hi, :], taken[0:n, lo:hi, 0:NE], MARK, None, ALU.is_equal))
                    settle()
                    ve.sem_inc(mask_ready, 2)
                    ve.wait_ge(ex_ready, 3 * (i + 1))
                    then(ve.tensor_tensor(ex[:, :, :], ex[:, :, :], mask[:, :, :], ALU.mult))
                    settle()
                    then(ve.tensor_reduce(inv[:, :], ex[:, :, :], AX.X, ALU.add))
                    settle()
                    then(ve.reciprocal(inv[0:P, 0:2], inv[0:P, 0:2]))
                    then(ve.reciprocal(inv[0:T2, 2:3], inv[0:T2, 2:3]))
                    settle()
                    ve.tensor_tensor(rec[:, :, D:REC], ex[:, :, :],
                                     inv[:, :].rearrange("p (t a) -> p t a", a=1).broadcast_to([P, 3, NE]),
                                     ALU.mult).then_inc(gate_ready, 1)
                    ve.wait_ge(rank_done, i + 1)
                    then(ve.tensor_tensor(places[:, bass.ds(3 * i, 3), :], b_rank[:, :, :], mask[:, :, :], ALU.mult))
                    then(ve.tensor_reduce(chosen[:, :], mask[:, :, :].rearrange("p t e -> p e t"), AX.X, ALU.add))
                    settle()
                    then(ve.tensor_tensor(carry[:, :], carry[:, :], chosen[:, :], ALU.add))
                    for t, n in PARTS:
                        then(ve.tensor_tensor(ex[0:n, t, :], b_rank[0:n, t, :], mask[0:n, t, :], ALU.mult))
                    settle()
                    for t, n in PARTS:
                        then(ve.max(rows_f[0:n, t, :], ex[0:n, t, :]))
                    settle()
                    for lo, hi, n in ((0, 2, P), (2, 3, T2)):
                        then(ve.tensor_scalar(rows_i[0:n, lo:hi, :], rows_f[0:n, lo:hi, :], -1.0, None, ALU.add))
                    settle()
                    ve.sem_inc(idx_ready, 1)

                with ve.Fori(0, PAIRS) as i:
                    body(i)


def plan(nc, es, sb, bank, a, v):
    carry, places, where, table = v["carry"], v["places"], v["where"], v["table"]
    ident, ones = v["ident"], v["ones"]
    with ExitStack() as local:
        def lsb(name, shape, dt=F32):
            return sb(name, shape, dt, local)

        def sem(name):
            return local.enter_context(nc.semaphore(name))

        ones_sq = lsb("ones_sq3", [P, P])
        regions = lsb("regions", [P, NE])
        steps = lsb("steps", [P, 21])
        tile_no = lsb("tile_no", [P, 2])
        counts = lsb("counts", [P, NE])
        over = lsb("over", [P, NE, 21])
        n_tiles = lsb("n_tiles", [P, NE])
        ends = lsb("ends", [P, NE])
        delta = lsb("delta", [P, NE])
        one = lsb("one_row", [P, NE])
        past = lsb("past", [P, 2, NE])
        expert = lsb("expert", [P, 2])
        start = lsb("start", [P, 2])
        row = lsb("row", [P, 2])
        shifted = lsb("shifted", [P, 3 * PAIRS, NE])
        best = lsb("best3", [P, 3 * PAIRS, 8])
        b_cnt = bank("b_cnt", [P, 512], local)
        b_tab = bank("b_tab", [P, 4, P], local)
        c_in, set0, dve, cnt_done, cols_ready, tab_done = (sem(n) for n in ("c_in3", "set0", "dve3", "cnt_done", "cols_ready", "tab_done"))
        with nc.Block() as block:
            @block.sync
            def _(sp):
                for t, n in ((regions, "region_all"), (steps, "steps"), (tile_no, "tile_no")):
                    sp.dma_start(t[:, :], a[n]).then_inc(c_in, 16)

            @block.gpsimd
            def _(po):
                po.memset(ones_sq[:, :], 1.0).then_inc(set0, 1)
                po.memset(one[:, :], 1.0).then_inc(set0, 1)

            @block.tensor
            def _(pe):
                pe.wait_ge(set0, 2)
                pe.matmul(b_cnt[:, 0:NE], ones_sq[:, :], carry[:, :], start=True, stop=True).then_inc(cnt_done, 1)
                pe.wait_ge(cols_ready, 1)
                for j in range(2):
                    pe.matmul(b_tab[0:1, j, :], row[:, j:j + 1], ident[:, :], start=True, stop=True)
                    last = pe.matmul(b_tab[0:1, 2 + j, :], expert[:, j:j + 1], ident[:, :], start=True, stop=True)
                last.then_inc(tab_done, 1)

            @block.vector
            def _(ve):
                n_ = [0]

                def step(ins):
                    ins.then_inc(dve, 1)
                    n_[0] += 1
                    ve.wait_ge(dve, n_[0])

                def wide(t, shape):
                    return t.broadcast_to(shape)

                ve.wait_ge(c_in, 48)
                ve.wait_ge(set0, 2)
                ve.wait_ge(cnt_done, 1)
                step(ve.tensor_copy(counts[:, :], b_cnt[:, 0:NE]))
                step(ve.tensor_tensor(over[:, :, :], wide(counts[:, :].rearrange("p (e a) -> p e a", a=1), [P, NE, 21]),
                                      wide(steps[:, :].rearrange("p (a k) -> p a k", a=1), [P, NE, 21]), ALU.is_gt))
                step(ve.tensor_reduce(n_tiles[:, :], over[:, :, :], AX.X, ALU.add))
                step(ve.tensor_tensor_scan(ends[:, :], one[:, :], n_tiles[:, :], 0.0, ALU.mult, ALU.add))
                step(ve.tensor_tensor(delta[:, :], ends[:, :], n_tiles[:, :], ALU.subtract))
                step(ve.scalar_tensor_tensor(out=delta[:, :], in0=delta[:, :], scalar=float(P), in1=regions[:, :],
                                             op0=ALU.mult, op1=ALU.subtract))
                step(ve.tensor_tensor(past[:, :, :], wide(tile_no[:, :].rearrange("p (j a) -> p j a", a=1), [P, 2, NE]),
                                      wide(ends[:, :].rearrange("p (a e) -> p a e", a=1), [P, 2, NE]), ALU.is_ge))
                step(ve.tensor_reduce(expert[:, :], past[:, :, :], AX.X, ALU.add))
                step(ve.tensor_tensor(past[:, :, :], past[:, :, :],
                                      wide(n_tiles[:, :].rearrange("p (a e) -> p a e", a=1), [P, 2, NE]), ALU.mult))
                step(ve.tensor_reduce(start[:, :], past[:, :, :], AX.X, ALU.add))
                step(ve.tensor_tensor(row[:, :], tile_no[:, :], start[:, :], ALU.subtract))
                step(ve.tensor_scalar(row[:, :], row[:, :], float(P), None, ALU.mult))
                step(ve.scalar_tensor_tensor(out=row[:, :], in0=expert[:, :], scalar=float(CAP), in1=row[:, :],
                                             op0=ALU.mult, op1=ALU.add))
                step(ve.tensor_scalar(row[:, :], row[:, :], float(NE * CAP), None, ALU.min))
                step(ve.tensor_scalar(expert[:, :], expert[:, :], float(NE - 1), None, ALU.min))
                ve.sem_inc(cols_ready, 1)
                step(ve.tensor_tensor(table[0:1, 2, 0:NE], counts[0:1, :], regions[0:1, :], ALU.add))
                ve.wait_ge(tab_done, 1)
                step(ve.tensor_copy(table[0:1, 0:2, :], b_tab[0:1, :, :].rearrange("p (a j) t -> p a (j t)", a=2)))
                step(ve.tensor_scalar(shifted[:, :, :], places[:, :, :], 0.0, None, ALU.is_gt))
                step(ve.tensor_tensor(shifted[:, :, :], shifted[:, :, :],
                                      wide(delta[:, :].rearrange("p (a e) -> p a e", a=1), [P, 3 * PAIRS, NE]), ALU.mult))
                step(ve.tensor_tensor(shifted[:, :, :], shifted[:, :, :], places[:, :, :], ALU.add))
                for t in range(3 * PAIRS):
                    ins = ve.max(best[:, t, :], shifted[:, t, :]).then_inc(dve, 1)
                    n_[0] += 1
                ve.wait_ge(dve, n_[0])
                step(ve.tensor_scalar(where[:, :, :], best[:, :, :], -1.0, None, ALU.add))


def experts(nc, es, sb, bank, a, v):
    ident, w_gu, w_d, weights_in = v["ident"], v["w_gu"], v["w_d"], v["weights_in"]
    table, dispatch, results = v["table"], v["dispatch"], v["results"]
    TS = 2
    SB = 3
    STEPS = ETILES // TS
    BODIES = STEPS // SB
    assert STEPS * TS == ETILES and BODIES * SB == STEPS
    with ExitStack() as local:
        def lsb(name, shape, dt=F32):
            return sb(name, shape, dt, local)

        def sem(name):
            return local.enter_context(nc.semaphore(name))

        zeros = lsb("zeros4", [P, REC])
        rec = lsb("rec4", [P, SB, TS, REC])
        xT = lsb("xT4", [P, SB, TS, P])
        act_g = lsb("act_g", [P, SB, TS, D])
        hid = lsb("hid", [P, SB, TS, D])
        hT = lsb("hT", [P, SB, TS, P])
        y = lsb("y4", [P, SB, TS, D])
        b_xT = bank("b_xT4", [P, TS, P], local)
        b_gu = [bank(f"b_gu{j}", [P, TS, 2 * D], local) for j in range(SB)]
        b_hT = bank("b_hT4", [P, TS, P], local)
        b_y = [bank(f"b_y{j}", [P, TS, D], local) for j in range(SB)]
        marker = sem("marker4")
        z_ready, z_out = sem("z_ready"), sem("z_out")
        rec_in = [sem(f"rec_in{j}") for j in range(SB)]
        xT_done = sem("xT_done4")
        xT_ready = sem("xT_ready4")
        gu_done = sem("gu_done")
        silu_ready = sem("silu_ready")
        hid_ready = sem("hid_ready")
        hT_done = sem("hT_done4")
        hT_ready = sem("hT_ready4")
        y_done = sem("y_done4")
        y_ready = sem("y_ready4")
        y_ready_d = sem("y_ready4d")
        stored = [sem(f"stored{j}") for j in range(SB)]

        def loop(eng, body):
            body(0, True, False)
            with eng.Fori(1, BODIES - 1) as i:
                body(i, False, False)
            body(BODIES - 1, False, True)

        def of_step(s):
            return s % SB

        def tile_value(eng, n, tile, hi):
            at = table[0:1, n, tile:tile + 1] if isinstance(tile, int) else table[0:1, n, bass.ds(tile, 1)]
            return eng.value_load(at, min_val=0, max_val=hi)

        with nc.Block() as block:
            @block.sync
            def _(sp):
                sp.wait_ge(z_ready, 1)
                with sp.Fori(0, NE) as e:
                    sp.dma_start(dispatch[bass.ds(tile_value(sp, 2, e, NE * CAP), P), :], zeros[:, :]).then_inc(z_out, 16)
                sp.wait_ge(z_out, 16 * NE)

                def load(j, i, s):
                    if isinstance(s, int) and s < SB:
                        pass
                    else:
                        sp.wait_ge(xT_done, s - SB + 1)
                        sp.sem_inc(marker, 1)
                        sp.wait_ge(y_ready, s - SB + 1)
                        sp.sem_inc(marker, 1)
                        sp.wait_ge(y_ready_d, s - SB + 1)
                        sp.sem_inc(marker, 1)
                    for t in range(TS):
                        r = tile_value(sp, 0, TS * s + t, NE * CAP)
                        sp.dma_start(rec[:, j, t, :], dispatch[bass.ds(r, P), :]).then_inc(rec_in[j], 16)

                for j in range(SB):
                    load(j, 0, j)
                with sp.Fori(1, BODIES) as i:
                    for j in range(SB):
                        load(j, i, SB * i + j)

            @block.gpsimd
            def _(po):
                po.memset(zeros[:, :], 0.0).then_inc(z_ready, 1)

                def body(i, first, last):
                    for j in range(SB):
                        s = SB * i + j
                        po.wait_ge(y_ready, s + 1)
                        po.sem_inc(marker, 1)
                        po.wait_ge(y_ready_d, s + 1)
                        po.sem_inc(marker, 1)
                        row = TS * P * s
                        dst = results[row:row + TS * P, :] if isinstance(row, int) else results[bass.ds(row, TS * P), :]
                        po.dma_start(dst.rearrange("(t p) d -> p t d", t=TS), y[:, j, :, :]).then_inc(stored[j], 16)

                loop(po, body)
                for j in range(SB):
                    po.wait_ge(stored[j], 16 * BODIES)

            @block.tensor
            def _(pe):
                pe.wait_ge(weights_in, 16 * 12)

                def transposes(j, i, s):
                    pe.wait_ge(rec_in[j], 16 * TS * (i + 1))
                    pe.sem_inc(marker, 1)
                    if not (isinstance(s, int) and s == 0):
                        pe.wait_ge(xT_ready, s)
                        pe.sem_inc(marker, 1)
                    for t in range(TS):
                        last = pe.transpose(b_xT[:, t, :], rec[:, j, t, 0:D], ident[:, :])
                    last.then_inc(xT_done, 1)

                def gate_up(j, s):
                    es_ = [tile_value(pe, 1, TS * s + t, NE - 1) for t in range(TS)]
                    pe.wait_ge(xT_ready, s + 1)
                    pe.sem_inc(marker, 1)
                    if not (isinstance(s, int) and s < SB):
                        pe.wait_ge(hid_ready, s - SB + 1)
                        pe.sem_inc(marker, 1)
                    for t in range(TS):
                        last = pe.matmul(b_gu[j][:, t, :], xT[:, j, t, :], w_gu[:, bass.ds(es_[t], 1), :].rearrange("p a n -> p (a n)"),
                                         start=True, stop=True)
                    last.then_inc(gu_done, 1)

                def hidden_transposes(j, s):
                    pe.wait_ge(hid_ready, s + 1)
                    pe.sem_inc(marker, 1)
                    if not (isinstance(s, int) and s == 0):
                        pe.wait_ge(hT_ready, s)
                        pe.sem_inc(marker, 1)
                    for t in range(TS):
                        last = pe.transpose(b_hT[:, t, :], hid[:, j, t, :], ident[:, :])
                    last.then_inc(hT_done, 1)

                def down(j, s):
                    es_ = [tile_value(pe, 1, TS * s + t, NE - 1) for t in range(TS)]
                    pe.wait_ge(hT_ready, s + 1)
                    pe.sem_inc(marker, 1)
                    if not (isinstance(s, int) and s < SB):
                        pe.wait_ge(y_ready, s - SB + 1)
                        pe.sem_inc(marker, 1)
                        pe.wait_ge(y_ready_d, s - SB + 1)
                        pe.sem_inc(marker, 1)
                    for t in range(TS):
                        last = pe.matmul(b_y[j][:, t, :], hT[:, j, t, :], w_d[:, bass.ds(es_[t], 1), :].rearrange("p a n -> p (a n)"),
                                         start=True, stop=True)
                    last.then_inc(y_done, 1)

                def body(i, first, last):
                    for j in range(SB):
                        s = SB * i + j
                        if not (last and j == SB - 1):
                            gate_up((j + 1) % SB, s + 1)
                        hidden_transposes(j, s)
                        if not (first and j == 0):
                            down((j - 1) % SB, s - 1)
                        if not (last and j >= SB - 2):
                            transposes((j + 2) % SB, i + (j + 2) // SB, s + 2)

                transposes(0, 0, 0)
                gate_up(0, 0)
                transposes(1, 0, 1)
                loop(pe, body)
                down(SB - 1, STEPS - 1)

            @block.scalar
            def _(act):
                def body(i, first, last):
                    for j in range(SB):
                        s = SB * i + j
                        act.wait_ge(gu_done, s + 1)
                        act.sem_inc(marker, 1)
                        if not (isinstance(s, int) and s < SB):
                            act.wait_ge(hid_ready, s - SB + 1)
                            act.sem_inc(marker, 1)
                        act.activation(act_g[:, j, :, :], b_gu[j][:, :, 0:D], ACT.Silu).then_inc(silu_ready, 1)
                        act.wait_ge(hT_done, s + 1)
                        act.sem_inc(marker, 1)
                        if not (isinstance(s, int) and s < SB):
                            act.wait_ge(y_done, s - SB + 1)
                            act.sem_inc(marker, 1)
                        act.activation(hT[:, j, :, :], b_hT[:, :, :], ACT.Copy).then_inc(hT_ready, 1)
                        if not (first and j == 0):
                            scale_y((j - 1) % SB, i - (1 if j == 0 else 0), s - 1)

                def scale_y(j, i, s):
                    e = tile_value(act, 1, TS * s, NE - 1)
                    act.wait_ge(y_done, s + 1)
                    act.sem_inc(marker, 1)
                    act.wait_ge(y_ready_d, s + 1)
                    act.sem_inc(marker, 1)
                    if not (isinstance(i, int) and i == 0):
                        act.wait_ge(stored[j], 16 * i)
                        act.sem_inc(marker, 1)
                    act.activation(y[:, j, 0, :], b_y[j][:, 0, :], ACT.Copy,
                                   scale=rec[:, j, 0, bass.ds(D + e, 1)]).then_inc(y_ready, 1)

                loop(act, body)
                scale_y(SB - 1, BODIES - 1, STEPS - 1)

            @block.vector
            def _(ve):
                def take_xT(j, s):
                    ve.wait_ge(xT_done, s + 1)
                    ve.sem_inc(marker, 1)
                    if not (isinstance(s, int) and s < SB):
                        ve.wait_ge(gu_done, s - SB + 1)
                        ve.sem_inc(marker, 1)
                    ve.tensor_copy(xT[:, j, :, :], b_xT[:, :, :]).then_inc(xT_ready, 1)

                def scale_y(j, i, s):
                    e = tile_value(ve, 1, TS * s + 1, NE - 1)
                    ve.wait_ge(y_done, s + 1)
                    ve.sem_inc(marker, 1)
                    if not (isinstance(i, int) and i == 0):
                        ve.wait_ge(stored[j], 16 * i)
                        ve.sem_inc(marker, 1)
                    ve.tensor_scalar(y[:, j, 1, :], b_y[j][:, 1, :], rec[:, j, 1, bass.ds(D + e, 1)], None,
                                     ALU.mult).then_inc(y_ready_d, 1)

                def body(i, first, last):
                    for j in range(SB):
                        s = SB * i + j
                        ve.wait_ge(silu_ready, s + 1)
                        ve.sem_inc(marker, 1)
                        if not (isinstance(s, int) and s < SB):
                            ve.wait_ge(hT_done, s - SB + 1)
                            ve.sem_inc(marker, 1)
                        ve.tensor_tensor(hid[:, j, :, :], act_g[:, j, :, :], b_gu[j][:, :, D:2 * D], ALU.mult).then_inc(hid_ready, 1)
                        if not (first and j == 0):
                            scale_y((j - 1) % SB, i - (1 if j == 0 else 0), s - 1)
                        if not (last and j >= SB - 2):
                            take_xT((j + 2) % SB, s + 2)

                take_xT(0, 0)
                take_xT(1, 1)
                loop(ve, body)
                scale_y(SB - 1, BODIES - 1, STEPS - 1)


def combine(nc, es, sb, bank, a, out, v):
    w_gu, w_d = v["w_gu"], v["w_d"]
    base, xT_all, where, results = v["base"], v["xT_all"], v["where"], v["results"]
    PARTS = ((0, P), (1, P), (2, T2))
    with ExitStack() as local:
        def lsb(name, shape, dt=F32):
            return sb(name, shape, dt, local)

        def sem(name):
            return local.enter_context(nc.semaphore(name))

        idx = lsb("idx", [P, 2, 3, 8], I32)
        got = lsb("got", [P, 2, 3, KE, D])
        total = lsb("total", [P, 2, 3, D])
        act_g = lsb("act_g5", [P, NS, PT])
        hT = lsb("hT5", [P, NS, PT])
        b_g = [bank(f"b_g{e}", [P, 512], local) for e in range(NS)]
        b_u = [bank(f"b_u{e}", [P, 512], local) for e in range(NS)]
        b_y = [bank(f"b_y5{u}", [P, 3, D], local) for u in range(2)]
        zeroed = sem("zeroed5")
        marker = sem("marker5")
        idx_ready = sem("idx_ready5")
        gathered = [sem(f"gathered{u}") for u in range(2)]
        gu_done = sem("gu_done5")
        silu_ready = sem("silu_ready5")
        h_ready = sem("h_ready5")
        y_done = sem("y_done5")
        sum_ready = sem("sum_ready5")
        total_ready = sem("total_ready")
        out_done = [sem(f"out_done{u}") for u in range(2)]

        def loop(eng, body):
            body(0, True)
            with eng.Fori(1, PAIRS // 2) as i:
                body(i, False)

        with nc.Block() as block:
            @block.gpsimd
            def _(po):
                po.memset(got[:, :, :, :, :], 0.0).then_inc(zeroed, 1)
                po.wait_ge(zeroed, 1)

                def body(i, first):
                    for u in range(2):
                        n = 2 * i + u
                        po.wait_ge(idx_ready, n + 1)
                        po.sem_inc(marker, 1)
                        if not first:
                            po.wait_ge(sum_ready, 3 * (n - 2) + 1)
                            po.sem_inc(marker, 1)
                        for t, r in PARTS:
                            for k in range(KE):
                                po.indirect_dma_start(got[0:r, u, t, k, :], None, results,
                                                      bass.IndirectOffsetOnAxis(idx[0:r, u, t, k:k + 1], 0)).then_inc(gathered[u], 16)

                loop(po, body)

            @block.tensor
            def _(pe):
                def body(i, first):
                    for u in range(2):
                        n = 2 * i + u
                        x = xT_all[:, n * PT:(n + 1) * PT] if first else xT_all[:, bass.ds(n * PT, PT)]
                        if not (first and u == 0):
                            pe.wait_ge(h_ready, 2 * n)
                            pe.sem_inc(marker, 1)
                        for e in range(NS):
                            pe.matmul(b_g[e][:, 0:PT], w_gu[:, NE + e, 0:D], x, start=True, stop=True)
                            last = pe.matmul(b_u[e][:, 0:PT], w_gu[:, NE + e, D:2 * D], x, start=True, stop=True)
                        last.then_inc(gu_done, 1)
                        pe.wait_ge(h_ready, 2 * (n + 1))
                        pe.sem_inc(marker, 1)
                        if not first:
                            pe.wait_ge(sum_ready, 3 * (n - 1))
                            pe.sem_inc(marker, 1)
                        at = 0
                        for t, r in PARTS:
                            for e in range(NS):
                                last = pe.matmul(b_y[u][0:r, t, :], hT[:, e, at:at + r], w_d[:, NE + e, :],
                                                 start=(e == 0), stop=(e == NS - 1))
                            at += r
                        last.then_inc(y_done, 1)

                loop(pe, body)

            @block.scalar
            def _(act):
                def body(i, first):
                    for u in range(2):
                        n = 2 * i + u
                        act.wait_ge(gu_done, n + 1)
                        act.sem_inc(marker, 1)
                        if not (first and u == 0):
                            act.wait_ge(h_ready, 2 * n)
                            act.sem_inc(marker, 1)
                        for e in range(NS):
                            act.activation(act_g[:, e, :], b_g[e][:, 0:PT], ACT.Silu).then_inc(silu_ready, 1)

                loop(act, body)

            @block.vector
            def _(ve):
                def body(i, first):
                    for u in range(2):
                        n = 2 * i + u
                        if not first:
                            ve.wait_ge(gathered[u], 16 * 3 * KE * i)
                            ve.sem_inc(marker, 1)
                        w = where[:, 3 * n:3 * n + 3, :] if first else where[:, bass.ds(3 * n, 3), :]
                        ve.tensor_copy(idx[:, u, :, :], w).then_inc(idx_ready, 1)
                    for u in range(2):
                        n = 2 * i + u
                        ve.wait_ge(silu_ready, 2 * (n + 1))
                        ve.sem_inc(marker, 1)
                        if not (first and u == 0):
                            ve.wait_ge(y_done, n)
                            ve.sem_inc(marker, 1)
                        for e in range(NS):
                            ve.tensor_tensor(hT[:, e, :], act_g[:, e, :], b_u[e][:, 0:PT], ALU.mult).then_inc(h_ready, 1)
                        if not first:
                            ve.wait_ge(out_done[u], 16 * 4 * i)
                            ve.sem_inc(marker, 1)
                        ve.wait_ge(gathered[u], 16 * 3 * KE * (i + 1))
                        ve.sem_inc(marker, 1)
                        ve.tensor_reduce(total[:, u, :, :], got[:, u, :, :, :].rearrange("p t k d -> p t d k"), AX.X,
                                         ALU.add).then_inc(sum_ready, 1)
                        ve.wait_ge(sum_ready, 3 * n + 1)
                        bs = base[:, 3 * n:3 * n + 3, :] if first else base[:, bass.ds(3 * n, 3), :]
                        ve.tensor_tensor(total[:, u, :, :], total[:, u, :, :], bs, ALU.add).then_inc(sum_ready, 1)
                        ve.wait_ge(sum_ready, 3 * n + 2)
                        ve.sem_inc(marker, 1)
                        ve.wait_ge(y_done, n + 1)
                        ve.tensor_tensor(total[:, u, 0:2, :], total[:, u, 0:2, :], b_y[u][:, 0:2, :], ALU.add).then_inc(total_ready, 1)
                        ve.tensor_tensor(total[0:T2, u, 2, :], total[0:T2, u, 2, :], b_y[u][0:T2, 2, :], ALU.add).then_inc(sum_ready, 1)

                loop(ve, body)

            @block.sync
            def _(sp):
                def body(i, first):
                    for u in range(2):
                        n = 2 * i + u
                        sp.wait_ge(total_ready, n + 1)
                        sp.sem_inc(marker, 1)
                        sp.wait_ge(sum_ready, 3 * (n + 1))
                        sp.sem_inc(marker, 1)
                        for w in range(2):
                            b = 2 * n + w
                            o = out[b, :, :] if first else out[bass.ds(b, 1), :, :].rearrange("a l d -> (a l) d")
                            sp.dma_start(o[NP_:L, :], total[:, u, w, :]).then_inc(out_done[u], 16)
                            sp.dma_start(o[0:NP_, :], total[w * NP_:(w + 1) * NP_, u, 2, :]).then_inc(out_done[u], 16)

                loop(sp, body)
                for u in range(2):
                    sp.wait_ge(out_done[u], 16 * 4 * (PAIRS // 2))


def kernel(**inputs):
    import concourse.bacc as bacc
    from concourse.bass_utils import run_bass_kernel_spmd

    x = {n.replace("L0_", ""): np.asarray(t) for n, t in inputs.items()}
    f32 = np.float32
    arrays = {}
    p = x["x"].reshape(B, 3, 6, 16, 6, 16).transpose(1, 3, 5, 0, 2, 4).reshape(CHUNKS, P, B * NP_)
    arrays["patches"] = np.ascontiguousarray(p.transpose(1, 0, 2))
    w_all = np.zeros((3, 16, 16, D), f32)
    w_all[..., 0:64] = x["tok_W_main"].reshape(64, 3, 16, 16).transpose(1, 2, 3, 0)
    sx = x["tok_W_sx"].reshape(16, 3, 16, 16).transpose(1, 2, 3, 0)
    sy = x["tok_W_sy"].reshape(16, 3, 16, 16).transpose(1, 2, 3, 0)
    w_all[:, :, 0:8, 64:80] = sx[:, :, 8:16]
    w_all[:, :, 8:16, 80:96] = sx[:, :, 0:8]
    w_all[:, 0:8, :, 96:112] = sy[:, 8:16]
    w_all[:, 8:16, :, 112:128] = sy[:, 0:8]
    arrays["w_all"] = np.ascontiguousarray(w_all.reshape(CHUNKS, P, D).transpose(1, 0, 2))
    perm = np.zeros((P, 5, D), f32)
    lo, hi, ylo, yhi = 64, 80, 96, 112
    for k in range(64):
        perm[k, 0, k] = 1
    for k in range(16):
        perm[hi + k, 0, 64 + k] = perm[lo + k, 0, 80 + k] = perm[yhi + k, 0, 96 + k] = perm[ylo + k, 0, 112 + k] = 1
        perm[lo + k, 1, 64 + k] = 1
        perm[hi + k, 2, 80 + k] = 1
        perm[ylo + k, 3, 96 + k] = 1
        perm[yhi + k, 4, 112 + k] = 1
    arrays["perm"] = perm
    arrays["ident"] = np.eye(P, dtype=f32)
    arrays["shift36"] = np.eye(NP_, 2 * NP_, k=NP_, dtype=f32)
    mask = np.zeros((P, H), f32)
    for h in range(H):
        mask[h * E:(h + 1) * E, h] = E ** -0.5
    arrays["head_mask"] = mask
    arrays["b_tok"] = np.concatenate([x["tok_b_main"], x["tok_b_sx"], x["tok_b_sx"], x["tok_b_sy"],
                                      x["tok_b_sy"]]).reshape(P, 1)
    arrays["rows"] = np.concatenate([x["attn_bv"], x["attn_bo"]]).reshape(1, 2 * D)
    for n in "qkvo":
        arrays["w" + n] = np.ascontiguousarray(x["attn_W" + n].T)
    for n in "qk":
        arrays["b" + n] = x["attn_b" + n].reshape(P, 1)
    arrays["ln_g"], arrays["ln_b"] = x["tok_ln_g"], x["tok_ln_b"]
    for n in ("g", "u", "d"):
        arrays["w_" + n] = np.concatenate([x["ffn_W" + n], x["ffn_sW" + n]]).transpose(1, 0, 2)
    arrays["w_gu"] = np.ascontiguousarray(np.concatenate([arrays.pop("w_g"), arrays.pop("w_u")], axis=2))
    arrays["w_d"] = np.ascontiguousarray(arrays["w_d"])
    arrays["wr"] = x["ffn_Wr"]
    arrays["tri"] = np.triu(np.ones((P, P), f32), 1)
    arrays["region"] = (np.arange(NE, dtype=f32) * CAP + 1).reshape(1, NE)
    arrays["region_all"] = np.tile(np.arange(NE, dtype=f32) * CAP, (P, 1))
    arrays["steps"] = np.tile(np.arange(21, dtype=f32) * P, (P, 1))
    arrays["tile_no"] = np.arange(2 * P, dtype=f32).reshape(2, P).T.copy()
    arrays["txt"] = np.ascontiguousarray(x["txt"].transpose(1, 0, 2))

    nc = bacc.Bacc("TRN2", target_bir_lowering=False, num_devices=1)
    aps = {n: nc.dram_tensor("in_" + n, t.shape, mybir.dt.from_np(t.dtype), kind="ExternalInput").ap() for n, t in arrays.items()}
    out = nc.dram_tensor("out_h", (B, L, D), F32, kind="ExternalOutput").ap()
    build(nc, aps, out)
    r = run_bass_kernel_spmd(nc, [{"in_" + n: t for n, t in arrays.items()}], core_ids=[0])
    return r.results[0]["out_h"]
```

```python
from contextlib import ExitStack

import concourse.bass as bass
import numpy as np
from concourse import mybir

F32 = mybir.dt.float32
I32 = mybir.dt.int32
ALU = mybir.AluOpType
ACT = mybir.ActivationFunctionType
AX = mybir.AxisListType

P = 128
B = 16
D = 128
NP_ = 36
NT = 128
L = NP_ + NT
H = 8
E = D // H
ROWS = H * L
PAIRS = B // 2
TILES = 2 * ROWS // P + 1
GT = 3
GROUPS = TILES // GT
MID = ROWS // P
TAIL = ROWS - MID * P
TOPK = 25
EPS = 1e-5
MARK = -3.0e38
CHUNKS = 6


NE = 64
NS = 2
KE = 6
T2 = 2 * NP_
PT = 2 * L
TOKENS = B * L
CAP = P + TOKENS
REC = D + NE
TS = 2
SB = 6
MOST = (TOKENS * KE + NE * (P - 1)) // P
ETILES = -(-MOST // (TS * SB)) * TS * SB
SENT = -2.9e38


def slot(g):
    return g % 3 if g < GROUPS - 1 else 3


def s_bank(g):
    return g % 2 if g < GROUPS - 1 else 2


def build(nc, a, out):
    es = ExitStack()
    with es:
        def sb(name, shape, dt=F32, where=es):
            return where.enter_context(nc.sbuf_tensor(name, shape, dt))

        def bank(name, shape, where):
            return where.enter_context(nc.psum_tensor(name, shape, F32))

        ident = sb("ident", [P, P])
        h_text = sb("h_text", [P, B, D])
        h_patch = sb("h_patch", [NP_, B, D])
        h2_patch = sb("h2_patch", [2 * NP_, PAIRS, D])
        shift36 = sb("shift36", [NP_, 2 * NP_])
        rows = sb("rows", [1, 2 * D])
        ones = sb("ones", [1, P])
        rstd_t = sb("rstd_t", [P, B])
        nbias_t = sb("nbias_t", [P, B])
        rstd_p = sb("rstd_p", [NP_, B])
        nbias_p = sb("nbias_p", [NP_, B])
        wq = sb("wq", [P, D])
        wk = sb("wk", [P, D])
        wv = sb("wv", [P, D])
        wo = sb("wo", [P, D])
        bq = sb("bq", [P, 1])
        bk = sb("bk", [P, 1])
        head_mask = sb("head_mask", [P, H])
        w_gu = sb("w_gu", [P, NE + NS, 2 * D])
        w_d = sb("w_d", [P, NE + NS, D])
        wr = sb("wr", [P, NE])
        tri = sb("tri", [P, P])
        ones_sq = sb("ones_sq", [P, P])
        region = sb("region", [1, NE])
        zeros = sb("zeros", [P, REC])
        weights_in = es.enter_context(nc.semaphore("weights_in"))
        dispatch = nc.dram_tensor("dispatch", (NE * CAP, REC), F32).ap()
        results = nc.dram_tensor("results", (ETILES * P, D), F32).ap()
        prologue(nc, es, sb, bank, a, dict(locals()))
        attention(nc, es, sb, bank, a, dict(locals()))
        base = sb("base", [P, 3 * PAIRS, D])
        xT_all = sb("xT_all", [P, PAIRS * PT])
        places = sb("places", [P, 3 * PAIRS, NE])
        carry = sb("carry", [P, NE])
        route(nc, es, sb, bank, a, dict(locals()))
        where = sb("where", [P, 3 * PAIRS, 8], I32)
        table = sb("table", [1, 2, 2 * P], I32)
        plan(nc, es, sb, bank, a, dict(locals()))
        experts(nc, es, sb, bank, a, dict(locals()))
        combine(nc, es, sb, bank, a, out, dict(locals()))


def prologue(nc, es, sb, bank, a, v):
    ident, h_text, h_patch, rows, ones = v["ident"], v["h_text"], v["h_patch"], v["rows"], v["ones"]
    with ExitStack() as local:
        def lsb(name, shape, dt=F32):
            return sb(name, shape, dt, local)

        def sem(name):
            return local.enter_context(nc.semaphore(name))

        patches = lsb("patches", [P, CHUNKS, B * NP_])
        w_all = lsb("w_all", [P, CHUNKS, D])
        perm = lsb("perm", [P, 5, D])
        grid = lsb("grid", [P, B, 8, 8])
        tok_T = lsb("tok_T", [P, B * NP_])
        b_tok = lsb("b_tok", [P, 1])
        gain = lsb("gain", [NP_, D])
        shiftb = lsb("shiftb", [NP_, D])
        stats_p = lsb("stats_p", [NP_, B, 6])
        stats_t = lsb("stats_t", [P, B, 6])
        mv_p = lsb("mv_p", [NP_, B, 2])
        mv_t = lsb("mv_t", [P, B, 2])
        sd_p = lsb("sd_p", [NP_, B])
        sd_t = lsb("sd_t", [P, B])
        ps_u = [bank(f"ps_u{i}", [P, 512], local) for i in range(2)]
        ps_tok = [bank(f"ps_tok{i}", [P, 4, D], local) for i in range(4)]
        w_in, c_in, t_in = sem("w_in"), sem("c_in"), sem("t_in")
        p_in = [sem(f"p_in{c}") for c in range(CHUNKS)]
        b_in = sem("b_in")
        proj_done, grid_zero, grid_ready, tok_ready = sem("proj_done"), sem("grid_zero"), sem("grid_ready"), sem("tok_ready")
        sum_ready, tokT_ready = sem("sum_ready"), sem("tokT_ready")
        dve, sd_ready, var_ready = sem("dve"), sem("sd_ready"), sem("var_ready")
        SPLIT = 14
        with nc.Block() as block:
            @block.sync
            def _(sp):
                sp.dma_start(w_all[:, :, :], a["w_all"]).then_inc(w_in, 16)
                for c in range(CHUNKS):
                    sp.dma_start(patches[:, c, :], a["patches"][:, c, :]).then_inc(p_in[c], 16)
                sp.dma_start(h_text[:, :, :], a["txt"]).then_inc(t_in, 16)

            @block.scalar
            def _(act):
                for t, n in ((ident, "ident"), (perm, "perm"), (v["shift36"], "shift36"), (rows, "rows"),
                             (v["wq"], "wq"), (v["wk"], "wk"), (v["wv"], "wv"), (v["wo"], "wo"),
                             (v["bq"], "bq"), (b_tok, "b_tok"), (v["bk"], "bk"), (v["head_mask"], "head_mask")):
                    act.dma_start(t.ap() if hasattr(t, "ap") else t[:], a[n]).then_inc(c_in, 16)
                act.dma_start(gain[:, :], a["ln_g"].partition_broadcast(NP_)).then_inc(b_in, 16)
                act.dma_start(shiftb[:, :], a["ln_b"].partition_broadcast(NP_)).then_inc(b_in, 16)
                act.wait_ge(grid_zero, 1)
                act.wait_ge(proj_done, 1)
                act.activation(grid[:, 0:SPLIT, 1:7, 1:7],
                               ps_u[0][:, 0:SPLIT * NP_].rearrange("p (b i j) -> p b i j", b=SPLIT, i=6),
                               ACT.Copy).then_inc(grid_ready, 1)
                act.wait_ge(proj_done, 2)
                act.activation(grid[:, SPLIT:B, 1:7, 1:7],
                               ps_u[1][:, 0:(B - SPLIT) * NP_].rearrange("p (b i j) -> p b i j", b=B - SPLIT, i=6),
                               ACT.Copy).then_inc(grid_ready, 1)
                for half, (lo, hi) in enumerate(((0, SPLIT), (SPLIT, B))):
                    act.wait_ge(c_in, 16 * 12)
                    act.wait_ge(sum_ready, half + 1)
                    act.activation(tok_T[:, lo * NP_:hi * NP_], ps_u[half][:, 0:(hi - lo) * NP_], ACT.Identity,
                                   bias=b_tok[:, 0:1]).then_inc(tokT_ready, 1)
                act.wait_ge(var_ready, 1)
                act.activation(sd_t[:, :], mv_t[:, :, 1], ACT.Sqrt).then_inc(sd_ready, 1)
                act.wait_ge(var_ready, 2)
                act.activation(sd_p[:, :], mv_p[:, :, 1], ACT.Sqrt).then_inc(sd_ready, 1)
                act.wait_ge(var_ready, 3)
                act.activation(sd_p[:, :], mv_p[:, :, 1], ACT.Sqrt).then_inc(sd_ready, 1)

            @block.tensor
            def _(pe):
                pe.wait_ge(w_in, 16)
                for half, (lo, hi) in enumerate(((0, SPLIT), (SPLIT, B))):
                    for c in range(CHUNKS):
                        if half == 0:
                            pe.wait_ge(p_in[c], 16)
                        last = pe.matmul(ps_u[half][:, 0:(hi - lo) * NP_], w_all[:, c, :],
                                         patches[:, c, lo * NP_:hi * NP_], start=(c == 0), stop=(c == CHUNKS - 1))
                    last.then_inc(proj_done, 1)
                pe.wait_ge(c_in, 16 * 12)
                for half, (lo, hi) in enumerate(((0, SPLIT), (SPLIT, B))):
                    pe.wait_ge(grid_ready, half + 1)
                    for s, (di, dj) in enumerate(((0, 0), (0, 1), (0, -1), (1, 0), (-1, 0))):
                        last = pe.matmul(ps_u[half][:, 0:(hi - lo) * NP_].rearrange("p (b i j) -> p b i j", i=6, j=6),
                                         perm[:, s, :], grid[:, lo:hi, 1 + di:7 + di, 1 + dj:7 + dj],
                                         start=(s == 0), stop=(s == 4))
                    last.then_inc(sum_ready, 1)
                for b in range(B):
                    pe.wait_ge(tokT_ready, 1 if b < SPLIT else 2)
                    pe.transpose(ps_tok[b // 4][0:NP_, b % 4, :], tok_T[:, b * NP_:(b + 1) * NP_],
                                 ident[:, :]).then_inc(tok_ready, 1)

            @block.vector
            def _(ve):
                n = [0]

                def then(ins):
                    ins.then_inc(dve, 1)
                    n[0] += 1

                def settle():
                    ve.wait_ge(dve, n[0])

                ve.memset(grid[:, :, :, :], 0.0).then_inc(grid_zero, 1)
                then(ve.memset(ones[:, :], 1.0))
                ve.wait_ge(t_in, 16)
                for b in range(B):
                    then(ve.bn_stats(stats_t[:, b, :], h_text[:, b, :]))
                settle()
                for b in range(B):
                    then(ve.bn_aggr(mv_t[:, b, :], stats_t[:, b, :]))
                settle()
                ve.tensor_scalar(mv_t[:, :, 1], mv_t[:, :, 1], EPS, None, ALU.add).then_inc(var_ready, 1)
                for b in range(B):
                    ve.wait_ge(tok_ready, b // 4 * 4 + 4)
                    then(ve.bn_stats(stats_p[:, b, :], ps_tok[b // 4][0:NP_, b % 4, :]))
                settle()
                for b in range(B):
                    then(ve.bn_aggr(mv_p[:, b, :], stats_p[:, b, :]))
                settle()
                ve.tensor_scalar(mv_p[:, :, 1], mv_p[:, :, 1], EPS, None, ALU.add).then_inc(var_ready, 1)
                ve.wait_ge(sd_ready, 2)
                then(ve.reciprocal(sd_p[:, :], sd_p[:, :]))
                settle()
                for b in range(B):
                    then(ve.tensor_scalar(h_patch[:, b, :], ps_tok[b // 4][0:NP_, b % 4, :], mv_p[:, b, 0:1],
                                          sd_p[:, b:b + 1], ALU.subtract, ALU.mult))
                ve.wait_ge(b_in, 32)
                settle()
                then(ve.tensor_tensor(h_patch[:, :, :], h_patch[:, :, :],
                                      gain[:, :].rearrange("p (a d) -> p a d", a=1).broadcast_to([NP_, B, D]), ALU.mult))
                settle()
                then(ve.tensor_tensor(h_patch[:, :, :], h_patch[:, :, :],
                                      shiftb[:, :].rearrange("p (a d) -> p a d", a=1).broadcast_to([NP_, B, D]), ALU.add))
                settle()
                for b in range(B):
                    then(ve.bn_stats(stats_p[:, b, :], h_patch[:, b, :]))
                settle()
                for b in range(B):
                    then(ve.bn_aggr(mv_p[:, b, :], stats_p[:, b, :]))
                settle()
                ve.tensor_scalar(mv_p[:, :, 1], mv_p[:, :, 1], EPS, None, ALU.add).then_inc(var_ready, 1)
                then(ve.reciprocal(v["rstd_t"][:, :], sd_t[:, :]))
                ve.wait_ge(sd_ready, 3)
                then(ve.reciprocal(v["rstd_p"][:, :], sd_p[:, :]))
                settle()
                for mv, rstd, nb in ((mv_t, "rstd_t", "nbias_t"), (mv_p, "rstd_p", "nbias_p")):
                    then(ve.scalar_tensor_tensor(out=v[nb][:, :], in0=mv[:, :, 0], scalar=-1.0, in1=v[rstd][:, :],
                                                 op0=ALU.mult, op1=ALU.mult))
                settle()


def attention(nc, es, sb, bank, a, v):
    ident, h_text, h_patch, rows, ones = v["ident"], v["h_text"], v["h_patch"], v["rows"], v["ones"]
    h2_patch, shift36, head_mask = v["h2_patch"], v["shift36"], v["head_mask"]
    wq, wk, wv, wo, bq, bk = (v[n] for n in ("wq", "wk", "wv", "wo", "bq", "bk"))
    rstd_t, nbias_t, rstd_p, nbias_p = (v[n] for n in ("rstd_t", "nbias_t", "rstd_p", "nbias_p"))
    with ExitStack() as local:
        def lsb(name, shape, dt=F32):
            return sb(name, shape, dt, local)

        def sem(name):
            return local.enter_context(nc.semaphore(name))

        xh_t = lsb("xh_t", [P, 2, D])
        xh_p = lsb("xh_p", [NP_, 2, D])
        x_T = lsb("x_T", [P, 2, L])
        q_T = lsb("q_T", [P, 2, L])
        k_T = lsb("k_T", [P, 2, L])
        q_exp = lsb("q_exp", [P, 2, H, L])
        q_flat = q_exp[:, :, :, :].rearrange("p u h l -> p (u h l)")
        v_t = lsb("v_t", [P, 2, H, D])
        v_p = lsb("v_p", [NP_, 2, H, D])
        scores = lsb("scores", [P, 4, GT, L])
        work = lsb("work", [P, 4, GT, L])
        e_all = lsb("e_all", [P, 4, GT, L])
        sum_all = lsb("sum_all", [P, 4, GT])
        sum_rest = lsb("sum_rest", [P, 4, GT])
        inv = lsb("inv", [P, 4, GT])
        minus_one = lsb("minus_one", [P, GT])
        top = lsb("top", [P, 4, GT, 8])
        topw = lsb("topw", [P, GT, 8])
        neg_max = lsb("neg_max", [P, 4, GT])
        pT_t = lsb("pT_t", [P, TILES * P])
        pT_p = lsb("pT_p", [NP_, TILES * P])
        oT_t = lsb("oT_t", [P, 2, NT])
        oT_p = lsb("oT_p", [P, 2 * NP_])
        b_scores = [bank(f"b_scores{i}", [P, 512], local) for i in range(3)]
        b_ptt = bank("b_ptt", [P, GT, P], local)
        b_ptp = bank("b_ptp", [P, GT, P], local)
        b_x = bank("b_x", [P, 512], local)
        b_q = bank("b_q", [P, 512], local)
        b_v = bank("b_v", [P, 4, D], local)

        zeroed = sem("zeroed")
        zeros_ready = sem("zeros_ready")
        r_in = sem("r_in")
        marker = sem("marker")
        xh_ready = sem("xh_ready")
        xT_done = sem("xT_done")
        xT_ready = sem("xT_ready")
        qkv_done = sem("qkv_done")
        q_ready = sem("q_ready")
        k_ready = sem("k_ready")
        v_ready = sem("v_ready")
        qe_ready = sem("qe_ready")
        s_done = sem("s_done")
        s_ready = sem("s_ready")
        m_ready = sem("m_ready")
        nm_ready = sem("nm_ready")
        w_ready = sem("w_ready")
        ea_ready = sem("ea_ready")
        er_ready = sem("er_ready")
        sum_ready = sem("sum_ready2")
        inv_ready = sem("inv_ready")
        diff_ready = sem("diff_ready")
        p_ready = sem("p_ready")
        pt_done = sem("pt_done")
        pt_ready = sem("pt_ready")
        o_done = sem("o_done")
        o_ready = sem("o_ready")
        y_done = sem("y_done")
        y_ready = sem("y_ready")
        chain = sem("chain")


        def loop(eng, body):
            body(0, True, False)
            with eng.Fori(1, PAIRS - 1) as i:
                body(i, False, False)
            body(PAIRS - 1, False, True)

        with nc.Block() as block:
            @block.sync
            def _(sp):
                for lo in range(0, NE + NS, 11):
                    sp.dma_start(v["w_gu"][:, lo:lo + 11, :], a["w_gu"][:, lo:lo + 11, :]).then_inc(v["weights_in"], 16)
                    sp.dma_start(v["w_d"][:, lo:lo + 11, :], a["w_d"][:, lo:lo + 11, :]).then_inc(v["weights_in"], 16)
                for t, n in ((v["wr"], "wr"), (v["tri"], "tri"), (v["region"], "region")):
                    sp.dma_start(t[:, :], a[n]).then_inc(r_in, 16)
                sp.wait_ge(zeros_ready, 1)
                sp.dma_start(v["dispatch"].rearrange("(e r) c -> r e c", e=NE)[0:P, :, :],
                             v["zeros"][:, :].rearrange("p (a c) -> p a c", a=1).broadcast_to([P, NE, REC])).then_inc(r_in, 16)
                sp.wait_ge(r_in, 64)

            @block.tensor
            def _(pe):
                def transposes(n):
                    pe.wait_ge(xh_ready, 4 * (n + 1))
                    pe.sem_inc(marker, 1)
                    for u in range(2):
                        pe.transpose(b_x[:, u * L:u * L + NP_], xh_p[:, u, :], ident[0:NP_, 0:NP_])
                        last = pe.transpose(b_x[:, u * L + NP_:u * L + L], xh_t[:, u, :], ident[:, :])
                    last.then_inc(xT_done, 1)

                def projections(n):
                    pe.wait_ge(xT_ready, n + 1)
                    pe.matmul(b_q[:, 0:2 * L], wq[:, :], x_T[:, :, :].rearrange("p u l -> p (u l)"), start=True, stop=True)
                    pe.matmul(b_x[:, 0:2 * L], wk[:, :], x_T[:, :, :].rearrange("p u l -> p (u l)"), start=True, stop=True)
                    for u in range(2):
                        for t, (lo, n_) in enumerate(((NP_, NT), (0, NP_))):
                            o = b_v[0:n_, 2 * t + u, :]
                            pe.matmul(o, x_T[:, u, lo:lo + n_], wv[:, :], start=True, stop=False)
                            last = pe.matmul(o, ones[0:1, 0:n_], rows[0:1, 0:D], start=False, stop=True)
                    last.then_inc(qkv_done, 1)

                def score_group(i, g, G):
                    if g == 0:
                        pe.wait_ge(k_ready, 2 * i + 1)
                        pe.sem_inc(marker, 1)
                        pe.wait_ge(qe_ready, 2 * i + 1)
                        pe.sem_inc(marker, 1)
                    if g == 3:
                        pe.wait_ge(k_ready, 2 * i + 2)
                        pe.sem_inc(marker, 1)
                        pe.wait_ge(qe_ready, 2 * i + 2)
                        pe.sem_inc(marker, 1)
                    back = {0: 3, 1: 3, GROUPS - 1: GROUPS}.get(g, 2)
                    if not (isinstance(G, int) and (G < 2 or G == GROUPS - 1)):
                        pe.wait_ge(ea_ready, 3 * (G - back + 1))
                        pe.sem_inc(marker, 1)
                        pe.wait_ge(s_ready, G - back + 1)
                        pe.sem_inc(marker, 1)
                    bk_ = b_scores[s_bank(g)]
                    for t in range(GT):
                        k = GT * g + t
                        o = bk_[:, t * L:(t + 1) * L]
                        if k < MID:
                            last = pe.matmul(o, q_flat[:, k * P:(k + 1) * P], k_T[:, 0, :], start=True, stop=True)
                        elif k == MID:
                            pe.matmul(o, q_flat[:, ROWS - (P - TAIL):ROWS + TAIL], k_T[:, 1, :], start=True, stop=True)
                            last = pe.matmul(bk_[0:TAIL, t * L:(t + 1) * L], q_flat[:, ROWS - TAIL:ROWS], k_T[:, 0, :],
                                             start=True, stop=True)
                        else:
                            r = ROWS + TAIL + (k - MID - 1) * P
                            last = pe.matmul(o, q_flat[:, r:r + P], k_T[:, 1, :], start=True, stop=True)
                    last.then_inc(s_done, 1)

                def prob_transposes(g, G):
                    pe.wait_ge(p_ready, G + 1)
                    if not isinstance(G, int) or G >= 1:
                        pe.sem_inc(marker, 1)
                        pe.wait_ge(pt_ready, 2 * G)
                    for t in range(GT):
                        pr = e_all[:, slot(g), t, :]
                        pe.transpose(b_ptt[:, t, :], pr[:, NP_:L], ident[:, :])
                        last = pe.transpose(b_ptp[0:NP_, t, :], pr[:, 0:NP_], ident[:, :])
                    last.then_inc(pt_done, 1)

                def attend(i, u, dst):
                    pe.wait_ge(pt_ready, 2 * (GROUPS * i + (4 if u == 0 else 7)))
                    pe.sem_inc(marker, 1)
                    if u == 0:
                        pe.wait_ge(v_ready, 2 * (i + 1))
                        pe.sem_inc(marker, 1)
                    base = 0 if u == 0 else TILES * P - ROWS
                    for h in range(H):
                        c = base + h * L
                        pe.matmul(dst, v_t[:, u, h, :], pT_t[:, c:c + L], start=(h == 0), stop=False)
                        last = pe.matmul(dst, v_p[:, u, h, :], pT_p[:, c:c + L], start=False, stop=(h == H - 1))
                    last.then_inc(o_done, 1)

                def out_projection(i):
                    pe.wait_ge(o_ready, 4 * (i + 1))
                    pe.sem_inc(marker, 1)
                    for u in range(2):
                        o = b_x[:, u * D:(u + 1) * D]
                        pe.matmul(o, oT_t[:, u, :], wo[:, :], start=True, stop=False)
                        pe.matmul(o, ident[:, :], h_text[:, 2 * i + u, :], start=False, stop=False)
                        pe.matmul(o, ones[0:1, :], rows[0:1, D:2 * D], start=False, stop=True)
                    o = b_x[0:2 * NP_, 2 * D:3 * D]
                    pe.matmul(o, oT_p[:, :], wo[:, :], start=True, stop=False)
                    for u in range(2):
                        sel = ident[0:NP_, 0:2 * NP_] if u == 0 else shift36[:, :]
                        pe.matmul(o, sel, h_patch[:, 2 * i + u, :], start=False, stop=False)
                    pe.matmul(o, ones[0:1, 0:2 * NP_], rows[0:1, D:2 * D], start=False, stop=True).then_inc(y_done, 1)

                def body(i, first, last):
                    for g in range(GROUPS):
                        G = GROUPS * i + g
                        if not (first and g < 2):
                            prob_transposes((g - 2) % GROUPS, G - 2)
                        if g + 2 < GROUPS:
                            score_group(i, g + 2, G + 2)
                        elif not last:
                            score_group(i + 1, g + 2 - GROUPS, G + 2)
                        if g == 1 and not last:
                            if not first:
                                pe.wait_ge(o_ready, 4 * i - 2)
                                pe.sem_inc(marker, 1)
                            transposes(i + 1)
                        if g == 2 and not first:
                            attend(i - 1, 1, b_q[:, 0:L])
                            out_projection(i - 1)
                        if g == 3 and not last:
                            if not first:
                                pe.wait_ge(o_ready, 4 * i)
                                pe.sem_inc(marker, 1)
                            pe.wait_ge(v_ready, 2 * (i + 1))
                            pe.sem_inc(marker, 1)
                            if not first:
                                pe.wait_ge(y_ready, 3 * i)
                                pe.sem_inc(marker, 1)
                            projections(i + 1)
                        if g == 6:
                            if not last:
                                pe.wait_ge(k_ready, 2 * (i + 2))
                                pe.sem_inc(marker, 1)
                            attend(i, 0, b_x[:, 0:L])

                pe.wait_ge(zeroed, 2)
                transposes(0)
                projections(0)
                for g in range(2):
                    score_group(0, g, g)
                loop(pe, body)
                for g in range(2):
                    prob_transposes(GROUPS - 2 + g, GROUPS * PAIRS - 2 + g)
                attend(PAIRS - 1, 1, b_q[:, 0:L])
                out_projection(PAIRS - 1)

            @block.scalar
            def _(act):
                def normalize(n, first):
                    if not first:
                        act.wait_ge(xT_done, n)
                    for u in range(2):
                        b = 2 * n + u
                        act.activation(xh_t[:, u, :], h_text[:, b, :], ACT.Identity, bias=nbias_t[:, b:b + 1] if isinstance(b, int) else nbias_t[:, bass.ds(b, 1)],
                                       scale=rstd_t[:, b:b + 1] if isinstance(b, int) else rstd_t[:, bass.ds(b, 1)]).then_inc(xh_ready, 1)
                        act.activation(xh_p[:, u, :], h_patch[:, b, :], ACT.Identity, bias=nbias_p[:, b:b + 1] if isinstance(b, int) else nbias_p[:, bass.ds(b, 1)],
                                       scale=rstd_p[:, b:b + 1] if isinstance(b, int) else rstd_p[:, bass.ds(b, 1)]).then_inc(xh_ready, 1)

                def take_xT(n):
                    act.wait_ge(xT_done, n + 1)
                    if not isinstance(n, int) or n > 0:
                        act.wait_ge(qkv_done, n)
                    act.activation(x_T[:, :, :], b_x[:, 0:2 * L].rearrange("p (u l) -> p u l", u=2), ACT.Copy).then_inc(xT_ready, 1)

                def take_q(n):
                    act.wait_ge(qkv_done, n + 1)
                    if not isinstance(n, int) or n > 0:
                        act.wait_ge(qe_ready, 2 * n)
                    act.activation(q_T[:, :, :], b_q[:, 0:2 * L].rearrange("p (u l) -> p u l", u=2), ACT.Identity,
                                   bias=bq[:, 0:1]).then_inc(q_ready, 1)

                def take_k(n, u, G):
                    act.wait_ge(s_done, G)
                    act.activation(k_T[:, u, :], b_x[:, u * L:(u + 1) * L], ACT.Identity, bias=bk[:, 0:1]).then_inc(k_ready, 1)

                def take_v(n):
                    act.wait_ge(qkv_done, n + 1)
                    if not isinstance(n, int) or n > 0:
                        act.wait_ge(o_done, 2 * n)
                    for t, (dst, rows_) in enumerate(((v_t, P), (v_p, NP_))):
                        flat = dst[:, :, :, :].rearrange("p u h d -> p u (h d)")
                        for u in range(2):
                            diag = bass.AP(tensor=flat.tensor, offset=flat[:, u, :].offset,
                                           ap=[flat.ap[0], [D + E, H], [1, E]])
                            ins = act.activation(diag, b_v[0:rows_, 2 * t + u, :].rearrange("p (h e) -> p h e", h=H), ACT.Copy)
                        ins.then_inc(v_ready, 1)

                def take_o(i, u, src):
                    act.wait_ge(o_done, 2 * i + u + 1)
                    if u == 0 and not (isinstance(i, int) and i == 0):
                        act.wait_ge(y_done, i)
                    act.activation(oT_t[:, u, :], src[:, NP_:L], ACT.Copy).then_inc(o_ready, 1)
                    act.activation(oT_p[:, u * NP_:(u + 1) * NP_], src[:, 0:NP_], ACT.Copy).then_inc(o_ready, 1)

                def take_y(i):
                    act.wait_ge(y_done, i + 1)
                    for u in range(2):
                        act.activation(h_text[:, 2 * i + u, :], b_x[:, u * D:(u + 1) * D], ACT.Copy).then_inc(y_ready, 1)
                    act.activation(h2_patch[:, i, :], b_x[0:2 * NP_, 2 * D:3 * D], ACT.Copy).then_inc(y_ready, 1)

                def copy_scores(i, g, G):
                    act.wait_ge(s_done, G + 1)
                    if not (isinstance(G, int) and G < 3):
                        act.wait_ge(w_ready, 3 * (G - 2))
                    act.activation(scores[:, slot(g), :, :], b_scores[s_bank(g)][:, 0:GT * L].rearrange("p (t l) -> p t l", t=GT),
                                   ACT.Copy).then_inc(s_ready, 1)

                def exp_all(g, G):
                    act.wait_ge(nm_ready, G + 1)
                    if not (isinstance(G, int) and G < 3):
                        act.wait_ge(pt_done, G - 2)
                    for t in range(GT):
                        act.activation(e_all[:, slot(g), t, :], b_scores[s_bank(g)][:, t * L:(t + 1) * L], ACT.Exp,
                                       bias=neg_max[:, slot(g), t:t + 1],
                                       accum_out=sum_all[:, slot(g), t:t + 1]).then_inc(ea_ready, 1)

                def exp_rest(g, G):
                    for t in range(GT):
                        act.wait_ge(w_ready, 3 * G + t + 1)
                        act.activation(work[:, slot(g), t, :], work[:, slot(g), t, :], ACT.Exp,
                                       bias=neg_max[:, slot(g), t:t + 1],
                                       accum_out=sum_rest[:, slot(g), t:t + 1]).then_inc(er_ready, 1)

                def take_pt(g, G):
                    act.wait_ge(pt_done, G + 1)
                    if g == 0 and not (isinstance(G, int) and G == 0):
                        act.wait_ge(o_done, 2 * (G // GROUPS) if isinstance(G, int) else 2 * G_pair[0])
                    lo = GT * g * P
                    act.activation(pT_t[:, lo:lo + GT * P], b_ptt[:, :, :].rearrange("p t r -> p (t r)"), ACT.Copy).then_inc(pt_ready, 1)
                    act.activation(pT_p[:, lo:lo + GT * P], b_ptp[0:NP_, :, :].rearrange("p t r -> p (t r)"), ACT.Copy).then_inc(pt_ready, 1)

                G_pair = [0]

                def body(i, first, last):
                    G_pair[0] = i
                    for g in range(GROUPS):
                        G = GROUPS * i + g
                        if not (first and g == 0):
                            exp_rest((g - 1) % GROUPS, G - 1)
                        exp_all(g, G)
                        if not (first and g < 2):
                            take_pt((g - 2) % GROUPS, G - 2)
                        if g + 2 < GROUPS:
                            copy_scores(i, g + 2, G + 2)
                        elif not last:
                            copy_scores(i + 1, g + 2 - GROUPS, G + 2)
                        if g == 0:
                            if not first:
                                take_o(i - 1, 0, b_x[:, 0:L])
                            if not last:
                                normalize(i + 1, False)
                        if g == 1 and not last:
                            take_xT(i + 1)
                        if g == 2 and not first:
                            take_o(i - 1, 1, b_q[:, 0:L])
                        if g == 3:
                            if not first:
                                take_v(i)
                                take_y(i - 1)
                        if g == 4 and not last:
                            take_q(i + 1)
                            take_k(i + 1, 0, GROUPS * i + 4)
                        if g == 5 and not last:
                            take_k(i + 1, 1, GROUPS * i + 7)

                normalize(0, True)
                take_xT(0)
                take_q(0)
                for u in range(2):
                    act.activation(k_T[:, u, :], b_x[:, u * L:(u + 1) * L], ACT.Identity, bias=bk[:, 0:1]).then_inc(k_ready, 1)
                take_v(0)
                for g in range(2):
                    copy_scores(0, g, g)
                loop(act, body)
                exp_rest(GROUPS - 1, GROUPS * PAIRS - 1)
                take_pt(GROUPS - 2, GROUPS * PAIRS - 2)
                take_pt(GROUPS - 1, GROUPS * PAIRS - 1)
                take_o(PAIRS - 1, 0, b_x[:, 0:L])
                take_o(PAIRS - 1, 1, b_q[:, 0:L])
                take_y(PAIRS - 1)

            @block.gpsimd
            def _(po):
                po.memset(v_t[:, :, :, :], 0.0).then_inc(zeroed, 1)
                po.memset(v_p[:, :, :, :], 0.0).then_inc(zeroed, 1)
                po.memset(minus_one[:, :], -1.0).then_inc(zeroed, 1)
                po.memset(v["zeros"][:, :], 0.0).then_inc(zeros_ready, 1)
                po.memset(v["ones_sq"][:, :], 1.0).then_inc(zeroed, 1)
                po.wait_ge(zeroed, 4)

                def spread(n, u):
                    if u == 0:
                        po.wait_ge(q_ready, n + 1)
                        if not isinstance(n, int) or n > 0:
                            po.sem_inc(marker, 1)
                    if not isinstance(n, int) or n > 0:
                        po.wait_ge(s_done, GROUPS * n - (3 if u == 0 else 0))
                    po.tensor_tensor(q_exp[:, u, :, :],
                                     q_T[:, u, :].rearrange("p (a l) -> p a l", a=1).broadcast_to([P, H, L]),
                                     head_mask[:, :].rearrange("p (h a) -> p h a", a=1).broadcast_to([P, H, L]),
                                     ALU.mult).then_inc(qe_ready, 1)

                def negate(g, G):
                    po.wait_ge(m_ready, G + 1)
                    po.sem_inc(marker, 1)
                    if not (isinstance(G, int) and G < 3):
                        po.wait_ge(er_ready, 3 * (G - 2))
                        po.sem_inc(marker, 1)
                    po.tensor_scalar(neg_max[:, slot(g), :], top[:, slot(g), :, 0], -1.0, None, ALU.mult).then_inc(nm_ready, 1)

                def probabilities(g, G):
                    po.wait_ge(er_ready, 3 * (G + 1))
                    po.tensor_tensor(inv[:, slot(g), :], sum_all[:, slot(g), :], sum_rest[:, slot(g), :], ALU.subtract).then_inc(sum_ready, 1)
                    po.tensor_tensor(e_all[:, slot(g), :, :], e_all[:, slot(g), :, :], work[:, slot(g), :, :],
                                     ALU.subtract).then_inc(diff_ready, 1)
                    po.wait_ge(sum_ready, G + 1)
                    po.tensor_tensor(inv[:, slot(g), :], inv[:, slot(g), :], minus_one[:, :], ALU.pow).then_inc(inv_ready, 1)
                    po.wait_ge(inv_ready, G + 1)
                    po.sem_inc(marker, 1)
                    po.wait_ge(diff_ready, G + 1)
                    po.tensor_tensor(e_all[:, slot(g), :, :], e_all[:, slot(g), :, :],
                                     inv[:, slot(g), :].rearrange("p (t a) -> p t a", a=1).broadcast_to([P, GT, L]),
                                     ALU.mult).then_inc(p_ready, 1)

                def body(i, first, last):
                    for g in range(GROUPS):
                        G = GROUPS * i + g
                        negate(g, G)
                        if g == 5 and not last:
                            spread(i + 1, 0)
                        if g == 6 and not last:
                            spread(i + 1, 1)
                        if not (first and g == 0):
                            probabilities((g - 1) % GROUPS, G - 1)

                spread(0, 0)
                spread(0, 1)
                loop(po, body)
                probabilities(GROUPS - 1, GROUPS * PAIRS - 1)

            @block.vector
            def _(ve):
                class Link:
                    def __init__(self):
                        self.n = 0

                    def __call__(self, ins):
                        self.n += 1
                        ins.then_inc(chain, 1)
                        return self.n

                    def settle(self):
                        ve.wait_ge(chain, self.n)

                def body(i, first, last):
                    link = Link()
                    ve.sem_clear(chain)
                    for g in range(GROUPS):
                        G = GROUPS * i + g
                        s = slot(g)
                        ve.wait_ge(s_ready, G + 1)
                        ve.sem_inc(marker, 1)
                        if not (isinstance(G, int) and G < 3):
                            ve.wait_ge(nm_ready, G - 2)
                            ve.sem_inc(marker, 1)
                            ve.wait_ge(diff_ready, G - 2)
                            ve.sem_inc(marker, 1)
                        seen = [link(ve.max(top[:, s, t, :], scores[:, s, t, :])) for t in range(GT)]
                        for t in range(GT):
                            ve.wait_ge(chain, seen[t])
                            if t == GT - 1:
                                ve.sem_inc(m_ready, 1)
                            seen[t] = link(ve.match_replace(work[:, s, t, :], top[:, s, t, :], scores[:, s, t, :], MARK))
                        for rnd in range(2):
                            for t in range(GT):
                                ve.wait_ge(chain, seen[t])
                                seen[t] = link(ve.max(topw[:, t, :], work[:, s, t, :]))
                            for t in range(GT):
                                ve.wait_ge(chain, seen[t])
                                seen[t] = link(ve.match_replace(work[:, s, t, :], topw[:, t, :], work[:, s, t, :], MARK))
                        for t in range(GT):
                            ve.wait_ge(chain, seen[t])
                            seen[t] = link(ve.max(topw[:, t, :], work[:, s, t, :]))
                        ve.wait_ge(chain, seen[GT - 1])
                        n = link(ve.memset(topw[:, :, 1:8], MARK))
                        for t in range(GT):
                            ve.wait_ge(chain, n)
                            ve.match_replace(work[:, s, t, :], topw[:, t, :], work[:, s, t, :], MARK).then_inc(w_ready, 1)
                    link.settle()
                    ve.wait_ge(w_ready, 3 * (GROUPS * (i + 1)))
                    ve.sem_inc(marker, 1)

                loop(ve, body)


def route(nc, es, sb, bank, a, v):
    ident, h_text, h2_patch, ones = v["ident"], v["h_text"], v["h2_patch"], v["ones"]
    base, xT_all, places, carry, dispatch = v["base"], v["xT_all"], v["places"], v["carry"], v["dispatch"]
    wr, tri, ones_sq, region = v["wr"], v["tri"], v["ones_sq"], v["region"]
    with ExitStack() as local:
        def lsb(name, shape, dt=F32):
            return sb(name, shape, dt, local)

        def sem(name):
            return local.enter_context(nc.semaphore(name))

        minus_half = lsb("minus_half", [P, 3])
        stats = lsb("stats", [P, 3, 6])
        mv = lsb("mv", [P, 3, 2])
        rstd = lsb("rstd", [P, 2, 3])
        nbias = lsb("nbias", [P, 2, 3])
        rec = lsb("rec", [P, 2, 3, REC])
        xT = lsb("xT", [P, PT])
        logits = lsb("logits", [P, 3, NE + 2])
        taken = lsb("taken", [P, 3, NE + 2])
        mask = lsb("mask", [P, 3, NE])
        chosen = lsb("chosen", [P, NE])
        best = lsb("best", [P, 3, 8])
        neg_max = lsb("neg_max2", [P, 3])
        ex = lsb("ex", [P, 3, NE])
        inv = lsb("inv2", [P, 3])
        rows_f = lsb("rows_f", [P, 3, 8])
        rows_i = lsb("rows_i", [P, 2, 3, 8], I32)
        b_xT = bank("b_xT", [P, 512], local)
        b_lg = bank("b_lg", [P, 3, NE], local)
        b_rank = bank("b_rank", [P, 3, NE], local)
        ready0 = sem("ready0")
        marker = sem("marker2")
        dve = sem("dve2")
        mv_ready = sem("mv_ready")
        rstd_ready = sem("rstd_ready")
        nb_ready = sem("nb_ready")
        xn_ready = sem("xn_ready")
        base_ready = sem("base_ready")
        xT_done = sem("xT_done2")
        xT_ready = sem("xT_ready2")
        lg_done = sem("lg_done")
        lg_ready = sem("lg_ready")
        nm_ready = sem("nm_ready2")
        ex_ready = sem("ex_ready")
        mask_ready = sem("mask_ready")
        rank_done = sem("rank_done")
        gate_ready = sem("gate_ready")
        idx_ready = sem("idx_ready")
        carried = sem("carried")
        sent = [sem(f"sent{p}") for p in range(2)]
        PARTS = ((0, P), (1, P), (2, T2))

        def source(i, t):
            return h_text[:, 2 * i + t, :] if t < 2 else h2_patch[:, i, :]
        def loop(eng, body):
            body(0, 0, False)
            with eng.Fori(0, PAIRS // 2 - 1) as i:
                body(2 * i + 1, 1, False, i)
                body(2 * i + 2, 0, False, i)
            body(PAIRS - 1, 1, True, PAIRS // 2 - 1)

        with nc.Block() as block:
            @block.gpsimd
            def _(po):
                po.memset(minus_half[:, :], -0.5).then_inc(ready0, 1)
                po.memset(mv[:, :, :], 1.0).then_inc(ready0, 1)
                po.memset(rec[:, :, :, :], 0.0).then_inc(ready0, 1)
                po.memset(carry[:, :], 0.0).then_inc(ready0, 1)
                po.memset(logits[:, :, :], SENT).then_inc(ready0, 1)
                po.memset(mask[:, :, :], 0.0).then_inc(ready0, 1)
                po.memset(ex[:, :, :], 1.0).then_inc(ready0, 1)

                def deviation(n, p):
                    po.wait_ge(mv_ready, n + 1)
                    po.sem_inc(marker, 1)
                    po.tensor_scalar(rstd[:, p, :], mv[:, :, 1], EPS, None, ALU.add).then_inc(rstd_ready, 1)
                    po.wait_ge(rstd_ready, 2 * n + 1)
                    po.tensor_tensor(rstd[:, p, :], rstd[:, p, :], minus_half[:, :], ALU.pow).then_inc(rstd_ready, 1)

                def body(n, p, last, i=0):
                    if not last:
                        deviation(n + 1, 1 - p)
                    po.wait_ge(xn_ready, 3 * (n + 1))
                    po.sem_inc(marker, 1)
                    for t, m in PARTS:
                        po.tensor_tensor(base[0:m, 3 * n + t, :], source(n, t), rec[0:m, p, t, 0:D], ALU.add).then_inc(base_ready, 1)
                    po.wait_ge(gate_ready, n + 1)
                    po.sem_inc(marker, 1)
                    po.wait_ge(idx_ready, n + 1)
                    po.sem_inc(marker, 1)
                    for t, m in PARTS:
                        for k in range(KE):
                            po.indirect_dma_start(dispatch, bass.IndirectOffsetOnAxis(rows_i[0:m, p, t, k:k + 1], 0),
                                                  rec[0:m, p, t, :], None).then_inc(sent[p], 16)

                po.wait_ge(ready0, 8)
                deviation(0, 0)
                loop(po, body)
                for p in range(2):
                    po.wait_ge(sent[p], 16 * 3 * KE * (PAIRS // 2))

            @block.scalar
            def _(act):
                act.wait_ge(ready0, 8)

                def normalize(n, p, i=None):
                    act.wait_ge(nb_ready, n + 1)
                    act.sem_inc(marker, 1)
                    if i is not None:
                        act.wait_ge(sent[p], (i + 1) * (16 * 3 * KE))
                        act.sem_inc(marker, 1)
                    for t, m in PARTS:
                        act.activation(rec[0:m, p, t, 0:D], source(n, t), ACT.Identity, bias=nbias[0:m, p, t:t + 1],
                                       scale=rstd[0:m, p, t:t + 1]).then_inc(xn_ready, 1)

                def body(n, p, last, i=None):
                    act.wait_ge(xT_done, n + 1)
                    act.activation(xT[:, :], b_xT[:, 0:PT], ACT.Copy).then_inc(xT_ready, 1)
                    act.activation(xT_all[:, n * PT:(n + 1) * PT] if isinstance(n, int) else xT_all[:, bass.ds(n * PT, PT)],
                                   b_xT[:, 0:PT], ACT.Copy).then_inc(xT_ready, 1)
                    act.wait_ge(lg_done, n + 1)
                    act.activation(logits[:, 0:2, 0:NE], b_lg[:, 0:2, :], ACT.Copy).then_inc(lg_ready, 1)
                    act.activation(logits[0:T2, 2, 0:NE], b_lg[0:T2, 2, :], ACT.Copy).then_inc(lg_ready, 1)
                    act.wait_ge(nm_ready, n + 1)
                    for t, m in PARTS:
                        act.activation(ex[0:m, t, :], logits[0:m, t, 0:NE], ACT.Exp, bias=neg_max[0:m, t:t + 1]).then_inc(ex_ready, 1)
                    if not last:
                        normalize(n + 1, 1 - p, i)

                normalize(0, 0)
                loop(act, body)

            @block.tensor
            def _(pe):
                def transposes(n, p):
                    pe.wait_ge(xn_ready, 3 * (n + 1))
                    pe.sem_inc(marker, 1)
                    at = 0
                    for t, m in PARTS:
                        last = pe.transpose(b_xT[:, at:at + m], rec[0:m, p, t, 0:D], ident[0:m, 0:m])
                        at += m
                    last.then_inc(xT_done, 1)

                def body(n, p, last, i=0):
                    pe.wait_ge(xT_ready, 2 * (n + 1))
                    pe.sem_inc(marker, 1)
                    at = 0
                    for t, m in PARTS:
                        done = pe.matmul(b_lg[0:m, t, :], xT[:, at:at + m], wr[:, :], start=True, stop=True)
                        at += m
                    done.then_inc(lg_done, 1)
                    pe.wait_ge(mask_ready, 2 * (n + 1))
                    pe.sem_inc(marker, 1)
                    for t, m in PARTS:
                        o = b_rank[:, t, :]
                        pe.matmul(o, ones[0:1, :], region[:, :], start=True, stop=False)
                        pe.matmul(o, ones_sq[:, :], carry[:, :], start=False, stop=False)
                        for before in range(t):
                            pe.matmul(o, ones_sq[:, :], mask[:, before, :], start=False, stop=False)
                        done = pe.matmul(o, tri[:, :], mask[:, t, :], start=False, stop=True)
                    done.then_inc(rank_done, 1)
                    if not last:
                        transposes(n + 1, 1 - p)

                transposes(0, 0)
                loop(pe, body)

            @block.vector
            def _(ve):
                ve.memset(base[64:P, :, :].rearrange("p (i t) d -> p i t d", t=3)[:, :, 2, :], 0.0).then_inc(ready0, 1)
                ve.wait_ge(ready0, 8)
                n_ = [0]

                def then(ins):
                    ins.then_inc(dve, 1)
                    n_[0] += 1

                def settle():
                    ve.wait_ge(dve, n_[0])

                def statistics(n):
                    for t, m in PARTS:
                        then(ve.bn_stats(stats[0:m, t, :], source(n, t)))
                    settle()
                    for t, m in PARTS:
                        then(ve.bn_aggr(mv[0:m, t, :], stats[0:m, t, :]))
                    settle()
                    ve.sem_inc(mv_ready, 1)

                def shift(n, p):
                    ve.wait_ge(rstd_ready, 2 * (n + 1))
                    ve.scalar_tensor_tensor(out=nbias[:, p, :], in0=mv[:, :, 0], scalar=-1.0, in1=rstd[:, p, :],
                                            op0=ALU.mult, op1=ALU.mult).then_inc(nb_ready, 1)

                def body(n, p, last, i=0):
                    n_[0] = 0
                    ve.sem_clear(dve)
                    if not last:
                        statistics(n + 1)
                    ve.wait_ge(lg_ready, 2 * (n + 1))
                    ve.sem_inc(marker, 1)
                    for t, m in PARTS:
                        then(ve.max(best[0:m, t, :], logits[0:m, t, 0:NE]))
                    settle()
                    for t, m in PARTS:
                        then(ve.tensor_scalar(neg_max[0:m, t:t + 1], best[0:m, t, 0:1], -1.0, None, ALU.mult))
                    settle()
                    ve.sem_inc(nm_ready, 1)
                    then(ve.memset(best[:, :, KE:8], SENT))
                    settle()
                    for t, m in PARTS:
                        then(ve.match_replace(taken[0:m, t, :], best[0:m, t, :], logits[0:m, t, :], MARK))
                    settle()
                    for lo, hi, m in ((0, 2, P), (2, 3, T2)):
                        then(ve.tensor_scalar(mask[0:m, lo:hi, :], taken[0:m, lo:hi, 0:NE], MARK, None, ALU.is_equal))
                    settle()
                    ve.sem_inc(mask_ready, 2)
                    ve.wait_ge(ex_ready, 3 * (n + 1))
                    then(ve.tensor_tensor(ex[:, :, :], ex[:, :, :], mask[:, :, :], ALU.mult))
                    settle()
                    then(ve.tensor_reduce(inv[:, :], ex[:, :, :], AX.X, ALU.add))
                    settle()
                    then(ve.reciprocal(inv[0:P, 0:2], inv[0:P, 0:2]))
                    then(ve.reciprocal(inv[0:T2, 2:3], inv[0:T2, 2:3]))
                    settle()
                    ve.tensor_tensor(rec[:, p, :, D:REC], ex[:, :, :],
                                     inv[:, :].rearrange("p (t a) -> p t a", a=1).broadcast_to([P, 3, NE]),
                                     ALU.mult).then_inc(gate_ready, 1)
                    ve.wait_ge(rank_done, n + 1)
                    then(ve.tensor_tensor(places[:, 3 * n:3 * n + 3, :] if isinstance(n, int) else places[:, bass.ds(3 * n, 3), :],
                                          b_rank[:, :, :], mask[:, :, :], ALU.mult))
                    then(ve.tensor_reduce(chosen[:, :], mask[:, :, :].rearrange("p t e -> p e t"), AX.X, ALU.add))
                    settle()
                    then(ve.tensor_tensor(carry[:, :], carry[:, :], chosen[:, :], ALU.add))
                    for t, m in PARTS:
                        then(ve.tensor_tensor(ex[0:m, t, :], b_rank[0:m, t, :], mask[0:m, t, :], ALU.mult))
                    settle()
                    for t, m in PARTS:
                        then(ve.max(rows_f[0:m, t, :], ex[0:m, t, :]))
                    settle()
                    for lo, hi, m in ((0, 2, P), (2, 3, T2)):
                        then(ve.tensor_scalar(rows_i[0:m, p, lo:hi, :], rows_f[0:m, lo:hi, :], -1.0, None, ALU.add))
                    settle()
                    ve.sem_inc(idx_ready, 1)
                    if not last:
                        shift(n + 1, 1 - p)

                statistics(0)
                shift(0, 0)
                loop(ve, body)


def plan(nc, es, sb, bank, a, v):
    carry, places, where, table = v["carry"], v["places"], v["where"], v["table"]
    ident, ones = v["ident"], v["ones"]
    with ExitStack() as local:
        def lsb(name, shape, dt=F32):
            return sb(name, shape, dt, local)

        def sem(name):
            return local.enter_context(nc.semaphore(name))

        ones_sq = lsb("ones_sq3", [P, P])
        regions = lsb("regions", [P, NE])
        names = lsb("names", [P, NE])
        steps = lsb("steps", [P, 21])
        tile_no = lsb("tile_no", [P, 2])
        counts = lsb("counts", [P, NE])
        over = lsb("over", [P, NE, 21])
        n_tiles = lsb("n_tiles", [P, NE])
        ends = lsb("ends", [P, NE])
        starts = lsb("starts", [P, NE])
        one = lsb("one_row", [P, NE])
        past = lsb("past", [P, 2, NE])
        mine = lsb("mine", [P, 2, NE])
        expert = lsb("expert", [P, 2])
        begin = lsb("begin", [P, 2])
        rows_of = lsb("rows_of", [P, 2])
        row = lsb("row", [P, 2])
        first_last = lsb("first_last", [P, NE])
        d_all = lsb("d_all", [P, NE])
        d_last = lsb("d_last", [P, NE])
        shifted = lsb("shifted", [P, 3 * PAIRS, NE])
        best = lsb("best3", [P, 3 * PAIRS, 8])
        b_cnt = bank("b_cnt", [P, 512], local)
        b_tab = bank("b_tab", [P, 4, P], local)
        c_in, set0, dve, cnt_done, cols_ready, tab_done = (sem(n) for n in ("c_in3", "set0", "dve3", "cnt_done", "cols_ready", "tab_done"))
        with nc.Block() as block:
            @block.sync
            def _(sp):
                for t, n in ((regions, "region_all"), (names, "names"), (steps, "steps"), (tile_no, "tile_no")):
                    sp.dma_start(t[:, :], a[n]).then_inc(c_in, 16)

            @block.gpsimd
            def _(po):
                po.memset(ones_sq[:, :], 1.0).then_inc(set0, 1)
                po.memset(one[:, :], 1.0).then_inc(set0, 1)

            @block.tensor
            def _(pe):
                pe.wait_ge(set0, 2)
                pe.matmul(b_cnt[:, 0:NE], ones_sq[:, :], carry[:, :], start=True, stop=True).then_inc(cnt_done, 1)
                pe.wait_ge(cols_ready, 1)
                for j in range(2):
                    pe.matmul(b_tab[0:1, j, :], row[:, j:j + 1], ident[:, :], start=True, stop=True)
                    last = pe.matmul(b_tab[0:1, 2 + j, :], expert[:, j:j + 1], ident[:, :], start=True, stop=True)
                last.then_inc(tab_done, 1)

            @block.vector
            def _(ve):
                n_ = [0]

                def step(ins):
                    ins.then_inc(dve, 1)
                    n_[0] += 1
                    ve.wait_ge(dve, n_[0])

                def by_tile(t):
                    return t[:, :].rearrange("p (a e) -> p a e", a=1).broadcast_to([P, 2, NE])

                def by_expert(t):
                    return t[:, :].rearrange("p (j a) -> p j a", a=1).broadcast_to([P, 2, NE])

                def by_token(t):
                    return t[:, :].rearrange("p (a e) -> p a e", a=1).broadcast_to([P, 3 * PAIRS, NE])

                ve.wait_ge(c_in, 64)
                ve.wait_ge(set0, 2)
                ve.wait_ge(cnt_done, 1)
                step(ve.tensor_copy(counts[:, :], b_cnt[:, 0:NE]))
                step(ve.tensor_tensor(over[:, :, :], counts[:, :].rearrange("p (e a) -> p e a", a=1).broadcast_to([P, NE, 21]),
                                      steps[:, :].rearrange("p (a k) -> p a k", a=1).broadcast_to([P, NE, 21]), ALU.is_gt))
                step(ve.tensor_reduce(n_tiles[:, :], over[:, :, :], AX.X, ALU.add))
                step(ve.tensor_tensor_scan(ends[:, :], one[:, :], n_tiles[:, :], 0.0, ALU.mult, ALU.add))
                step(ve.tensor_tensor(past[:, :, :], by_expert(tile_no), by_tile(ends), ALU.is_ge))
                step(ve.tensor_reduce(expert[:, :], past[:, :, :], AX.X, ALU.add))
                step(ve.tensor_tensor(past[:, :, :], past[:, :, :], by_tile(n_tiles), ALU.mult))
                step(ve.tensor_reduce(begin[:, :], past[:, :, :], AX.X, ALU.add))
                step(ve.tensor_tensor(mine[:, :, :], by_expert(expert), by_tile(names), ALU.is_equal))
                step(ve.tensor_tensor(past[:, :, :], mine[:, :, :], by_tile(counts), ALU.mult))
                step(ve.tensor_reduce(rows_of[:, :], past[:, :, :], AX.X, ALU.add))
                step(ve.tensor_tensor(past[:, :, :], mine[:, :, :], by_tile(regions), ALU.mult))
                step(ve.tensor_tensor(row[:, :], tile_no[:, :], begin[:, :], ALU.subtract))
                step(ve.tensor_scalar(row[:, :], row[:, :], float(P), float(P), ALU.mult, ALU.add))
                step(ve.tensor_tensor(row[:, :], row[:, :], rows_of[:, :], ALU.min))
                step(ve.tensor_reduce(begin[:, :], past[:, :, :], AX.X, ALU.add))
                step(ve.tensor_tensor(row[:, :], row[:, :], begin[:, :], ALU.add))
                step(ve.tensor_scalar(expert[:, :], expert[:, :], float(NE - 1), None, ALU.min))
                ve.sem_inc(cols_ready, 1)
                ve.wait_ge(tab_done, 1)
                step(ve.tensor_copy(table[0:1, :, :], b_tab[0:1, :, :].rearrange("p (a j) t -> p a (j t)", a=2)))
                step(ve.tensor_tensor(starts[:, :], ends[:, :], n_tiles[:, :], ALU.subtract))
                step(ve.scalar_tensor_tensor(out=d_all[:, :], in0=starts[:, :], scalar=float(P), in1=regions[:, :],
                                             op0=ALU.mult, op1=ALU.subtract))
                step(ve.tensor_scalar(d_all[:, :], d_all[:, :], float(-P), None, ALU.add))
                step(ve.scalar_tensor_tensor(out=first_last[:, :], in0=n_tiles[:, :], scalar=float(P), in1=regions[:, :],
                                             op0=ALU.mult, op1=ALU.add))
                step(ve.scalar_tensor_tensor(out=d_last[:, :], in0=n_tiles[:, :], scalar=float(P), in1=counts[:, :],
                                             op0=ALU.mult, op1=ALU.subtract))
                step(ve.tensor_tensor(shifted[:, :, :], places[:, :, :], by_token(first_last), ALU.is_gt))
                step(ve.tensor_tensor(shifted[:, :, :], shifted[:, :, :], by_token(d_last), ALU.mult))
                step(ve.tensor_tensor(shifted[:, :, :], shifted[:, :, :], by_token(d_all), ALU.add))
                step(ve.tensor_tensor(shifted[:, :, :], shifted[:, :, :], places[:, :, :], ALU.add))
                step(ve.scalar_tensor_tensor(out=shifted[:, :, :], in0=places[:, :, :], scalar=0.0, in1=shifted[:, :, :],
                                             op0=ALU.is_gt, op1=ALU.mult))
                for t in range(3 * PAIRS):
                    ve.max(best[:, t, :], shifted[:, t, :]).then_inc(dve, 1)
                    n_[0] += 1
                ve.wait_ge(dve, n_[0])
                step(ve.tensor_scalar(where[:, :, :], best[:, :, :], -1.0, None, ALU.add))


def experts(nc, es, sb, bank, a, v):
    ident, w_gu, w_d, weights_in = v["ident"], v["w_gu"], v["w_d"], v["weights_in"]
    table, dispatch, results = v["table"], v["dispatch"], v["results"]
    STEPS = ETILES // TS
    BODIES = STEPS // SB
    assert STEPS * TS == ETILES and BODIES * SB == STEPS
    with ExitStack() as local:
        def lsb(name, shape, dt=F32):
            return sb(name, shape, dt, local)

        def sem(name):
            return local.enter_context(nc.semaphore(name))

        rec = lsb("rec4", [P, SB, TS, REC])
        xT = lsb("xT4", [P, SB, TS, P])
        act_g = lsb("act_g", [P, SB, TS, D])
        hid = lsb("hid", [P, SB, TS, D])
        hT = lsb("hT", [P, SB, TS, P])
        y = lsb("y4", [P, SB, TS, D])
        b_xT = bank("b_xT4", [P, TS, P], local)
        b_gu = [bank(f"b_gu{j}", [P, TS, 2 * D], local) for j in range(3)]
        b_hT = bank("b_hT4", [P, TS, P], local)
        b_y = [bank(f"b_y{j}", [P, TS, D], local) for j in range(3)]
        marker = sem("marker4")
        rec_in = [sem(f"rec_in{j}") for j in range(SB)]
        xT_done = sem("xT_done4")
        xT_ready = sem("xT_ready4")
        gu_done = sem("gu_done")
        silu_ready = sem("silu_ready")
        hid_ready = sem("hid_ready")
        hT_done = sem("hT_done4")
        hT_ready = sem("hT_ready4")
        y_done = sem("y_done4")
        y_ready = sem("y_ready4")
        stored = [sem(f"stored{j}") for j in range(SB)]

        def loop(eng, body):
            body(0, True, False)
            with eng.Fori(1, BODIES - 1) as i:
                body(i, False, False)
            body(BODIES - 1, False, True)

        def tile_values(engine, n, tile, count, hi):
            at = table[0:1, n, tile:tile + count] if isinstance(tile, int) else table[0:1, n, bass.ds(tile, count)]
            return nc.values_load_multi_w_load_instructions(
                at, engines=[engine], min_val=0, max_val=hi,
                skip_runtime_bounds_check_because="the table's entries are clamped when it is made")[1]

        with nc.Block() as block:
            @block.sync
            def _(sp):
                def load(i, first):
                    rows_ = tile_values(mybir.EngineType.SP, 0, TS * SB * i, TS * SB, NE * CAP - P)
                    for j in range(SB):
                        if not first:
                            sp.wait_ge(y_ready, 2 * (SB * (i - 1) + j + 1))
                            sp.sem_inc(marker, 1)
                        for t in range(TS):
                            sp.dma_start(rec[:, j, t, :], dispatch[bass.ds(rows_[TS * j + t], P), :]).then_inc(rec_in[j], 16)

                load(0, True)
                with sp.Fori(1, BODIES) as i:
                    load(i, False)

            @block.gpsimd
            def _(po):
                def body(i, first, last):
                    for j in range(SB):
                        s = SB * i + j
                        po.wait_ge(y_ready, 2 * (s + 1))
                        po.sem_inc(marker, 1)
                        row = TS * P * s
                        dst = results[row:row + TS * P, :] if isinstance(row, int) else results[bass.ds(row, TS * P), :]
                        po.dma_start(dst.rearrange("(t p) d -> p t d", t=TS), y[:, j, :, :]).then_inc(stored[j], 16)

                loop(po, body)
                for j in range(SB):
                    po.wait_ge(stored[j], 16 * BODIES)

            @block.tensor
            def _(pe):
                pe.wait_ge(weights_in, 16 * 12)

                def transposes(j, i, s):
                    pe.wait_ge(rec_in[j], 16 * TS * (i + 1))
                    pe.sem_inc(marker, 1)
                    if not (isinstance(s, int) and s == 0):
                        pe.wait_ge(xT_ready, s)
                        pe.sem_inc(marker, 1)
                    for t in range(TS):
                        last = pe.transpose(b_xT[:, t, :], rec[:, j, t, 0:D], ident[:, :])
                    last.then_inc(xT_done, 1)

                def gate_up(j, s, e):
                    pe.wait_ge(xT_ready, s + 1)
                    for t in range(TS):
                        last = pe.matmul(b_gu[j % 3][:, t, :], xT[:, j, t, :],
                                         w_gu[:, bass.ds(e[t], 1), :].rearrange("p a n -> p (a n)"), start=True, stop=True)
                    last.then_inc(gu_done, 1)

                def hidden_transposes(j, s):
                    pe.wait_ge(hid_ready, s + 1)
                    for t in range(TS):
                        last = pe.transpose(b_hT[:, t, :], hid[:, j, t, :], ident[:, :])
                    last.then_inc(hT_done, 1)

                def down(j, s, e):
                    pe.wait_ge(hT_ready, s + 1)
                    pe.sem_inc(marker, 1)
                    if not (isinstance(s, int) and s < 3):
                        pe.wait_ge(y_ready, 2 * (s - 2))
                    for t in range(TS):
                        last = pe.matmul(b_y[j % 3][:, t, :], hT[:, j, t, :],
                                         w_d[:, bass.ds(e[t], 1), :].rearrange("p a n -> p (a n)"), start=True, stop=True)
                    last.then_inc(y_done, 1)

                def body(i, first, last):
                    lo = 0 if first else TS * (SB * i - 1)
                    n = TS * (SB + (0 if first else 1) + (0 if last else 1))
                    e = tile_values(mybir.EngineType.PE, 1, lo, n, NE - 1)

                    def of(k):
                        at = TS * (k + (0 if first else 1))
                        return e[at:at + TS]

                    for j in range(SB):
                        s = SB * i + j
                        if not (last and j == SB - 1):
                            gate_up((j + 1) % SB, s + 1, of(j + 1))
                        if not (first and j == 0):
                            down((j - 1) % SB, s - 1, of(j - 1))
                        hidden_transposes(j, s)
                        if not (last and j >= SB - 3):
                            transposes((j + 3) % SB, i + (j + 3) // SB, s + 3)
                    if last:
                        down(SB - 1, STEPS - 1, of(SB - 1))

                transposes(0, 0, 0)
                transposes(1, 0, 1)
                gate_up(0, 0, tile_values(mybir.EngineType.PE, 1, 0, TS, NE - 1))
                transposes(2, 0, 2)
                loop(pe, body)

            @block.scalar
            def _(act):
                def body(i, first, last):
                    lo = 0 if first else TS * (SB * i - 1)
                    e = tile_values(mybir.EngineType.Activation, 1, lo, TS * (SB + (0 if first else 1)), NE - 1)

                    def of(k):
                        at = TS * (k + (0 if first else 1))
                        return e[at:at + TS]

                    for j in range(SB):
                        s = SB * i + j
                        act.wait_ge(gu_done, s + 1)
                        act.activation(act_g[:, j, :, :], b_gu[j % 3][:, :, 0:D], ACT.Silu).then_inc(silu_ready, 1)
                        if not (first and j == 0):
                            scale_y((j - 1) % SB, i - (1 if j == 0 else 0), s - 1, of(j - 1))
                        act.wait_ge(hT_done, s + 1)
                        act.activation(hT[:, j, :, :], b_hT[:, :, :], ACT.Copy).then_inc(hT_ready, 1)
                    if last:
                        scale_y(SB - 1, BODIES - 1, STEPS - 1, of(SB - 1))

                def scale_y(j, i, s, e):
                    act.wait_ge(y_done, s + 1)
                    act.sem_inc(marker, 1)
                    if not (isinstance(i, int) and i == 0):
                        act.wait_ge(stored[j], 16 * i)
                        act.sem_inc(marker, 1)
                    for t in range(TS):
                        act.activation(y[:, j, t, :], b_y[j % 3][:, t, :], ACT.Copy,
                                       scale=rec[:, j, t, bass.ds(D + e[t], 1)]).then_inc(y_ready, 1)

                loop(act, body)

            @block.vector
            def _(ve):
                def take_xT(j, s):
                    ve.wait_ge(xT_done, s + 1)
                    ve.tensor_copy(xT[:, j, :, :], b_xT[:, :, :]).then_inc(xT_ready, 1)

                def body(i, first, last):
                    for j in range(SB):
                        s = SB * i + j
                        ve.wait_ge(silu_ready, s + 1)
                        ve.tensor_tensor(hid[:, j, :, :], act_g[:, j, :, :], b_gu[j % 3][:, :, D:2 * D], ALU.mult).then_inc(hid_ready, 1)
                        if not (last and j >= SB - 3):
                            take_xT((j + 3) % SB, s + 3)

                for s in range(3):
                    take_xT(s, s)
                loop(ve, body)


def combine(nc, es, sb, bank, a, out, v):
    w_gu, w_d = v["w_gu"], v["w_d"]
    base, xT_all, where, results = v["base"], v["xT_all"], v["where"], v["results"]
    PARTS = ((0, P), (1, P), (2, T2))
    with ExitStack() as local:
        def lsb(name, shape, dt=F32):
            return sb(name, shape, dt, local)

        def sem(name):
            return local.enter_context(nc.semaphore(name))

        idx = lsb("idx", [P, 2, 3, 8], I32)
        got = lsb("got", [P, 2, 3, KE, D])
        total = lsb("total", [P, 2, 3, D])
        act_g = lsb("act_g5", [P, NS, PT])
        hT = lsb("hT5", [P, NS, PT])
        b_g = [bank(f"b_g{e}", [P, 512], local) for e in range(NS)]
        b_u = [bank(f"b_u{e}", [P, 512], local) for e in range(NS)]
        b_y = [bank(f"b_y5{u}", [P, 3, D], local) for u in range(2)]
        zeroed = sem("zeroed5")
        marker = sem("marker5")
        idx_ready = sem("idx_ready5")
        gathered = [sem(f"gathered{u}") for u in range(2)]
        gu_done = sem("gu_done5")
        silu_ready = sem("silu_ready5")
        h_ready = sem("h_ready5")
        y_done = sem("y_done5")
        sum_ready = sem("sum_ready5")
        total_ready = sem("total_ready")
        out_done = [sem(f"out_done{u}") for u in range(2)]

        def loop(eng, body):
            body(0, True)
            with eng.Fori(1, PAIRS // 2) as i:
                body(i, False)

        with nc.Block() as block:
            @block.gpsimd
            def _(po):
                po.memset(got[:, :, :, :, :], 0.0).then_inc(zeroed, 1)
                po.wait_ge(zeroed, 1)

                def body(i, first):
                    for u in range(2):
                        n = 2 * i + u
                        po.wait_ge(idx_ready, n + 1)
                        po.sem_inc(marker, 1)
                        if not first:
                            po.wait_ge(sum_ready, 3 * (n - 2) + 1)
                            po.sem_inc(marker, 1)
                        for t, r in PARTS:
                            for k in range(KE):
                                po.indirect_dma_start(got[0:r, u, t, k, :], None, results,
                                                      bass.IndirectOffsetOnAxis(idx[0:r, u, t, k:k + 1], 0)).then_inc(gathered[u], 16)

                loop(po, body)

            @block.tensor
            def _(pe):
                def body(i, first):
                    for u in range(2):
                        n = 2 * i + u
                        x = xT_all[:, n * PT:(n + 1) * PT] if first else xT_all[:, bass.ds(n * PT, PT)]
                        if not (first and u == 0):
                            pe.wait_ge(h_ready, 2 * n)
                            pe.sem_inc(marker, 1)
                        for e in range(NS):
                            pe.matmul(b_g[e][:, 0:PT], w_gu[:, NE + e, 0:D], x, start=True, stop=True)
                            last = pe.matmul(b_u[e][:, 0:PT], w_gu[:, NE + e, D:2 * D], x, start=True, stop=True)
                        last.then_inc(gu_done, 1)
                        pe.wait_ge(h_ready, 2 * (n + 1))
                        pe.sem_inc(marker, 1)
                        if not first:
                            pe.wait_ge(sum_ready, 3 * (n - 1))
                            pe.sem_inc(marker, 1)
                        at = 0
                        for t, r in PARTS:
                            for e in range(NS):
                                last = pe.matmul(b_y[u][0:r, t, :], hT[:, e, at:at + r], w_d[:, NE + e, :],
                                                 start=(e == 0), stop=(e == NS - 1))
                            at += r
                        last.then_inc(y_done, 1)

                loop(pe, body)

            @block.scalar
            def _(act):
                def body(i, first):
                    for u in range(2):
                        n = 2 * i + u
                        act.wait_ge(gu_done, n + 1)
                        act.sem_inc(marker, 1)
                        if not (first and u == 0):
                            act.wait_ge(h_ready, 2 * n)
                            act.sem_inc(marker, 1)
                        for e in range(NS):
                            act.activation(act_g[:, e, :], b_g[e][:, 0:PT], ACT.Silu).then_inc(silu_ready, 1)

                loop(act, body)

            @block.vector
            def _(ve):
                def body(i, first):
                    for u in range(2):
                        n = 2 * i + u
                        if not first:
                            ve.wait_ge(gathered[u], 16 * 3 * KE * i)
                            ve.sem_inc(marker, 1)
                        w = where[:, 3 * n:3 * n + 3, :] if first else where[:, bass.ds(3 * n, 3), :]
                        ve.tensor_copy(idx[:, u, :, :], w).then_inc(idx_ready, 1)
                    for u in range(2):
                        n = 2 * i + u
                        ve.wait_ge(silu_ready, 2 * (n + 1))
                        ve.sem_inc(marker, 1)
                        if not (first and u == 0):
                            ve.wait_ge(y_done, n)
                            ve.sem_inc(marker, 1)
                        for e in range(NS):
                            ve.tensor_tensor(hT[:, e, :], act_g[:, e, :], b_u[e][:, 0:PT], ALU.mult).then_inc(h_ready, 1)
                        if not first:
                            ve.wait_ge(out_done[u], 16 * 4 * i)
                            ve.sem_inc(marker, 1)
                        ve.wait_ge(gathered[u], 16 * 3 * KE * (i + 1))
                        ve.sem_inc(marker, 1)
                        ve.tensor_reduce(total[:, u, :, :], got[:, u, :, :, :].rearrange("p t k d -> p t d k"), AX.X,
                                         ALU.add).then_inc(sum_ready, 1)
                        ve.wait_ge(sum_ready, 3 * n + 1)
                        bs = base[:, 3 * n:3 * n + 3, :] if first else base[:, bass.ds(3 * n, 3), :]
                        ve.tensor_tensor(total[:, u, :, :], total[:, u, :, :], bs, ALU.add).then_inc(sum_ready, 1)
                        ve.wait_ge(sum_ready, 3 * n + 2)
                        ve.sem_inc(marker, 1)
                        ve.wait_ge(y_done, n + 1)
                        ve.tensor_tensor(total[:, u, 0:2, :], total[:, u, 0:2, :], b_y[u][:, 0:2, :], ALU.add).then_inc(total_ready, 1)
                        ve.tensor_tensor(total[0:T2, u, 2, :], total[0:T2, u, 2, :], b_y[u][0:T2, 2, :], ALU.add).then_inc(sum_ready, 1)

                loop(ve, body)

            @block.sync
            def _(sp):
                def body(i, first):
                    for u in range(2):
                        n = 2 * i + u
                        sp.wait_ge(total_ready, n + 1)
                        sp.sem_inc(marker, 1)
                        sp.wait_ge(sum_ready, 3 * (n + 1))
                        sp.sem_inc(marker, 1)
                        for w in range(2):
                            b = 2 * n + w
                            o = out[b, :, :] if first else out[bass.ds(b, 1), :, :].rearrange("a l d -> (a l) d")
                            sp.dma_start(o[NP_:L, :], total[:, u, w, :]).then_inc(out_done[u], 16)
                            sp.dma_start(o[0:NP_, :], total[w * NP_:(w + 1) * NP_, u, 2, :]).then_inc(out_done[u], 16)

                loop(sp, body)
                for u in range(2):
                    sp.wait_ge(out_done[u], 16 * 4 * (PAIRS // 2))


def kernel(**inputs):
    import concourse.bacc as bacc
    from concourse.bass_utils import run_bass_kernel_spmd

    x = {n.replace("L0_", ""): np.asarray(t) for n, t in inputs.items()}
    f32 = np.float32
    arrays = {}
    p = x["x"].reshape(B, 3, 6, 16, 6, 16).transpose(1, 3, 5, 0, 2, 4).reshape(CHUNKS, P, B * NP_)
    arrays["patches"] = np.ascontiguousarray(p.transpose(1, 0, 2))
    w_all = np.zeros((3, 16, 16, D), f32)
    w_all[..., 0:64] = x["tok_W_main"].reshape(64, 3, 16, 16).transpose(1, 2, 3, 0)
    sx = x["tok_W_sx"].reshape(16, 3, 16, 16).transpose(1, 2, 3, 0)
    sy = x["tok_W_sy"].reshape(16, 3, 16, 16).transpose(1, 2, 3, 0)
    w_all[:, :, 0:8, 64:80] = sx[:, :, 8:16]
    w_all[:, :, 8:16, 80:96] = sx[:, :, 0:8]
    w_all[:, 0:8, :, 96:112] = sy[:, 8:16]
    w_all[:, 8:16, :, 112:128] = sy[:, 0:8]
    arrays["w_all"] = np.ascontiguousarray(w_all.reshape(CHUNKS, P, D).transpose(1, 0, 2))
    perm = np.zeros((P, 5, D), f32)
    lo, hi, ylo, yhi = 64, 80, 96, 112
    for k in range(64):
        perm[k, 0, k] = 1
    for k in range(16):
        perm[hi + k, 0, 64 + k] = perm[lo + k, 0, 80 + k] = perm[yhi + k, 0, 96 + k] = perm[ylo + k, 0, 112 + k] = 1
        perm[lo + k, 1, 64 + k] = 1
        perm[hi + k, 2, 80 + k] = 1
        perm[ylo + k, 3, 96 + k] = 1
        perm[yhi + k, 4, 112 + k] = 1
    arrays["perm"] = perm
    arrays["ident"] = np.eye(P, dtype=f32)
    arrays["shift36"] = np.eye(NP_, 2 * NP_, k=NP_, dtype=f32)
    mask = np.zeros((P, H), f32)
    for h in range(H):
        mask[h * E:(h + 1) * E, h] = E ** -0.5
    arrays["head_mask"] = mask
    arrays["b_tok"] = np.concatenate([x["tok_b_main"], x["tok_b_sx"], x["tok_b_sx"], x["tok_b_sy"],
                                      x["tok_b_sy"]]).reshape(P, 1)
    arrays["rows"] = np.concatenate([x["attn_bv"], x["attn_bo"]]).reshape(1, 2 * D)
    for n in "qkvo":
        arrays["w" + n] = np.ascontiguousarray(x["attn_W" + n].T)
    for n in "qk":
        arrays["b" + n] = x["attn_b" + n].reshape(P, 1)
    arrays["ln_g"], arrays["ln_b"] = x["tok_ln_g"], x["tok_ln_b"]
    for n in ("g", "u", "d"):
        arrays["w_" + n] = np.concatenate([x["ffn_W" + n], x["ffn_sW" + n]]).transpose(1, 0, 2)
    arrays["w_gu"] = np.ascontiguousarray(np.concatenate([arrays.pop("w_g"), arrays.pop("w_u")], axis=2))
    arrays["w_d"] = np.ascontiguousarray(arrays["w_d"])
    arrays["wr"] = x["ffn_Wr"]
    arrays["tri"] = np.triu(np.ones((P, P), f32), 1)
    arrays["region"] = (np.arange(NE, dtype=f32) * CAP + P + 1).reshape(1, NE)
    arrays["region_all"] = np.tile(np.arange(NE, dtype=f32) * CAP, (P, 1))
    arrays["names"] = np.tile(np.arange(NE, dtype=f32), (P, 1))
    arrays["steps"] = np.tile(np.arange(21, dtype=f32) * P, (P, 1))
    arrays["tile_no"] = np.arange(2 * P, dtype=f32).reshape(2, P).T.copy()
    arrays["txt"] = np.ascontiguousarray(x["txt"].transpose(1, 0, 2))

    nc = bacc.Bacc("TRN2", target_bir_lowering=False, num_devices=1)
    aps = {n: nc.dram_tensor("in_" + n, t.shape, mybir.dt.from_np(t.dtype), kind="ExternalInput").ap() for n, t in arrays.items()}
    out = nc.dram_tensor("out_h", (B, L, D), F32, kind="ExternalOutput").ap()
    build(nc, aps, out)
    r = run_bass_kernel_spmd(nc, [{"in_" + n: t for n, t in arrays.items()}], core_ids=[0])
    return r.results[0]["out_h"]
```

```python
from contextlib import ExitStack

import concourse.bass as bass
import numpy as np
from concourse import mybir

F32 = mybir.dt.float32
I32 = mybir.dt.int32
ALU = mybir.AluOpType
ACT = mybir.ActivationFunctionType
AX = mybir.AxisListType

P = 128
B = 16
D = 128
NP_ = 36
NT = 128
L = NP_ + NT
H = 8
E = D // H
ROWS = H * L
PAIRS = B // 2
TILES = 2 * ROWS // P + 1
GT = 3
GROUPS = TILES // GT
MID = ROWS // P
TAIL = ROWS - MID * P
TOPK = 25
EPS = 1e-5
MARK = -3.0e38
CHUNKS = 6


NE = 64
NS = 2
KE = 6
SHARE = (4, 4, 0, 5, 0, 3, 2)
SCATTERED = sum(SHARE[3:])
EARLY = 3
T2 = 2 * NP_
PT = 2 * L
TOKENS = B * L
CAP = P + TOKENS
REC = D + NE + 1
TS = 2
SB = 6
MOST = (TOKENS * KE + NE * (P - 1)) // P
ETILES = -(-MOST // TS) * TS
SENT = -2.9e38


def slot(g):
    return g % 3 if g < GROUPS - 1 else 3


def s_bank(g):
    return g % 2 if g < GROUPS - 1 else 2


def build(nc, a, out):
    es = ExitStack()
    with es:
        def sb(name, shape, dt=F32, where=es):
            return where.enter_context(nc.sbuf_tensor(name, shape, dt))

        def bank(name, shape, where):
            return where.enter_context(nc.psum_tensor(name, shape, F32))

        ident = sb("ident", [P, P])
        h_text = sb("h_text", [P, B, D])
        h_patch = sb("h_patch", [NP_, B, D])
        h2_patch = sb("h2_patch", [2 * NP_, PAIRS, D])
        shift36 = sb("shift36", [NP_, 2 * NP_])
        rows = sb("rows", [1, D])
        ones = sb("ones", [1, P])
        rstd_t = sb("rstd_t", [P, B])
        nbias_t = sb("nbias_t", [P, B])
        rstd_p = sb("rstd_p", [NP_, B])
        nbias_p = sb("nbias_p", [NP_, B])
        wq = sb("wq", [P, D])
        wk = sb("wk", [P, D])
        wv = sb("wv", [P, D])
        wo = sb("wo", [P, D])
        bq = sb("bq", [P, 1])
        bk = sb("bk", [P, 1])
        bv = sb("bv", [P, 1])
        head_mask = sb("head_mask", [P, H])
        w_gu = sb("w_gu", [P, NE + NS, 2 * D])
        wr = sb("wr", [P, NE])
        tri = sb("tri", [P, P])
        ones_sq = sb("ones_sq", [P, P])
        zeros = sb("zeros", [P, REC])
        codes = sb("codes", [P, 3 * PAIRS])
        before = sb("before", [P, 2 * NE])
        weights_in = es.enter_context(nc.semaphore("weights_in"))
        dispatch = nc.dram_tensor("dispatch", (NE * CAP, REC), F32).ap()
        results = nc.dram_tensor("results", (3 * PAIRS * P * KE + 2 * P * P, D), F32).ap()
        shared_in = es.enter_context(nc.semaphore("shared_in"))
        wd_in = es.enter_context(nc.semaphore("wd_in"))
        base = sb("base", [P, 3 * PAIRS, D])
        xT_all = sb("xT_all", [P, PAIRS * PT])
        carry = sb("carry", [P, 3, NE])
        router = Router(nc, sb, lambda name: es.enter_context(nc.semaphore(name)), dict(locals()))
        with ExitStack() as values:
            v_t = sb("v_t", [P, 2, H, D], where=values)
            v_p = sb("v_p", [NP_, 2, H, D], where=values)
            prologue(nc, es, sb, bank, a, dict(locals()))
            attention(nc, es, sb, bank, a, dict(locals()))
        w_d = sb("w_d", [P, NE + NS, D])
        aside = sb("aside", [P, 2 * P])
        table = sb("table", [1, 2, 2 * P], I32)
        plan(nc, es, sb, bank, a, dict(locals()))
        experts(nc, es, sb, bank, a, dict(locals()))
        combine(nc, es, sb, bank, a, out, dict(locals()))


def prologue(nc, es, sb, bank, a, v):
    ident, h_text, h_patch, rows, ones = v["ident"], v["h_text"], v["h_patch"], v["rows"], v["ones"]
    with ExitStack() as local:
        def lsb(name, shape, dt=F32):
            return sb(name, shape, dt, local)

        def sem(name):
            return local.enter_context(nc.semaphore(name))

        patches = lsb("patches", [P, CHUNKS, B * NP_])
        w_all = lsb("w_all", [P, CHUNKS, D])
        perm = lsb("perm", [P, 5, D])
        grid = lsb("grid", [P, B, 8, 8])
        tok_T = lsb("tok_T", [P, B * NP_])
        b_tok = lsb("b_tok", [P, 1])
        gain = lsb("gain", [NP_, D])
        shiftb = lsb("shiftb", [NP_, D])
        stats_p = lsb("stats_p", [NP_, B, 6])
        stats_t = lsb("stats_t", [P, B, 6])
        mv_p = lsb("mv_p", [NP_, B, 2])
        mv_t = lsb("mv_t", [P, B, 2])
        sd_p = lsb("sd_p", [NP_, B])
        sd_t = lsb("sd_t", [P, B])
        ps_u = [bank(f"ps_u{i}", [P, 512], local) for i in range(2)]
        ps_tok = [bank(f"ps_tok{i}", [P, 4, D], local) for i in range(4)]
        w_in, c_in, t_in = sem("w_in"), sem("c_in"), sem("t_in")
        p_in = [sem(f"p_in{c}") for c in range(CHUNKS)]
        b_in = sem("b_in")
        proj_done, grid_zero, grid_ready, tok_ready = sem("proj_done"), sem("grid_zero"), sem("grid_ready"), sem("tok_ready")
        sum_ready, tokT_ready = sem("sum_ready"), sem("tokT_ready")
        dve, sd_ready, var_ready = sem("dve"), sem("sd_ready"), sem("var_ready")
        SPLIT = 14
        zeroed = sem("zeroed0")
        with nc.Block() as block:
            @block.gpsimd
            def _(po):
                for t, value in ((v["v_t"], 0.0), (v["v_p"], 0.0), (v["zeros"], 0.0), (v["ones_sq"], 1.0)):
                    po.memset(t.ap(), value).then_inc(zeroed, 1)
                v["router"].constants(po)
                po.wait_ge(zeroed, 4)
                po.wait_ge(v["router"].set0, 9)

            @block.sync
            def _(sp):
                sp.dma_start(w_all[:, :, :], a["w_all"]).then_inc(w_in, 16)
                for c in range(CHUNKS):
                    sp.dma_start(patches[:, c, :], a["patches"][:, c, :]).then_inc(p_in[c], 16)
                sp.dma_start(h_text[:, :, :], a["txt"]).then_inc(t_in, 16)

            @block.scalar
            def _(act):
                for t, n in ((ident, "ident"), (perm, "perm"), (v["shift36"], "shift36"), (rows, "rows"),
                             (v["wq"], "wq"), (v["wk"], "wk"), (v["wv"], "wv"), (v["wo"], "wo"),
                             (v["bq"], "bq"), (b_tok, "b_tok"), (v["bk"], "bk"), (v["bv"], "bv"), (v["head_mask"], "head_mask")):
                    act.dma_start(t.ap(), a[n]).then_inc(c_in, 16)
                act.dma_start(gain[:, :], a["ln_g"].partition_broadcast(NP_)).then_inc(b_in, 16)
                act.dma_start(shiftb[:, :], a["ln_b"].partition_broadcast(NP_)).then_inc(b_in, 16)
                act.wait_ge(grid_zero, 1)
                act.wait_ge(proj_done, 1)
                act.activation(grid[:, 0:SPLIT, 1:7, 1:7],
                               ps_u[0][:, 0:SPLIT * NP_].rearrange("p (b i j) -> p b i j", b=SPLIT, i=6),
                               ACT.Copy).then_inc(grid_ready, 1)
                act.wait_ge(proj_done, 2)
                act.activation(grid[:, SPLIT:B, 1:7, 1:7],
                               ps_u[1][:, 0:(B - SPLIT) * NP_].rearrange("p (b i j) -> p b i j", b=B - SPLIT, i=6),
                               ACT.Copy).then_inc(grid_ready, 1)
                for half, (lo, hi) in enumerate(((0, SPLIT), (SPLIT, B))):
                    act.wait_ge(c_in, 16 * 13)
                    act.wait_ge(sum_ready, half + 1)
                    act.activation(tok_T[:, lo * NP_:hi * NP_], ps_u[half][:, 0:(hi - lo) * NP_], ACT.Identity,
                                   bias=b_tok[:, 0:1]).then_inc(tokT_ready, 1)
                act.wait_ge(var_ready, 1)
                act.activation(sd_t[:, :], mv_t[:, :, 1], ACT.Sqrt).then_inc(sd_ready, 1)
                act.wait_ge(var_ready, 2)
                act.activation(sd_p[:, :], mv_p[:, :, 1], ACT.Sqrt).then_inc(sd_ready, 1)
                act.wait_ge(var_ready, 3)
                act.activation(sd_p[:, :], mv_p[:, :, 1], ACT.Sqrt).then_inc(sd_ready, 1)

            @block.tensor
            def _(pe):
                pe.wait_ge(w_in, 16)
                for half, (lo, hi) in enumerate(((0, SPLIT), (SPLIT, B))):
                    for c in range(CHUNKS):
                        if half == 0:
                            pe.wait_ge(p_in[c], 16)
                        last = pe.matmul(ps_u[half][:, 0:(hi - lo) * NP_], w_all[:, c, :],
                                         patches[:, c, lo * NP_:hi * NP_], start=(c == 0), stop=(c == CHUNKS - 1))
                    last.then_inc(proj_done, 1)
                pe.wait_ge(c_in, 16 * 13)
                for half, (lo, hi) in enumerate(((0, SPLIT), (SPLIT, B))):
                    pe.wait_ge(grid_ready, half + 1)
                    for s, (di, dj) in enumerate(((0, 0), (0, 1), (0, -1), (1, 0), (-1, 0))):
                        last = pe.matmul(ps_u[half][:, 0:(hi - lo) * NP_].rearrange("p (b i j) -> p b i j", i=6, j=6),
                                         perm[:, s, :], grid[:, lo:hi, 1 + di:7 + di, 1 + dj:7 + dj],
                                         start=(s == 0), stop=(s == 4))
                    last.then_inc(sum_ready, 1)
                for b in range(B):
                    pe.wait_ge(tokT_ready, 1 if b < SPLIT else 2)
                    pe.transpose(ps_tok[b // 4][0:NP_, b % 4, :], tok_T[:, b * NP_:(b + 1) * NP_],
                                 ident[:, :]).then_inc(tok_ready, 1)

            @block.vector
            def _(ve):
                n = [0]

                def then(ins):
                    ins.then_inc(dve, 1)
                    n[0] += 1

                def settle():
                    ve.wait_ge(dve, n[0])

                ve.memset(grid[:, :, :, :], 0.0).then_inc(grid_zero, 1)
                then(ve.memset(ones[:, :], 1.0))
                ve.wait_ge(t_in, 16)
                for b in range(B):
                    then(ve.bn_stats(stats_t[:, b, :], h_text[:, b, :]))
                settle()
                for b in range(B):
                    then(ve.bn_aggr(mv_t[:, b, :], stats_t[:, b, :]))
                settle()
                ve.tensor_scalar(mv_t[:, :, 1], mv_t[:, :, 1], EPS, None, ALU.add).then_inc(var_ready, 1)
                for b in range(B):
                    ve.wait_ge(tok_ready, b // 4 * 4 + 4)
                    then(ve.bn_stats(stats_p[:, b, :], ps_tok[b // 4][0:NP_, b % 4, :]))
                settle()
                for b in range(B):
                    then(ve.bn_aggr(mv_p[:, b, :], stats_p[:, b, :]))
                settle()
                ve.tensor_scalar(mv_p[:, :, 1], mv_p[:, :, 1], EPS, None, ALU.add).then_inc(var_ready, 1)
                ve.wait_ge(sd_ready, 2)
                then(ve.reciprocal(sd_p[:, :], sd_p[:, :]))
                settle()
                for b in range(B):
                    then(ve.tensor_scalar(h_patch[:, b, :], ps_tok[b // 4][0:NP_, b % 4, :], mv_p[:, b, 0:1],
                                          sd_p[:, b:b + 1], ALU.subtract, ALU.mult))
                ve.wait_ge(b_in, 32)
                settle()
                then(ve.tensor_tensor(h_patch[:, :, :], h_patch[:, :, :],
                                      gain[:, :].rearrange("p (a d) -> p a d", a=1).broadcast_to([NP_, B, D]), ALU.mult))
                settle()
                then(ve.tensor_tensor(h_patch[:, :, :], h_patch[:, :, :],
                                      shiftb[:, :].rearrange("p (a d) -> p a d", a=1).broadcast_to([NP_, B, D]), ALU.add))
                settle()
                for b in range(B):
                    then(ve.bn_stats(stats_p[:, b, :], h_patch[:, b, :]))
                settle()
                for b in range(B):
                    then(ve.bn_aggr(mv_p[:, b, :], stats_p[:, b, :]))
                settle()
                ve.tensor_scalar(mv_p[:, :, 1], mv_p[:, :, 1], EPS, None, ALU.add).then_inc(var_ready, 1)
                then(ve.reciprocal(v["rstd_t"][:, :], sd_t[:, :]))
                ve.wait_ge(sd_ready, 3)
                then(ve.reciprocal(v["rstd_p"][:, :], sd_p[:, :]))
                settle()
                for mv, rstd, nb in ((mv_t, "rstd_t", "nbias_t"), (mv_p, "rstd_p", "nbias_p")):
                    then(ve.scalar_tensor_tensor(out=v[nb][:, :], in0=mv[:, :, 0], scalar=-1.0, in1=v[rstd][:, :],
                                                 op0=ALU.mult, op1=ALU.mult))
                settle()


def attention(nc, es, sb, bank, a, v):
    ident, h_text, h_patch, rows, ones = v["ident"], v["h_text"], v["h_patch"], v["rows"], v["ones"]
    h2_patch, shift36, head_mask = v["h2_patch"], v["shift36"], v["head_mask"]
    wq, wk, wv, wo, bq, bk, bv = (v[n] for n in ("wq", "wk", "wv", "wo", "bq", "bk", "bv"))
    rstd_t, nbias_t, rstd_p, nbias_p = (v[n] for n in ("rstd_t", "nbias_t", "rstd_p", "nbias_p"))
    with ExitStack() as local:
        def lsb(name, shape, dt=F32):
            return sb(name, shape, dt, local)

        def sem(name):
            return local.enter_context(nc.semaphore(name))

        xh_t = lsb("xh_t", [P, 2, D])
        xh_p = lsb("xh_p", [NP_, 2, D])
        x_T = lsb("x_T", [P, 2, L])
        q_T = lsb("q_T", [P, 2, L])
        k_T = lsb("k_T", [P, 2, L])
        q_exp = lsb("q_exp", [P, 2, H, L])
        q_flat = q_exp[:, :, :, :].rearrange("p u h l -> p (u h l)")
        v_t, v_p = v["v_t"], v["v_p"]
        scores = lsb("scores", [P, 4, GT, L])
        work = lsb("work", [P, 4, GT, L])
        e_all = lsb("e_all", [P, 4, GT, L])
        sum_all = lsb("sum_all", [P, 4, GT])
        sum_rest = lsb("sum_rest", [P, 4, GT])
        inv = lsb("inv", [P, 4, GT])
        minus_one = lsb("minus_one", [P, GT])
        top = lsb("top", [P, 4, GT, 8])
        topw = lsb("topw", [P, GT, 8])
        neg_max = lsb("neg_max", [P, 4, GT])
        pT_t = lsb("pT_t", [P, TILES * P])
        pT_p = lsb("pT_p", [NP_, TILES * P])
        oT_t = lsb("oT_t", [P, 2, NT])
        oT_p = lsb("oT_p", [P, 2 * NP_])
        b_scores = [bank(f"b_scores{i}", [P, 512], local) for i in range(3)]
        b_ptt = bank("b_ptt", [P, GT, P], local)
        b_ptp = bank("b_ptp", [P, GT, P], local)
        b_x = bank("b_x", [P, 512], local)
        b_q = bank("b_q", [P, 512], local)
        b_v = bank("b_v", [P, 4, D], local)
        b_k = b_v[:, :, :].rearrange("p a d -> p (a d)")

        zeroed = sem("zeroed")
        r_in = sem("r_in")
        zeros_out = sem("zeros_out")
        marker = sem("marker")
        xh_ready = sem("xh_ready")
        xT_done = sem("xT_done")
        xT_ready = sem("xT_ready")
        q_done = sem("q_done")
        k_done = sem("k_done")
        v_done = sem("v_done")
        q_ready = sem("q_ready")
        k_ready = sem("k_ready")
        v_ready = sem("v_ready")
        qe_ready = sem("qe_ready")
        s_done = sem("s_done")
        s_ready = sem("s_ready")
        nm_ready = sem("nm_ready")
        w_ready = sem("w_ready")
        ea_ready = sem("ea_ready")
        er_ready = sem("er_ready")
        sum_ready = sem("sum_ready2")
        inv_ready = sem("inv_ready")
        diff_ready = sem("diff_ready")
        p_ready = sem("p_ready")
        pt_done = sem("pt_done")
        pt_ready = sem("pt_ready")
        o_done = sem("o_done")
        o_ready = sem("o_ready")
        y_done = sem("y_done")
        y_ready = sem("y_ready")
        chain = sem("chain")



        def loop(eng, body):
            for i in range(3):
                body(i, i == 0, False)
            with eng.Fori(3, PAIRS - 1) as i:
                body(i, False, False)
            body(PAIRS - 1, False, True)

        def has(i, back):
            return not isinstance(i, int) or i >= back

        router = v["router"]
        with nc.Block() as block:
            @block.sync
            def _(sp):
                for t, n in ((v["wr"], "wr"), (v["tri"], "tri"), (v["carry"][:, 0, :], "region"),
                             (v["codes"], "codes"), (v["before"], "before")):
                    sp.dma_start(t if n == "region" else t[:, :], a[n]).then_inc(r_in, 16)
                for lo in range(0, NE + NS, 11):
                    sp.dma_start(v["w_gu"][:, lo:lo + 11, :], a["w_gu"][:, lo:lo + 11, :]).then_inc(v["weights_in"], 16)
                sp.dma_start(v["dispatch"].rearrange("(e r) c -> r e c", e=NE)[0:P, :, :],
                             v["zeros"][:, :].rearrange("p (a c) -> p a c", a=1).broadcast_to([P, NE, REC])).then_inc(zeros_out, 16)
                sp.wait_ge(zeros_out, 16)

            @block.tensor
            def _(pe):
                def transposes(n):
                    pe.wait_ge(xh_ready, 4 * (n + 1))
                    pe.sem_inc(marker, 1)
                    for u in range(2):
                        pe.transpose(b_x[:, u * L:u * L + NP_], xh_p[:, u, :], ident[0:NP_, 0:NP_])
                        last = pe.transpose(b_x[:, u * L + NP_:u * L + L], xh_t[:, u, :], ident[:, :])
                    last.then_inc(xT_done, 1)

                def project_q(n):
                    pe.wait_ge(xT_ready, n + 1)
                    pe.matmul(b_q[:, 0:2 * L], wq[:, :], x_T[:, :, :].rearrange("p u l -> p (u l)"),
                              start=True, stop=True).then_inc(q_done, 1)

                def project_k(n):
                    pe.matmul(b_k[:, 0:2 * L], wk[:, :], x_T[:, :, :].rearrange("p u l -> p (u l)"),
                              start=True, stop=True).then_inc(k_done, 1)

                def project_v(n):
                    for u in range(2):
                        for t, (lo, n_) in enumerate(((NP_, NT), (0, NP_))):
                            last = pe.matmul(b_v[0:n_, 2 * t + u, :], x_T[:, u, lo:lo + n_], wv[:, :], start=True, stop=True)
                    last.then_inc(v_done, 1)

                def score_group(i, g, G):
                    if g == 0:
                        pe.wait_ge(k_ready, 2 * i + 1)
                        pe.sem_inc(marker, 1)
                        pe.wait_ge(qe_ready, 2 * i + 1)
                        pe.sem_inc(marker, 1)
                    if g == 3:
                        pe.wait_ge(k_ready, 2 * i + 2)
                        pe.sem_inc(marker, 1)
                        pe.wait_ge(qe_ready, 2 * i + 2)
                        pe.sem_inc(marker, 1)
                    back = {0: 3, 1: 3, GROUPS - 1: GROUPS}.get(g, 2)
                    if not (isinstance(G, int) and (G < 2 or G == GROUPS - 1)):
                        pe.wait_ge(ea_ready, 3 * (G - back + 1))
                        pe.sem_inc(marker, 1)
                        pe.wait_ge(s_ready, G - back + 1)
                        pe.sem_inc(marker, 1)
                    bk_ = b_scores[s_bank(g)]
                    for t in range(GT):
                        k = GT * g + t
                        o = bk_[:, t * L:(t + 1) * L]
                        if k < MID:
                            last = pe.matmul(o, q_flat[:, k * P:(k + 1) * P], k_T[:, 0, :], start=True, stop=True)
                        elif k == MID:
                            pe.matmul(o, q_flat[:, ROWS - (P - TAIL):ROWS + TAIL], k_T[:, 1, :], start=True, stop=True)
                            last = pe.matmul(bk_[0:TAIL, t * L:(t + 1) * L], q_flat[:, ROWS - TAIL:ROWS], k_T[:, 0, :],
                                             start=True, stop=True)
                        else:
                            r = ROWS + TAIL + (k - MID - 1) * P
                            last = pe.matmul(o, q_flat[:, r:r + P], k_T[:, 1, :], start=True, stop=True)
                    last.then_inc(s_done, 1)

                def prob_transposes(g, G):
                    pe.wait_ge(p_ready, G + 1)
                    if not isinstance(G, int) or G >= 1:
                        pe.sem_inc(marker, 1)
                        pe.wait_ge(pt_ready, 2 * G)
                    for t in range(GT):
                        pr = e_all[:, slot(g), t, :]
                        pe.transpose(b_ptt[:, t, :], pr[:, NP_:L], ident[:, :])
                        last = pe.transpose(b_ptp[0:NP_, t, :], pr[:, 0:NP_], ident[:, :])
                    last.then_inc(pt_done, 1)

                def attend(i, u, half):
                    pe.wait_ge(pt_ready, 2 * (GROUPS * i + (2, 4, 6, 7)[2 * u + half]))
                    pe.sem_inc(marker, 1)
                    if u == 0 and half == 0:
                        pe.wait_ge(v_ready, 2 * (i + 1))
                        pe.sem_inc(marker, 1)
                    first_row = 0 if u == 0 else TILES * P - ROWS
                    for h in range(4 * half, 4 * half + 4):
                        c = first_row + h * L
                        pe.matmul(b_x[:, 0:L], v_t[:, u, h, :], pT_t[:, c:c + L], start=(h == 0), stop=False)
                        last = pe.matmul(b_x[:, 0:L], v_p[:, u, h, :], pT_p[:, c:c + L], start=False, stop=(h == H - 1))
                    if half == 1:
                        last.then_inc(o_done, 1)

                def out_projection(i):
                    pe.wait_ge(o_ready, 4 * (i + 1))
                    pe.sem_inc(marker, 1)
                    for u in range(2):
                        o = b_x[:, u * D:(u + 1) * D]
                        pe.matmul(o, oT_t[:, u, :], wo[:, :], start=True, stop=False)
                        pe.matmul(o, ident[:, :], h_text[:, 2 * i + u, :], start=False, stop=False)
                        pe.matmul(o, ones[0:1, :], rows[0:1, :], start=False, stop=True)
                    o = b_x[0:2 * NP_, 2 * D:3 * D]
                    pe.matmul(o, oT_p[:, :], wo[:, :], start=True, stop=False)
                    for u in range(2):
                        sel = ident[0:NP_, 0:2 * NP_] if u == 0 else shift36[:, :]
                        pe.matmul(o, sel, h_patch[:, 2 * i + u, :], start=False, stop=False)
                    pe.matmul(o, ones[0:1, 0:2 * NP_], rows[0:1, :], start=False, stop=True).then_inc(y_done, 1)

                def body(i, first, last):
                    for g in range(GROUPS):
                        G = GROUPS * i + g
                        if not (first and g < 2):
                            prob_transposes((g - 2) % GROUPS, G - 2)
                        if g + 2 < GROUPS:
                            score_group(i, g + 2, G + 2)
                        elif not last:
                            score_group(i + 1, g + 2 - GROUPS, G + 2)
                        if g == 0:
                            if not first:
                                pe.wait_ge(v_ready, 2 * i)
                                pe.sem_inc(marker, 1)
                            pe.wait_ge(k_ready, 2 * (i + 1))
                            pe.sem_inc(marker, 1)
                            project_v(i)
                            if not last:
                                if not first:
                                    pe.wait_ge(o_ready, 4 * i - 2)
                                    pe.sem_inc(marker, 1)
                                transposes(i + 1)
                        if g == 0 and has(i, 2):
                            if isinstance(i, int):
                                pe.wait_ge(r_in, 80)
                                pe.sem_inc(marker, 1)
                            router.project(pe, i - 2, b_q)
                        if g == 1 and not first:
                            if last:
                                pe.wait_ge(o_ready, 4 * i - 2)
                            else:
                                pe.wait_ge(xT_ready, i + 2)
                            pe.sem_inc(marker, 1)
                            attend(i - 1, 1, 0)
                        if g == 2 and has(i, 2):
                            router.rank(pe, i - 2, b_q)
                        if g == 2 and not first:
                            attend(i - 1, 1, 1)
                        if g == 3 and not first:
                            out_projection(i - 1)
                        if g == 3 and not last:
                            if has(i, 2):
                                pe.wait_ge(router.rank_read, i - 1)
                                pe.sem_inc(marker, 1)
                            project_q(i + 1)
                        if g == 4 and not last:
                            pe.wait_ge(v_ready, 2 * (i + 1))
                            pe.sem_inc(marker, 1)
                            project_k(i + 1)
                        if g == 5:
                            if not first:
                                pe.wait_ge(y_ready, 3 * i)
                                pe.sem_inc(marker, 1)
                            attend(i, 0, 0)
                        if g == 6 and has(i, 1):
                            if not last:
                                pe.wait_ge(q_ready, i + 2)
                                pe.sem_inc(marker, 1)
                            router.transposes(pe, i - 1, b_q)
                        if g == 6:
                            attend(i, 0, 1)

                transposes(0)
                project_q(0)
                project_k(0)
                for g in range(2):
                    score_group(0, g, g)
                loop(pe, body)
                prob_transposes(GROUPS - 2, GROUPS * PAIRS - 2)
                router.project(pe, PAIRS - 2, b_q)
                prob_transposes(GROUPS - 1, GROUPS * PAIRS - 1)
                pe.wait_ge(o_ready, 4 * PAIRS - 2)
                pe.sem_inc(marker, 1)
                attend(PAIRS - 1, 1, 0)
                router.rank(pe, PAIRS - 2, b_q)
                attend(PAIRS - 1, 1, 1)
                out_projection(PAIRS - 1)

            @block.scalar
            def _(act):
                def normalize(n, first):
                    if not first:
                        act.wait_ge(xT_done, n)
                    for u in range(2):
                        b = 2 * n + u
                        act.activation(xh_t[:, u, :], h_text[:, b, :], ACT.Identity, bias=nbias_t[:, b:b + 1] if isinstance(b, int) else nbias_t[:, bass.ds(b, 1)],
                                       scale=rstd_t[:, b:b + 1] if isinstance(b, int) else rstd_t[:, bass.ds(b, 1)]).then_inc(xh_ready, 1)
                        act.activation(xh_p[:, u, :], h_patch[:, b, :], ACT.Identity, bias=nbias_p[:, b:b + 1] if isinstance(b, int) else nbias_p[:, bass.ds(b, 1)],
                                       scale=rstd_p[:, b:b + 1] if isinstance(b, int) else rstd_p[:, bass.ds(b, 1)]).then_inc(xh_ready, 1)

                def take_xT(n):
                    act.wait_ge(xT_done, n + 1)
                    if not isinstance(n, int) or n > 0:
                        act.wait_ge(v_done, n)
                    act.activation(x_T[:, :, :], b_x[:, 0:2 * L].rearrange("p (u l) -> p u l", u=2), ACT.Copy).then_inc(xT_ready, 1)

                def take_q(n):
                    act.wait_ge(q_done, n + 1)
                    if not isinstance(n, int) or n > 0:
                        act.wait_ge(qe_ready, 2 * n)
                    act.activation(q_T[:, :, :], b_q[:, 0:2 * L].rearrange("p (u l) -> p u l", u=2), ACT.Identity,
                                   bias=bq[:, 0:1]).then_inc(q_ready, 1)

                def take_k(n, u, G):
                    if u == 0:
                        act.wait_ge(k_done, n + 1)
                    act.wait_ge(s_done, G)
                    act.activation(k_T[:, u, :], b_k[:, u * L:(u + 1) * L], ACT.Identity, bias=bk[:, 0:1]).then_inc(k_ready, 1)

                def take_v(n):
                    act.wait_ge(v_done, n + 1)
                    if not isinstance(n, int) or n > 0:
                        act.wait_ge(o_done, 2 * n)
                    for t, (dst, rows_) in enumerate(((v_t, P), (v_p, NP_))):
                        flat = dst[:, :, :, :].rearrange("p u h d -> p u (h d)")
                        for u in range(2):
                            diag = bass.AP(tensor=flat.tensor, offset=flat[:, u, :].offset,
                                           ap=[flat.ap[0], [D + E, H], [1, E]])
                            ins = act.activation(diag, b_v[0:rows_, 2 * t + u, :].rearrange("p (h e) -> p h e", h=H), ACT.Copy)
                        ins.then_inc(v_ready, 1)

                def take_o(i, u):
                    src = b_x[:, 0:L]
                    act.wait_ge(o_done, 2 * i + u + 1)
                    if u == 0 and not (isinstance(i, int) and i == 0):
                        act.wait_ge(y_done, i)
                    act.activation(oT_t[:, u, :], src[:, NP_:L], ACT.Identity, bias=bv[:, 0:1]).then_inc(o_ready, 1)
                    act.activation(oT_p[:, u * NP_:(u + 1) * NP_], src[:, 0:NP_], ACT.Identity, bias=bv[:, 0:1]).then_inc(o_ready, 1)

                def take_y(i):
                    act.wait_ge(y_done, i + 1)
                    for u in range(2):
                        act.activation(h_text[:, 2 * i + u, :], b_x[:, u * D:(u + 1) * D], ACT.Copy).then_inc(y_ready, 1)
                    act.activation(h2_patch[:, i, :], b_x[0:2 * NP_, 2 * D:3 * D], ACT.Copy).then_inc(y_ready, 1)

                def copy_scores(i, g, G):
                    act.wait_ge(s_done, G + 1)
                    if not (isinstance(G, int) and G < 3):
                        act.wait_ge(w_ready, 3 * (G - 2))
                    act.activation(scores[:, slot(g), :, :], b_scores[s_bank(g)][:, 0:GT * L].rearrange("p (t l) -> p t l", t=GT),
                                   ACT.Copy).then_inc(s_ready, 1)

                def exp_all(g, G):
                    act.wait_ge(nm_ready, G + 1)
                    if not (isinstance(G, int) and G < 3):
                        act.wait_ge(pt_done, G - 2)
                    for t in range(GT):
                        act.activation(e_all[:, slot(g), t, :], b_scores[s_bank(g)][:, t * L:(t + 1) * L], ACT.Exp,
                                       bias=neg_max[:, slot(g), t:t + 1],
                                       accum_out=sum_all[:, slot(g), t:t + 1]).then_inc(ea_ready, 1)

                def exp_rest(g, G):
                    for t in range(GT):
                        act.wait_ge(w_ready, 3 * G + t + 1)
                        act.activation(work[:, slot(g), t, :], work[:, slot(g), t, :], ACT.Exp,
                                       bias=neg_max[:, slot(g), t:t + 1],
                                       accum_out=sum_rest[:, slot(g), t:t + 1]).then_inc(er_ready, 1)

                def take_pt(i, g, G):
                    act.wait_ge(pt_done, G + 1)
                    if g in (0, 3) and not (isinstance(i, int) and i == 0):
                        act.wait_ge(o_done, 2 * i - (1 if g == 0 else 0))
                    lo = GT * g * P
                    act.activation(pT_t[:, lo:lo + GT * P], b_ptt[:, :, :].rearrange("p t r -> p (t r)"), ACT.Copy).then_inc(pt_ready, 1)
                    act.activation(pT_p[:, lo:lo + GT * P], b_ptp[0:NP_, :, :].rearrange("p t r -> p (t r)"), ACT.Copy).then_inc(pt_ready, 1)

                def body(i, first, last):
                    for g in range(GROUPS):
                        G = GROUPS * i + g
                        if g == 0 and not last:
                            normalize(i + 1, False)
                        if not (first and g == 0):
                            exp_rest((g - 1) % GROUPS, G - 1)
                        exp_all(g, G)
                        if not (first and g < 2):
                            take_pt(i if g >= 2 else i - 1, (g - 2) % GROUPS, G - 2)
                        if g + 2 < GROUPS:
                            copy_scores(i, g + 2, G + 2)
                        elif not last:
                            copy_scores(i + 1, g + 2 - GROUPS, G + 2)
                        if g == 0 and not last:
                            take_xT(i + 1)
                        if g == 2 and not first:
                            take_o(i - 1, 1)
                        if g == 2:
                            take_v(i)
                        if g == 3:
                            if not first:
                                take_y(i - 1)
                            if not last:
                                take_q(i + 1)
                        if g == 4 and not last:
                            take_k(i + 1, 0, GROUPS * i + 4)
                        if g == 5 and not last:
                            take_k(i + 1, 1, GROUPS * i + 7)
                        if g == 5 and has(i, 1):
                            router.normalize(act, i - 1)
                        if g == 6:
                            take_o(i, 0)
                        if g == 6 and has(i, 1):
                            router.take_xT(act, i - 1, b_q)
                        if g == 0 and has(i, 2):
                            router.take_logits(act, i - 2, b_q)
                        if g == 1 and has(i, 2):
                            router.exponentials(act, i - 2)
                        if g == 2 and has(i, 2):
                            router.record(act, i - 2)

                normalize(0, True)
                take_xT(0)
                take_q(0)
                act.wait_ge(k_done, 1)
                for u in range(2):
                    act.activation(k_T[:, u, :], b_k[:, u * L:(u + 1) * L], ACT.Identity, bias=bk[:, 0:1]).then_inc(k_ready, 1)
                for g in range(2):
                    copy_scores(0, g, g)
                loop(act, body)
                exp_rest(GROUPS - 1, GROUPS * PAIRS - 1)
                take_pt(PAIRS - 1, GROUPS - 2, GROUPS * PAIRS - 2)
                router.take_logits(act, PAIRS - 2, b_q)
                router.exponentials(act, PAIRS - 2)
                take_pt(PAIRS - 1, GROUPS - 1, GROUPS * PAIRS - 1)
                take_o(PAIRS - 1, 1)
                take_y(PAIRS - 1)
                router.record(act, PAIRS - 2)

            @block.gpsimd
            def _(po):
                po.memset(minus_one[:, :], -1.0).then_inc(zeroed, 1)
                po.wait_ge(zeroed, 1)

                def spread(n, u):
                    if u == 0:
                        po.wait_ge(q_ready, n + 1)
                        if not isinstance(n, int) or n > 0:
                            po.sem_inc(marker, 1)
                    if not isinstance(n, int) or n > 0:
                        po.wait_ge(s_done, GROUPS * n - (3 if u == 0 else 0))
                    po.tensor_tensor(q_exp[:, u, :, :],
                                     q_T[:, u, :].rearrange("p (a l) -> p a l", a=1).broadcast_to([P, H, L]),
                                     head_mask[:, :].rearrange("p (h a) -> p h a", a=1).broadcast_to([P, H, L]),
                                     ALU.mult).then_inc(qe_ready, 1)

                def probabilities(g, G):
                    po.wait_ge(er_ready, 3 * (G + 1))
                    po.tensor_tensor(inv[:, slot(g), :], sum_all[:, slot(g), :], sum_rest[:, slot(g), :], ALU.subtract).then_inc(sum_ready, 1)
                    po.tensor_tensor(e_all[:, slot(g), :, :], e_all[:, slot(g), :, :], work[:, slot(g), :, :],
                                     ALU.subtract).then_inc(diff_ready, 1)
                    po.wait_ge(sum_ready, G + 1)
                    po.tensor_tensor(inv[:, slot(g), :], inv[:, slot(g), :], minus_one[:, :], ALU.pow).then_inc(inv_ready, 1)
                    po.wait_ge(inv_ready, G + 1)
                    po.sem_inc(marker, 1)
                    po.wait_ge(diff_ready, G + 1)
                    po.tensor_tensor(e_all[:, slot(g), :, :], e_all[:, slot(g), :, :],
                                     inv[:, slot(g), :].rearrange("p (t a) -> p t a", a=1).broadcast_to([P, GT, L]),
                                     ALU.mult).then_inc(p_ready, 1)

                def body(i, first, last):
                    for g in range(GROUPS):
                        G = GROUPS * i + g
                        if g == 4 and not last:
                            spread(i + 1, 0)
                        if g == 5 and has(i, 1):
                            router.deviation(po, i - 1)
                        if g == 6 and not last:
                            spread(i + 1, 1)
                        if not (first and g == 0):
                            probabilities((g - 1) % GROUPS, G - 1)
                        if g == 6 and has(i, 1):
                            router.add_base(po, i - 1)
                        if g >= 3 and has(i, 2):
                            router.scatter(po, i - 2, sum(SHARE[3:g]), sum(SHARE[3:g + 1]))
                        if g < 2 and has(i, 3):
                            router.scatter(po, i - 3, SCATTERED + sum(SHARE[:g]), SCATTERED + sum(SHARE[:g + 1]))

                spread(0, 0)
                spread(0, 1)
                loop(po, body)
                probabilities(GROUPS - 1, GROUPS * PAIRS - 1)
                router.scatter(po, PAIRS - 3, SCATTERED, 3 * KE)

            @block.vector
            def _(ve):
                def body(i, first, last):
                    link = Chain(ve, chain)
                    ve.sem_clear(chain)
                    for g in range(GROUPS):
                        G = GROUPS * i + g
                        s = slot(g)
                        ve.wait_ge(s_ready, G + 1)
                        ve.sem_inc(marker, 1)
                        if not (isinstance(G, int) and G < 3):
                            ve.wait_ge(diff_ready, G - 2)
                            ve.sem_inc(marker, 1)
                        seen = [link(ve.max(top[:, s, t, :], scores[:, s, t, :])) for t in range(GT)]
                        for t in range(GT):
                            ve.wait_ge(chain, seen[t])
                            seen[t] = link(ve.match_replace(work[:, s, t, :], top[:, s, t, :], scores[:, s, t, :], MARK))
                        ve.tensor_scalar(neg_max[:, s, :], top[:, s, :, 0], -1.0, None, ALU.mult).then_inc(nm_ready, 1)
                        for rnd in range(2):
                            for t in range(GT):
                                ve.wait_ge(chain, seen[t])
                                seen[t] = link(ve.max(topw[:, t, :], work[:, s, t, :]))
                            for t in range(GT):
                                ve.wait_ge(chain, seen[t])
                                seen[t] = link(ve.match_replace(work[:, s, t, :], topw[:, t, :], work[:, s, t, :], MARK))
                        for t in range(GT):
                            ve.wait_ge(chain, seen[t])
                            seen[t] = link(ve.max(topw[:, t, :], work[:, s, t, :]))
                        if g == 1 and has(i, 2):
                            if isinstance(i, int):
                                ve.wait_ge(r_in, 80)
                                ve.sem_inc(marker, 1)
                            router.choose(ve, i - 2, link)
                        if g == 4 and has(i, 1):
                            ve.wait_ge(y_ready, 3 * i)
                            ve.sem_inc(marker, 1)
                            router.statistics(ve, i - 1, link)
                        if g == 2 and has(i, 2):
                            router.gates(ve, i - 2, link)
                            router.places(ve, i - 2, link, b_q)
                        ve.wait_ge(chain, seen[GT - 1])
                        n = link(ve.memset(topw[:, :, 1:8], MARK))
                        for t in range(GT):
                            ve.wait_ge(chain, n)
                            ve.match_replace(work[:, s, t, :], topw[:, t, :], work[:, s, t, :], MARK).then_inc(w_ready, 1)
                    link.settle()
                    ve.wait_ge(w_ready, 3 * (GROUPS * (i + 1)))
                    ve.sem_inc(marker, 1)

                loop(ve, body)
                link = Chain(ve, chain)
                ve.sem_clear(chain)
                router.choose(ve, PAIRS - 2, link)
                router.gates(ve, PAIRS - 2, link)
                router.places(ve, PAIRS - 2, link, b_q)


class Chain:

    def __init__(self, ve, sem):
        self.ve, self.sem, self.n = ve, sem, 0

    def __call__(self, ins):
        self.n += 1
        ins.then_inc(self.sem, 1)
        return self.n

    def settle(self):
        self.ve.wait_ge(self.sem, self.n)


PARTS = ((0, P), (1, P), (2, T2))


class Router:

    def __init__(self, nc, sb, sem, v):
        self.nc = nc
        self.ident, self.ones, self.h_text, self.h2_patch = v["ident"], v["ones"], v["h_text"], v["h2_patch"]
        self.wr, self.tri, self.ones_sq, self.codes = v["wr"], v["tri"], v["ones_sq"], v["codes"]
        self.base, self.xT_all, self.carry, self.dispatch = v["base"], v["xT_all"], v["carry"], v["dispatch"]
        self.minus_half = sb("minus_half", [P, 3])
        self.minus_one = sb("minus_one2", [P, 3])
        self.stats = sb("stats", [P, 3, 6])
        self.mv = sb("mv", [P, 3, 2])
        self.rstd = sb("rstd", [P, 3])
        self.nbias = sb("nbias", [P, 3])
        self.xn = sb("xn", [P, 3, D])
        self.rec = sb("rec", [P, 3, REC])
        self.xT = sb("xT", [P, PT])
        self.logits = sb("logits", [P, 3, NE + 2])
        self.taken = sb("taken", [P, 3, NE + 2])
        self.mask = sb("mask", [P, 3, NE])
        self.best = sb("best", [P, 3, 8])
        self.neg_max = sb("neg_max2", [P, 3])
        self.ex = sb("ex", [P, 3, NE])
        self.inv = sb("inv2", [P, 3])
        self.ranks = sb("ranks", [P, 3, NE])
        self.rows_f = sb("rows_f", [P, 3, 8])
        self.rows_i = sb("rows_i", [P, 3, 8], I32)
        self.marker = sem("marker2")
        self.set0 = sem("set2")
        self.mv_ready = sem("mv_ready")
        self.rstd_ready = sem("rstd_ready")
        self.neg_ready = sem("neg_ready")
        self.nb_ready = sem("nb_ready")
        self.xn_ready = sem("xn_ready")
        self.base_ready = sem("base_ready")
        self.xT_done = sem("xT_done2")
        self.xT_ready = sem("xT_ready2")
        self.lg_done = sem("lg_done")
        self.lg_ready = sem("lg_ready")
        self.nm_ready = sem("nm_ready2")
        self.mask_ready = sem("mask_ready")
        self.ex_ready = sem("ex_ready")
        self.rank_done = sem("rank_done")
        self.rank_read = sem("rank_read")
        self.gate_ready = sem("gate_ready")
        self.rec_ready = sem("rec_ready")
        self.idx_ready = sem("idx_ready")
        self.sent = sem("sent")

    def source(self, n, t):
        return self.h_text[:, 2 * n + t, :] if t < 2 else self.h2_patch[:, n, :]

    def constants(self, po):
        for t, value in ((self.minus_half, -0.5), (self.minus_one, -1.0), (self.mv, 1.0), (self.logits, SENT), (self.mask, 0.0), (self.ex, 1.0),
                         (self.best, 0.0), (self.xn, 0.0), (self.rec, 0.0)):
            po.memset(t.ap(), value).then_inc(self.set0, 1)

    def deviation(self, po, n):
        po.wait_ge(self.mv_ready, n + 1)
        po.sem_inc(self.marker, 1)
        po.tensor_scalar(self.rstd[:, :], self.mv[:, :, 1], EPS, None, ALU.add).then_inc(self.rstd_ready, 1)
        po.wait_ge(self.rstd_ready, 2 * n + 1)
        po.tensor_tensor(self.rstd[:, :], self.rstd[:, :], self.minus_half[:, :], ALU.pow).then_inc(self.rstd_ready, 1)
        po.tensor_tensor(self.nbias[:, :], self.mv[:, :, 0], self.minus_one[:, :], ALU.mult).then_inc(self.neg_ready, 1)
        po.wait_ge(self.neg_ready, n + 1)
        po.sem_inc(self.marker, 1)
        po.wait_ge(self.rstd_ready, 2 * (n + 1))
        po.tensor_tensor(self.nbias[:, :], self.nbias[:, :], self.rstd[:, :], ALU.mult).then_inc(self.nb_ready, 1)

    def add_base(self, po, n):
        po.wait_ge(self.xn_ready, 3 * (n + 1))
        po.sem_inc(self.marker, 1)
        for t, m in PARTS:
            po.tensor_tensor(self.base[0:m, 3 * n + t, :], self.source(n, t), self.xn[0:m, t, :], ALU.add).then_inc(self.base_ready, 1)

    def scatter(self, po, n, lo, hi):
        if lo == 0:
            po.wait_ge(self.idx_ready, n + 1)
            po.sem_inc(self.marker, 1)
            po.wait_ge(self.gate_ready, n + 1)
            po.sem_inc(self.marker, 1)
            po.wait_ge(self.rec_ready, n + 1)
            po.sem_inc(self.marker, 1)
        for t, m in PARTS:
            for k in range(KE):
                if lo <= KE * t + k < hi:
                    po.indirect_dma_start(self.dispatch, bass.IndirectOffsetOnAxis(self.rows_i[0:m, t, k:k + 1], 0),
                                          self.rec[0:m, t, :], None).then_inc(self.sent, 16)

    def normalize(self, act, n):
        act.wait_ge(self.nb_ready, n + 1)
        act.sem_inc(self.marker, 1)
        if not (isinstance(n, int) and n == 0):
            act.wait_ge(self.base_ready, 3 * n)
            act.sem_inc(self.marker, 1)
            act.wait_ge(self.rec_ready, n)
            act.sem_inc(self.marker, 1)
        for t, m in PARTS:
            act.activation(self.xn[0:m, t, :], self.source(n, t), ACT.Identity, bias=self.nbias[0:m, t:t + 1],
                           scale=self.rstd[0:m, t:t + 1]).then_inc(self.xn_ready, 1)

    def take_xT(self, act, n, bank):
        act.wait_ge(self.xT_done, n + 1)
        act.activation(self.xT[:, :], bank[:, 0:PT], ACT.Copy).then_inc(self.xT_ready, 1)
        act.activation(self.xT_all[:, n * PT:(n + 1) * PT] if isinstance(n, int) else self.xT_all[:, bass.ds(n * PT, PT)],
                       bank[:, 0:PT], ACT.Copy).then_inc(self.xT_ready, 1)

    def take_logits(self, act, n, bank):
        act.wait_ge(self.lg_done, n + 1)
        for lo, hi, m in ((0, 2, P), (2, 3, T2)):
            act.activation(self.logits[0:m, lo:hi, 0:NE], bank[0:m, lo * NE:hi * NE].rearrange("p (t e) -> p t e", e=NE),
                           ACT.Copy).then_inc(self.lg_ready, 1)

    def exponentials(self, act, n):
        act.wait_ge(self.nm_ready, n + 1)
        for t, m in PARTS:
            act.activation(self.ex[0:m, t, :], self.logits[0:m, t, 0:NE], ACT.Exp,
                           bias=self.neg_max[0:m, t:t + 1]).then_inc(self.ex_ready, 1)

    def record(self, act, n):
        if not (isinstance(n, int) and n == 0):
            act.wait_ge(self.sent, 16 * 3 * KE * n)
        act.activation(self.rec[:, :, 0:D], self.xn[:, :, :], ACT.Copy).then_inc(self.rec_ready, 1)

    def transposes(self, pe, n, bank):
        pe.wait_ge(self.xn_ready, 3 * (n + 1))
        pe.sem_inc(self.marker, 1)
        at = 0
        for t, m in PARTS:
            last = pe.transpose(bank[:, at:at + m], self.xn[0:m, t, :], self.ident[0:m, 0:m])
            at += m
        last.then_inc(self.xT_done, 1)

    def project(self, pe, n, bank):
        pe.wait_ge(self.xT_ready, 2 * (n + 1))
        pe.sem_inc(self.marker, 1)
        at = 0
        for t, m in PARTS:
            last = pe.matmul(bank[0:m, t * NE:(t + 1) * NE], self.xT[:, at:at + m], self.wr[:, :], start=True, stop=True)
            at += m
        last.then_inc(self.lg_done, 1)

    def rank(self, pe, n, bank):
        pe.wait_ge(self.mask_ready, n + 1)
        pe.sem_inc(self.marker, 1)
        o = bank[:, 3 * NE:6 * NE]
        pe.matmul(o, self.ones_sq[:, :], self.carry[:, :, :].rearrange("p t e -> p (t e)"), start=True, stop=False)
        last = pe.matmul(o, self.tri[:, :], self.mask[:, :, :].rearrange("p t e -> p (t e)"), start=False, stop=True)
        last.then_inc(self.rank_done, 1)

    def statistics(self, ve, n, then):
        for t, m in PARTS:
            then(ve.bn_stats(self.stats[0:m, t, :], self.source(n, t)))
        then.settle()
        for t, m in PARTS:
            then(ve.bn_aggr(self.mv[0:m, t, :], self.stats[0:m, t, :]))
        then.settle()
        ve.sem_inc(self.mv_ready, 1)

    def choose(self, ve, n, then):
        best, logits, taken, mask = self.best, self.logits, self.taken, self.mask
        ve.wait_ge(self.lg_ready, 2 * (n + 1))
        ve.sem_inc(self.marker, 1)
        for t, m in PARTS:
            then(ve.max(best[0:m, t, :], logits[0:m, t, 0:NE]))
        then.settle()
        ve.tensor_scalar(self.neg_max[:, :], best[:, :, 0], -1.0, None, ALU.mult).then_inc(self.nm_ready, 1)
        then(ve.memset(best[:, :, KE:8], SENT))
        then.settle()
        for t, m in PARTS:
            then(ve.match_replace(taken[0:m, t, :], best[0:m, t, :], logits[0:m, t, :], MARK))
        then.settle()
        for lo, hi, m in ((0, 2, P), (2, 3, T2)):
            then(ve.tensor_scalar(mask[0:m, lo:hi, :], taken[0:m, lo:hi, 0:NE], MARK, None, ALU.is_equal))
        then.settle()
        for t in range(2):
            then(ve.tensor_tensor(self.carry[:, t + 1, :], self.carry[:, t, :], mask[:, t, :], ALU.add))
            then.settle()
        ve.sem_inc(self.mask_ready, 1)

    def gates(self, ve, n, then):
        ex, mask, inv, rec = self.ex, self.mask, self.inv, self.rec
        ve.wait_ge(self.ex_ready, 3 * (n + 1))
        then(ve.tensor_tensor(ex[:, :, :], ex[:, :, :], mask[:, :, :], ALU.mult))
        then.settle()
        then(ve.tensor_reduce(inv[:, :], ex[:, :, :], AX.X, ALU.add))
        then.settle()
        then(ve.reciprocal(inv[0:P, 0:2], inv[0:P, 0:2]))
        then(ve.reciprocal(inv[0:T2, 2:3], inv[0:T2, 2:3]))
        then.settle()
        then(ve.tensor_tensor(ex[:, :, :], ex[:, :, :], inv[:, :].rearrange("p (t a) -> p t a", a=1).broadcast_to([P, 3, NE]),
                              ALU.mult))

    def places(self, ve, n, then, bank):
        mask, carry, ranks = self.mask, self.carry, self.ranks
        ve.wait_ge(self.rank_done, n + 1)
        for t, m in PARTS:
            then(ve.tensor_tensor(ranks[0:m, t, :], bank[0:m, (3 + t) * NE:(4 + t) * NE], mask[0:m, t, :], ALU.mult))
        then.settle()
        ve.sem_inc(self.rank_read, 1)
        then(ve.tensor_tensor(carry[:, 0, :], carry[:, 2, :], mask[:, 2, :], ALU.add))
        for t, m in PARTS:
            then(ve.max(self.rows_f[0:m, t, :], ranks[0:m, t, :]))
        then.settle()
        if not (isinstance(n, int) and n == 0):
            ve.wait_ge(self.sent, 16 * 3 * KE * n)
            ve.sem_inc(self.marker, 1)
        ve.scalar_tensor_tensor(out=self.rec[:, :, D:D + NE], in0=mask[:, :, :], scalar=-1.0, in1=self.ex[:, :, :],
                                op0=ALU.add, op1=ALU.add).then_inc(self.gate_ready, 1)
        then(ve.tensor_copy(self.rec[:, :, D + NE], self.codes[:, 3 * n:3 * n + 3] if isinstance(n, int)
                            else self.codes[:, bass.ds(3 * n, 3)]))
        for lo, hi, m in ((0, 2, P), (2, 3, T2)):
            then(ve.tensor_scalar(self.rows_i[0:m, lo:hi, :], self.rows_f[0:m, lo:hi, :], -1.0, None, ALU.add))
        then.settle()
        ve.sem_inc(self.idx_ready, 1)


class Shared:

    def __init__(self, nc, sb, bank, where, v, suffix, first):
        self.w_gu, self.w_d, self.base, self.xT_all = v["w_gu"], v["w_d"], v["base"], v["xT_all"]
        self.first = first
        self.act_g = sb("act_g5" + suffix, [P, NS, PT], F32, where)
        self.hT = sb("hT5" + suffix, [P, NS, PT], F32, where)
        self.b_g = [bank(f"b_g{e}" + suffix, [P, 512], where) for e in range(NS)]
        self.b_u = [bank(f"b_u{e}" + suffix, [P, 512], where) for e in range(NS)]
        self.b_y = bank("b_y5" + suffix, [P, 3, D], where)
        names = ("gu_done", "silu_ready", "h_ready", "y_done", "added")
        self.gu_done, self.silu_ready, self.h_ready, self.y_done, self.added = (
            where.enter_context(nc.semaphore(n + "5" + suffix)) for n in names)

    def products(self, pe, n):
        k = n - self.first
        x = self.xT_all[:, n * PT:(n + 1) * PT]
        if k > 0:
            pe.wait_ge(self.h_ready, 2 * k)
        for e in range(NS):
            pe.matmul(self.b_g[e][:, 0:PT], self.w_gu[:, NE + e, 0:D], x, start=True, stop=True)
            pe.matmul(self.b_u[e][:, 0:PT], self.w_gu[:, NE + e, D:2 * D], x, start=True, stop=True).then_inc(self.gu_done, 1)
        if k > 0:
            pe.wait_ge(self.added, 2 * k)
        pe.wait_ge(self.h_ready, 2 * (k + 1))
        for t, r in PARTS:
            for e in range(NS):
                last = pe.matmul(self.b_y[0:r, t, :], self.hT[:, e, t * P:t * P + r], self.w_d[:, NE + e, :],
                                 start=(e == 0), stop=(e == NS - 1))
        last.then_inc(self.y_done, 1)

    def silu(self, act, n):
        k = n - self.first
        for e in range(NS):
            act.wait_ge(self.gu_done, 2 * k + e + 1)
            act.activation(self.act_g[:, e, :], self.b_g[e][:, 0:PT], ACT.Silu).then_inc(self.silu_ready, 1)

    def hidden(self, ve, n):
        k = n - self.first
        for e in range(NS):
            ve.wait_ge(self.silu_ready, 2 * k + e + 1)
            if e == 0 and k > 0:
                ve.wait_ge(self.y_done, k)
            ve.tensor_tensor(self.hT[:, e, :], self.act_g[:, e, :], self.b_u[e][:, 0:PT], ALU.mult).then_inc(self.h_ready, 1)

    def add(self, ve, n):
        ve.wait_ge(self.y_done, n - self.first + 1)
        for lo, hi, m in ((0, 2, P), (2, 3, T2)):
            o = self.base[0:m, 3 * n + lo:3 * n + hi, :]
            ve.tensor_tensor(o, o, self.b_y[0:m, lo:hi, :], ALU.add).then_inc(self.added, 1)


def plan(nc, es, sb, bank, a, v):
    carry, table, aside = v["carry"], v["table"], v["aside"]
    ident, ones_sq, router = v["ident"], v["ones_sq"], v["router"]
    with ExitStack() as local:
        def lsb(name, shape, dt=F32):
            return sb(name, shape, dt, local)

        def sem(name):
            return local.enter_context(nc.semaphore(name))

        regions = lsb("regions", [P, NE])
        names = lsb("names", [P, NE])
        steps = lsb("steps", [P, 21])
        tile_no = lsb("tile_no", [P, 2])
        counts = lsb("counts", [P, NE])
        over = lsb("over", [P, NE, 21])
        n_tiles = lsb("n_tiles", [P, NE])
        ends = lsb("ends", [P, NE])
        one = lsb("one_row", [P, NE])
        past = lsb("past", [P, 2, NE])
        mine = lsb("mine", [P, 2, NE])
        expert = lsb("expert", [P, 2])
        begin = lsb("begin", [P, 2])
        rows_of = lsb("rows_of", [P, 2])
        row = lsb("row", [P, 2])
        skip = lsb("skip", [P, 2])
        by_itself = lsb("by_itself", [P, 2, P])
        spare = lsb("spare", [P, 2 * P])
        part_no = lsb("part_no", [P, 1])
        b_route = bank("b_route", [P, 512], local)
        b_cnt = bank("b_cnt", [P, 512], local)
        b_skip = b_cnt[:, 0:2 * P].rearrange("p (j t) -> p j t", j=2)
        shared = Shared(nc, sb, bank, local, v, "", 0)
        b_tab = bank("b_tab", [P, 4, P], local)
        c_in, set0, dve, cnt_done, cols_ready, tab_done = (sem(n) for n in ("c_in3", "set0", "dve3", "cnt_done", "cols_ready", "tab_done"))
        skip_done = sem("skip_done")
        n = PAIRS - 1
        with nc.Block() as block:
            @block.sync
            def _(sp):
                for lo in range(NE + NS - 11, -1, -11):
                    sp.dma_start(v["w_d"][:, lo:lo + 11, :], a["w_d"][:, lo:lo + 11, :]).then_inc(
                        v["wd_in"] if lo < NE - 11 else v["shared_in"], 16)
                for t, n in ((regions, "region_all"), (names, "names"), (steps, "steps"), (tile_no, "tile_no"),
                             (spare, "spare"), (part_no, "part_no")):
                    sp.dma_start(t[:, :], a[n]).then_inc(c_in, 16)

            @block.gpsimd
            def _(po):
                po.memset(one[:, :], 1.0).then_inc(set0, 1)
                router.deviation(po, n)
                router.scatter(po, n - 1, 0, 3 * KE)
                router.add_base(po, n)
                router.scatter(po, n, 0, 3 * KE)
                po.wait_ge(router.sent, 16 * 3 * KE * PAIRS)

            @block.scalar
            def _(act):
                router.normalize(act, n)
                router.take_xT(act, n, b_route)
                router.take_logits(act, n, b_route)
                router.exponentials(act, n)
                for k in range(EARLY - 1):
                    shared.silu(act, k)
                router.record(act, n)
                shared.silu(act, EARLY - 1)

            @block.tensor
            def _(pe):
                router.transposes(pe, n, b_route)
                router.project(pe, n, b_route)
                router.rank(pe, n, b_route)
                pe.wait_ge(v["shared_in"], 16)
                pe.wait_ge(v["weights_in"], 96)
                for k in range(EARLY - 1):
                    shared.products(pe, k)
                pe.wait_ge(router.idx_ready, PAIRS)
                pe.matmul(b_cnt[:, 0:NE], ones_sq[:, :], carry[:, 0, :], start=True, stop=True).then_inc(cnt_done, 1)
                pe.wait_ge(cols_ready, 1)
                for j in range(2):
                    pe.matmul(b_tab[0:1, j, :], row[:, j:j + 1], ident[:, :], start=True, stop=True)
                    last = pe.matmul(b_tab[0:1, 2 + j, :], expert[:, j:j + 1], ident[:, :], start=True, stop=True)
                last.then_inc(tab_done, 1)
                pe.matmul(b_skip[:, :, :].rearrange("p j t -> p (j t)"), ones_sq[:, :],
                          by_itself[:, :, :].rearrange("p j t -> p (j t)"), start=True, stop=True).then_inc(skip_done, 1)
                shared.products(pe, EARLY - 1)

            @block.vector
            def _(ve):
                then = Chain(ve, dve)

                def step(ins):
                    then(ins)
                    then.settle()

                def by_tile(t):
                    return t[:, :].rearrange("p (a e) -> p a e", a=1).broadcast_to([P, 2, NE])

                def by_expert(t):
                    return t[:, :].rearrange("p (j a) -> p j a", a=1).broadcast_to([P, 2, NE])

                router.statistics(ve, n, then)
                router.choose(ve, n, then)
                router.gates(ve, n, then)
                for k in range(EARLY - 1):
                    shared.hidden(ve, k)
                    shared.add(ve, k)
                router.places(ve, n, then, b_route)
                ve.wait_ge(c_in, 96)
                ve.wait_ge(set0, 1)
                ve.wait_ge(cnt_done, 1)
                step(ve.tensor_tensor(counts[:, :], b_cnt[:, 0:NE], regions[:, :], ALU.subtract))
                step(ve.tensor_scalar(counts[:, :], counts[:, :], float(-P - 1), None, ALU.add))
                step(ve.tensor_tensor(over[:, :, :], counts[:, :].rearrange("p (e a) -> p e a", a=1).broadcast_to([P, NE, 21]),
                                      steps[:, :].rearrange("p (a k) -> p a k", a=1).broadcast_to([P, NE, 21]), ALU.is_gt))
                step(ve.tensor_reduce(n_tiles[:, :], over[:, :, :], AX.X, ALU.add))
                step(ve.tensor_tensor_scan(ends[:, :], one[:, :], n_tiles[:, :], 0.0, ALU.mult, ALU.add))
                step(ve.tensor_tensor(past[:, :, :], by_expert(tile_no), by_tile(ends), ALU.is_ge))
                step(ve.tensor_reduce(expert[:, :], past[:, :, :], AX.X, ALU.add))
                step(ve.tensor_tensor(past[:, :, :], past[:, :, :], by_tile(n_tiles), ALU.mult))
                step(ve.tensor_reduce(begin[:, :], past[:, :, :], AX.X, ALU.add))
                step(ve.tensor_tensor(mine[:, :, :], by_expert(expert), by_tile(names), ALU.is_equal))
                step(ve.tensor_tensor(past[:, :, :], mine[:, :, :], by_tile(counts), ALU.mult))
                step(ve.tensor_reduce(rows_of[:, :], past[:, :, :], AX.X, ALU.add))
                step(ve.tensor_tensor(past[:, :, :], mine[:, :, :], by_tile(regions), ALU.mult))
                step(ve.tensor_tensor(row[:, :], tile_no[:, :], begin[:, :], ALU.subtract))
                step(ve.tensor_scalar(row[:, :], row[:, :], float(P), float(P), ALU.mult, ALU.add))
                step(ve.tensor_copy(skip[:, :], row[:, :]))
                step(ve.tensor_tensor(row[:, :], row[:, :], rows_of[:, :], ALU.min))
                step(ve.tensor_tensor(skip[:, :], skip[:, :], row[:, :], ALU.subtract))
                for j in range(2):
                    step(ve.tensor_scalar(by_itself[:, j, :], ident[:, :], skip[:, j:j + 1], None, ALU.mult))
                step(ve.tensor_reduce(begin[:, :], past[:, :, :], AX.X, ALU.add))
                step(ve.tensor_tensor(row[:, :], row[:, :], begin[:, :], ALU.add))
                step(ve.tensor_scalar(expert[:, :], expert[:, :], float(NE - 1), None, ALU.min))
                ve.sem_inc(cols_ready, 1)
                ve.wait_ge(tab_done, 1)
                step(ve.tensor_copy(table[0:1, :, :], b_tab[0:1, :, :].rearrange("p (a j) t -> p a (j t)", a=2)))
                ve.wait_ge(skip_done, 1)
                step(ve.scalar_tensor_tensor(out=aside[:, :], in0=b_skip[:, :, :].rearrange("p j t -> p (j t)"),
                                             scalar=part_no[:, 0:1], in1=spare[:, :], op0=ALU.is_gt, op1=ALU.mult))
                shared.hidden(ve, EARLY - 1)
                shared.add(ve, EARLY - 1)


def experts(nc, es, sb, bank, a, v):
    ident, w_gu, w_d, weights_in = v["ident"], v["w_gu"], v["w_d"], v["weights_in"]
    table, dispatch, results, before = v["table"], v["dispatch"], v["results"], v["before"]
    aside = v["aside"]
    STEPS = ETILES // TS
    BODIES = -(-STEPS // SB)
    LAST = STEPS - SB * (BODIES - 1)
    assert STEPS * TS == ETILES and 3 <= LAST <= SB

    with ExitStack() as local:
        def lsb(name, shape, dt=F32):
            return sb(name, shape, dt, local)

        def sem(name):
            return local.enter_context(nc.semaphore(name))

        rec = lsb("rec4", [P, SB, TS, REC])
        xT = lsb("xT4", [P, SB, TS, P])
        w_now = lsb("w_now", [P, 3, TS, 2 * D])
        act_g = lsb("act_g", [P, SB, TS, P])
        hid = lsb("hid", [P, SB, TS, P])
        y = lsb("y4", [P, SB, TS, D])
        b_xT = [bank(f"b_xT4{j}", [P, TS, P], local) for j in range(2)]
        b_gu = [bank(f"b_gu{j}", [P, 2, TS, P], local) for j in range(3)]
        b_y = [bank(f"b_y{j}", [P, TS, D], local) for j in range(3)]
        chosen = lsb("chosen4", [P, SB, TS, NE])
        nth = lsb("nth", [P, SB, TS])
        dest = lsb("dest", [P, SB, TS], I32)
        marker = sem("marker4")
        rec_in = [sem(f"rec_in{j}") for j in range(SB)]
        xT_done = sem("xT_done4")
        xT_ready = sem("xT_ready4")
        w_ready = sem("w_ready4")
        gu_done = sem("gu_done")
        silu_ready = sem("silu_ready")
        hid_ready = sem("hid_ready")
        dest_ready = sem("dest_ready")
        dve = sem("dve4")
        y_done = sem("y_done4")
        y_ready = sem("y_ready4")
        stored = [sem(f"stored{j}") for j in range(SB)]

        def loop(eng, body):
            body(0, True, False)
            with eng.Fori(1, BODIES - 1) as i:
                body(i, False, False)
            body(BODIES - 1, False, True)

        def tile_values(engine, n, tile, count, hi):
            at = table[0:1, n, tile:tile + count] if isinstance(tile, int) else table[0:1, n, bass.ds(tile, count)]
            return nc.values_load_multi_w_load_instructions(
                at, engines=[engine], min_val=0, max_val=hi,
                skip_runtime_bounds_check_because="the table's entries are clamped when it is made")[1]

        with nc.Block() as block:
            @block.sync
            def _(sp):
                def load(i, first, last):
                    rows_ = tile_values(mybir.EngineType.SP, 0, TS * SB * i, TS * (LAST if last else SB), NE * CAP - P)
                    for j in range(LAST if last else SB):
                        if not first:
                            sp.wait_ge(dest_ready, SB * (i - 1) + j + 1)
                            sp.sem_inc(marker, 1)
                            sp.wait_ge(y_ready, 2 * (SB * (i - 1) + j + 1))
                            sp.sem_inc(marker, 1)
                        for t in range(TS):
                            sp.dma_start(rec[:, j, t, :], dispatch[bass.ds(rows_[TS * j + t], P), :]).then_inc(rec_in[j], 16)

                loop(sp, load)

            @block.gpsimd
            def _(po):
                def body(i, first, last):
                    for j in range(LAST if last else SB):
                        s = SB * i + j
                        po.wait_ge(y_ready, 2 * (s + 1))
                        po.sem_inc(marker, 1)
                        for t in range(TS):
                            po.indirect_dma_start(results, bass.IndirectOffsetOnAxis(dest[:, j, t:t + 1], 0),
                                                  y[:, j, t, :], None).then_inc(stored[j], 16)

                loop(po, body)
                for j in range(SB):
                    po.wait_ge(stored[j], 16 * TS * (BODIES if j < LAST else BODIES - 1))

            @block.tensor
            def _(pe):
                pe.wait_ge(v["wd_in"], 16 * 5)

                def transposes(j, i, s):
                    pe.wait_ge(rec_in[j], 16 * TS * (i + 1))
                    pe.sem_inc(marker, 1)
                    if not (isinstance(s, int) and s < 2):
                        pe.wait_ge(xT_ready, s - 1)
                        pe.sem_inc(marker, 1)
                    for t in range(TS):
                        last = pe.transpose(b_xT[j % 2][:, t, :], rec[:, j, t, 0:D], ident[:, :])
                    last.then_inc(xT_done, 1)

                def gate_up(j, s):
                    pe.wait_ge(w_ready, TS * (s + 1))
                    pe.sem_inc(marker, 1)
                    pe.wait_ge(xT_ready, s + 1)
                    for t in range(TS):
                        for half in range(2):
                            last = pe.matmul(b_gu[j % 3][:, half, t, :], w_now[:, j % 3, t, half * D:(half + 1) * D],
                                             xT[:, j, t, :], start=True, stop=True)
                    last.then_inc(gu_done, 1)

                def down(j, s, e):
                    pe.wait_ge(hid_ready, s + 1)
                    if not (isinstance(s, int) and s < 3):
                        pe.sem_inc(marker, 1)
                        pe.wait_ge(y_ready, 2 * (s - 2))
                    for t in range(TS):
                        last = pe.matmul(b_y[j % 3][:, t, :], hid[:, j, t, :],
                                         w_d[:, bass.ds(e[t], 1), :].rearrange("p a n -> p (a n)"), start=True, stop=True)
                    last.then_inc(y_done, 1)

                def body(i, first, last):
                    n = LAST if last else SB
                    e = tile_values(mybir.EngineType.PE, 1, TS * SB * i, TS * n, NE - 1)
                    for j in range(n):
                        s = SB * i + j
                        if not last or j + 1 < n:
                            gate_up((j + 1) % SB, s + 1)
                        if not last or j + 3 < n:
                            transposes((j + 3) % SB, i + (j + 3) // SB, s + 3)
                        down(j, s, e[TS * j:TS * (j + 1)])

                transposes(0, 0, 0)
                transposes(1, 0, 1)
                gate_up(0, 0)
                transposes(2, 0, 2)
                loop(pe, body)

            @block.scalar
            def _(act):
                def take_xT(j, s):
                    act.wait_ge(xT_done, s + 1)
                    act.activation(xT[:, j, :, :], b_xT[j % 2][:, :, :], ACT.Copy).then_inc(xT_ready, 1)

                def silu(j, s):
                    act.wait_ge(gu_done, s + 1)
                    act.activation(act_g[:, j, :, :], b_gu[j % 3][:, 0, :, :], ACT.Silu).then_inc(silu_ready, 1)

                def scale_y(j, i, s, e):
                    act.wait_ge(dest_ready, s + 1)
                    act.sem_inc(marker, 1)
                    act.wait_ge(y_done, s + 1)
                    act.sem_inc(marker, 1)
                    if not (isinstance(i, int) and i == 0):
                        act.wait_ge(stored[j], 16 * TS * i)
                        act.sem_inc(marker, 1)
                    for t in range(TS):
                        act.activation(y[:, j, t, :], b_y[j % 3][:, t, :], ACT.Copy,
                                       scale=rec[:, j, t, bass.ds(D + e[t], 1)]).then_inc(y_ready, 1)

                def body(i, first, last):
                    n = LAST if last else SB
                    lo = 0 if first else TS * (SB * i - 1)
                    e = tile_values(mybir.EngineType.Activation, 1, lo, TS * (n + (0 if first else 1)), NE - 1)

                    def of(k):
                        at = TS * (k + (0 if first else 1))
                        return e[at:at + TS]

                    for j in range(n):
                        s = SB * i + j
                        if not (first and j == 0):
                            scale_y((j - 1) % SB, i - (1 if j == 0 else 0), s - 1, of(j - 1))
                        if not last or j + 1 < n:
                            silu((j + 1) % SB, s + 1)
                        if not last or j + 3 < n:
                            take_xT((j + 3) % SB, s + 3)
                    if last:
                        scale_y(LAST - 1, BODIES - 1, STEPS - 1, of(LAST - 1))

                take_xT(0, 0)
                take_xT(1, 1)
                silu(0, 0)
                take_xT(2, 2)
                loop(act, body)

            @block.vector
            def _(ve):
                ve.wait_ge(weights_in, 16 * 6)

                def copy_weights(j, s, e, t):
                    if t == 0 and not (isinstance(s, int) and s < 3):
                        ve.wait_ge(gu_done, s - 2)
                        ve.sem_inc(marker, 1)
                    ve.tensor_copy(w_now[:, j % 3, t, :],
                                   w_gu[:, bass.ds(e[t], 1), :].rearrange("p a n -> p (a n)")).then_inc(w_ready, 1)

                def hidden(j, s):
                    ve.wait_ge(silu_ready, s + 1)
                    ve.tensor_tensor(hid[:, j, :, :], act_g[:, j, :, :], b_gu[j % 3][:, 1, :, :], ALU.mult).then_inc(hid_ready, 1)

                def mark_chosen(j, i, e, then):
                    ve.wait_ge(rec_in[j], 16 * TS * (i + 1))
                    if not (isinstance(i, int) and i == 0):
                        ve.sem_inc(marker, 1)
                        ve.wait_ge(stored[j], 16 * TS * i)
                        ve.sem_inc(marker, 1)
                    for t in range(TS):
                        then(ve.scalar_tensor_tensor(out=chosen[:, j, t, :], in0=rec[:, j, t, D:D + NE], scalar=0.0,
                                                     in1=before[:, bass.ds(NE - e[t], NE)], op0=ALU.is_ge, op1=ALU.mult))

                def count_chosen(j, then):
                    then.settle()
                    then(ve.tensor_reduce(nth[:, j, :], chosen[:, j, :, :], AX.X, ALU.add))

                def add_first(j, then):
                    then.settle()
                    then(ve.tensor_tensor(nth[:, j, :], nth[:, j, :], rec[:, j, :, D + NE], ALU.add))

                def put_aside(j, s, then):
                    then.settle()
                    ve.tensor_tensor(dest[:, j, :], nth[:, j, :],
                                     aside[:, TS * s:TS * (s + 1)] if isinstance(s, int) else aside[:, bass.ds(TS * s, TS)],
                                     ALU.max).then_inc(dest_ready, 1)

                def body(i, first, last):
                    n = LAST if last else SB
                    e = tile_values(mybir.EngineType.DVE, 1, TS * SB * i, TS * (n + (0 if last else 3)), NE - 1)
                    ve.sem_clear(dve)
                    then = Chain(ve, dve)
                    for j in range(n):
                        s = SB * i + j
                        next_ = (j + 1) % SB
                        rows_too = not last or j + 1 < n
                        weights_too = not last or j + 3 < n
                        e3 = e[TS * (j + 3):TS * (j + 4)]
                        if rows_too:
                            mark_chosen(next_, i + (j + 1) // SB, e[TS * (j + 1):TS * (j + 2)], then)
                        if weights_too:
                            copy_weights((j + 3) % SB, s + 3, e3, 0)
                        if rows_too:
                            count_chosen(next_, then)
                        if weights_too:
                            copy_weights((j + 3) % SB, s + 3, e3, 1)
                        if rows_too:
                            add_first(next_, then)
                            hidden(next_, s + 1)
                            put_aside(next_, s + 1, then)

                e = tile_values(mybir.EngineType.DVE, 1, 0, TS * 3, NE - 1)
                for s in range(3):
                    for t in range(TS):
                        copy_weights(s, s, e[TS * s:TS * (s + 1)], t)
                then = Chain(ve, dve)
                mark_chosen(0, 0, e[0:TS], then)
                count_chosen(0, then)
                add_first(0, then)
                put_aside(0, 0, then)
                hidden(0, 0)
                loop(ve, body)


def combine(nc, es, sb, bank, a, out, v):
    base, results = v["base"], v["results"]
    RING = 3
    with ExitStack() as local:
        def lsb(name, shape, dt=F32):
            return sb(name, shape, dt, local)

        def sem(name):
            return local.enter_context(nc.semaphore(name))

        got = lsb("got", [P, RING, 3, KE, D])
        total = lsb("total", [P, RING, 3, D])
        shared = Shared(nc, sb, bank, local, v, "_late", EARLY)
        loaded = [sem(f"loaded{u}") for u in range(RING)]
        sum_ready = sem("sum_ready5")
        total_ready = sem("total_ready")
        patch_sums = sem("patch_sums")
        patch_ready = sem("patch_ready")
        out_done = [sem(f"out_done{u}") for u in range(RING)]

        def store(act, n):
            u = n % RING
            act.wait_ge(total_ready, n + 1)
            act.wait_ge(patch_ready, n + 1)
            for w in range(2):
                b = 2 * n + w
                act.dma_start(out[b, NP_:L, :], total[:, u, w, :]).then_inc(out_done[u], 16)
                act.dma_start(out[b, 0:NP_, :], total[w * NP_:(w + 1) * NP_, u, 2, :]).then_inc(out_done[u], 16)

        with nc.Block() as block:
            @block.sync
            def _(sp):
                for n in range(PAIRS):
                    u = n % RING
                    if n >= RING:
                        sp.wait_ge(sum_ready, n - RING + 1)
                        sp.wait_ge(patch_sums, 3 * (n - RING + 1))
                    at = KE * 3 * P * n
                    sp.dma_start(got[:, u, 0:2, :, :], results[at:at + 2 * P * KE, :].rearrange("(t p k) d -> p t (k d)", t=2, k=KE)
                                 .rearrange("p t (k d) -> p t k d", k=KE)).then_inc(loaded[u], 16)
                    at += 2 * P * KE
                    sp.dma_start(got[0:T2, u, 2, :, :], results[at:at + T2 * KE, :].rearrange("(p k) d -> p k d", k=KE)).then_inc(loaded[u], 16)

            @block.tensor
            def _(pe):
                for n in range(EARLY, PAIRS):
                    shared.products(pe, n)

            @block.scalar
            def _(act):
                for n in range(PAIRS):
                    if EARLY + n < PAIRS:
                        shared.silu(act, EARLY + n)
                    if n > 0:
                        store(act, n - 1)
                store(act, PAIRS - 1)
                for u in range(RING):
                    act.wait_ge(out_done[u], 16 * 4 * len(range(u, PAIRS, RING)))

            @block.gpsimd
            def _(po):
                for n in range(PAIRS):
                    u = n % RING
                    g, o = got[0:T2, u, 2, :, :], total[0:T2, u, 2, :]
                    po.wait_ge(loaded[u], 16 * 2 * (n // RING + 1))
                    po.tensor_tensor(g[:, 0:3, :], g[:, 0:3, :], g[:, 3:6, :], ALU.add).then_inc(patch_sums, 1)
                    po.wait_ge(patch_sums, 3 * n + 1)
                    if n >= RING:
                        po.wait_ge(out_done[u], 16 * 4 * (n // RING))
                    po.tensor_tensor(o, g[:, 0, :], g[:, 1, :], ALU.add).then_inc(patch_sums, 1)
                    po.wait_ge(patch_sums, 3 * n + 2)
                    po.tensor_tensor(o, o, g[:, 2, :], ALU.add).then_inc(patch_sums, 1)
                    po.wait_ge(patch_sums, 3 * n + 3)
                    if EARLY <= n:
                        po.wait_ge(shared.added, 2 * (n - EARLY + 1))
                    po.tensor_tensor(o, o, base[0:T2, 3 * n + 2, :], ALU.add).then_inc(patch_ready, 1)

            @block.vector
            def _(ve):
                for n in range(PAIRS):
                    u = n % RING
                    if EARLY + n < PAIRS:
                        shared.hidden(ve, EARLY + n)
                    if n >= RING:
                        ve.wait_ge(out_done[u], 16 * 4 * (n // RING))
                    ve.wait_ge(loaded[u], 16 * 2 * (n // RING + 1))
                    ve.tensor_reduce(total[:, u, 0:2, :], got[:, u, 0:2, :, :].rearrange("p t k d -> p t d k"), AX.X,
                                     ALU.add).then_inc(sum_ready, 1)
                    if n >= EARLY:
                        ve.wait_ge(shared.added, 2 * (n - EARLY + 1))
                    ve.wait_ge(sum_ready, n + 1)
                    ve.tensor_tensor(total[:, u, 0:2, :], total[:, u, 0:2, :], base[:, 3 * n:3 * n + 2, :],
                                     ALU.add).then_inc(total_ready, 1)
                    if EARLY + n < PAIRS:
                        shared.add(ve, EARLY + n)


def kernel(**inputs):
    import concourse.bacc as bacc
    from concourse.bass_utils import run_bass_kernel_spmd

    x = {n.replace("L0_", ""): np.asarray(t) for n, t in inputs.items()}
    f32 = np.float32
    arrays = {}
    p = x["x"].reshape(B, 3, 6, 16, 6, 16).transpose(1, 3, 5, 0, 2, 4).reshape(CHUNKS, P, B * NP_)
    arrays["patches"] = np.ascontiguousarray(p.transpose(1, 0, 2))
    w_all = np.zeros((3, 16, 16, D), f32)
    w_all[..., 0:64] = x["tok_W_main"].reshape(64, 3, 16, 16).transpose(1, 2, 3, 0)
    sx = x["tok_W_sx"].reshape(16, 3, 16, 16).transpose(1, 2, 3, 0)
    sy = x["tok_W_sy"].reshape(16, 3, 16, 16).transpose(1, 2, 3, 0)
    w_all[:, :, 0:8, 64:80] = sx[:, :, 8:16]
    w_all[:, :, 8:16, 80:96] = sx[:, :, 0:8]
    w_all[:, 0:8, :, 96:112] = sy[:, 8:16]
    w_all[:, 8:16, :, 112:128] = sy[:, 0:8]
    arrays["w_all"] = np.ascontiguousarray(w_all.reshape(CHUNKS, P, D).transpose(1, 0, 2))
    perm = np.zeros((P, 5, D), f32)
    lo, hi, ylo, yhi = 64, 80, 96, 112
    for k in range(64):
        perm[k, 0, k] = 1
    for k in range(16):
        perm[hi + k, 0, 64 + k] = perm[lo + k, 0, 80 + k] = perm[yhi + k, 0, 96 + k] = perm[ylo + k, 0, 112 + k] = 1
        perm[lo + k, 1, 64 + k] = 1
        perm[hi + k, 2, 80 + k] = 1
        perm[ylo + k, 3, 96 + k] = 1
        perm[yhi + k, 4, 112 + k] = 1
    arrays["perm"] = perm
    arrays["ident"] = np.eye(P, dtype=f32)
    arrays["shift36"] = np.eye(NP_, 2 * NP_, k=NP_, dtype=f32)
    mask = np.zeros((P, H), f32)
    for h in range(H):
        mask[h * E:(h + 1) * E, h] = E ** -0.5
    arrays["head_mask"] = mask
    arrays["b_tok"] = np.concatenate([x["tok_b_main"], x["tok_b_sx"], x["tok_b_sx"], x["tok_b_sy"],
                                      x["tok_b_sy"]]).reshape(P, 1)
    arrays["rows"] = x["attn_bo"].reshape(1, D)
    for n in "qkvo":
        arrays["w" + n] = np.ascontiguousarray(x["attn_W" + n].T)
    for n in "qkv":
        arrays["b" + n] = x["attn_b" + n].reshape(P, 1)
    arrays["ln_g"], arrays["ln_b"] = x["tok_ln_g"], x["tok_ln_b"]
    for n in ("g", "u", "d"):
        arrays["w_" + n] = np.concatenate([x["ffn_W" + n], x["ffn_sW" + n]]).transpose(1, 0, 2)
    arrays["w_gu"] = np.ascontiguousarray(np.concatenate([arrays.pop("w_g"), arrays.pop("w_u")], axis=2))
    arrays["w_d"] = np.ascontiguousarray(arrays["w_d"])
    arrays["wr"] = x["ffn_Wr"]
    arrays["tri"] = np.triu(np.ones((P, P), f32), 1)
    arrays["region"] = np.zeros((P, NE), f32)
    arrays["region"][0] = np.arange(NE) * CAP + P + 1
    arrays["region_all"] = np.tile(np.arange(NE, dtype=f32) * CAP, (P, 1))
    arrays["codes"] = (KE * (np.arange(3 * PAIRS) * P + np.arange(P)[:, None])).astype(f32)
    arrays["spare"] = (3 * PAIRS * P * KE + np.arange(2 * P) * P + np.arange(P)[:, None]).astype(f32)
    arrays["part_no"] = np.arange(P, dtype=f32).reshape(P, 1)
    arrays["before"] = np.tile((np.arange(2 * NE) < NE).astype(f32), (P, 1))
    arrays["names"] = np.tile(np.arange(NE, dtype=f32), (P, 1))
    arrays["steps"] = np.tile(np.arange(21, dtype=f32) * P, (P, 1))
    arrays["tile_no"] = np.arange(2 * P, dtype=f32).reshape(2, P).T.copy()
    arrays["txt"] = np.ascontiguousarray(x["txt"].transpose(1, 0, 2))

    nc = bacc.Bacc("TRN2", target_bir_lowering=False, num_devices=1)
    aps = {n: nc.dram_tensor("in_" + n, t.shape, mybir.dt.from_np(t.dtype), kind="ExternalInput").ap() for n, t in arrays.items()}
    out = nc.dram_tensor("out_h", (B, L, D), F32, kind="ExternalOutput").ap()
    build(nc, aps, out)
    r = run_bass_kernel_spmd(nc, [{"in_" + n: t for n, t in arrays.items()}], core_ids=[0])
    return r.results[0]["out_h"]
```
